# Optimizing a Trainium2 kernel written in Bass

```python
import numpy as np
import jax
import jax.numpy as jnp

def _softmax(x, axis=-1):
    return jax.nn.softmax(x, axis=axis)

def _gelu(x):
    return jax.nn.gelu(x, approximate=True)

def _silu(x):
    return jax.nn.silu(x)

def _sigmoid(x):
    return jax.nn.sigmoid(x)

def _layernorm(x, axis=-1, eps=1e-05):
    m = jnp.mean(x, axis=axis, keepdims=True)
    v = jnp.var(x, axis=axis, keepdims=True)
    return (x - m) / jnp.sqrt(v + eps)

def _scatter_add(tgt, idx, src, axis=0):
    return tgt.at[idx].add(src)

def _segment_sum(src, seg, n):
    return jax.ops.segment_sum(src, seg, n)
kernel_name = 'mk_xattn_ffn_d4_seqx_r8_2c4082'

def setup_inputs(seed: int=0):
    np.random.seed(seed)
    _w = jnp.asarray

    def _rec_inputs():
        import jax
        import jax.numpy as jnp
        _rk = jax.random.key(seed)
        x = -0.0002928 + 1 * jax.random.normal(jax.random.fold_in(_rk, 1), (16, 128, 128), jnp.float32)
        _lenS = 128 - jax.random.randint(jax.random.fold_in(_rk, 7), (16,), 0, max(1, 128 // 4) + 1, jnp.int32)
        _lenS2 = 77 - jax.random.randint(jax.random.fold_in(_rk, 8), (16,), 0, max(1, 77 // 4) + 1, jnp.int32)
        _ctx_768P = jax.random.normal(jax.random.fold_in(_rk, 11), (16, 16, 96), jnp.float32)
        _ctx_768c = jax.random.dirichlet(jax.random.fold_in(_rk, 511), 0.3 * jnp.ones((16,), jnp.float32), (16, 77))
        _ctx_768t = jnp.einsum('bsk,bkd->bsd', _ctx_768c, _ctx_768P)
        _ctx_768t = _ctx_768t * jax.lax.rsqrt(jnp.mean(jnp.square(_ctx_768t)) + 1e-12) * 0.953939
        ctx_768 = 2.09791e-05 + 1.00001 * (_ctx_768t + 0.3 * jax.random.normal(jax.random.fold_in(_rk, 611), (16, 77, 96), jnp.float32))
        _validS = jnp.arange(128)[None, :] < _lenS[:, None]
        _validS2 = jnp.arange(77)[None, :] < _lenS2[:, None]
        _causal = jnp.tril(jnp.ones((128, 128), dtype=bool))
        mask_BxS2_bf1 = jnp.ones((16, 77), dtype=bool)
        return (x, ctx_768, mask_BxS2_bf1)
    x, ctx_768, mask_BxS2_bf1 = _rec_inputs()

    def _L0_xattn_setup():
        import jax, jax.numpy as jnp
        import numpy as np
        B, LQ, LKV = (2, 256, 256)
        C, CTX, H, DK = (128, 96, 16, 64)
        SCALE = DK ** (-0.5)
        key = jax.random.key(seed)
        kx, ky, kq, kkv, kp, kb = jax.random.split(key, 6)
        return {'x': jax.random.normal(kx, (B, LQ, C), dtype=jnp.float32), 'y': jax.random.normal(ky, (B, LKV, CTX), dtype=jnp.float32), 'Wq': jax.random.normal(kq, (C, H * DK), dtype=jnp.float32) * C ** (-0.5), 'Wkv': jax.random.normal(kkv, (CTX, 2 * H * DK), dtype=jnp.float32) * CTX ** (-0.5), 'Wproj': jax.random.normal(kp, (H * DK, C), dtype=jnp.float32) * (H * DK) ** (-0.5), 'bproj': jax.random.normal(kb, (C,), dtype=jnp.float32) * 0.01}
    _L0_xattn_all = _L0_xattn_setup()
    _L0_xattn_in = {k: v for k, v in _L0_xattn_all.items() if k in ('Wq', 'Wkv', 'Wproj', 'bproj')}
    del _L0_xattn_all

    def _L0_ffn_setup():
        import jax, jax.numpy as jnp
        import numpy as np
        B, T, D, F_FF, E, TOP_K = (8, 256, 128, 512, 8, 2)
        CAP_FACTOR = 1.25
        key = jax.random.key(seed)
        ks = jax.random.split(key, 7)
        s = 0.02
        return {'x': jax.random.normal(ks[0], (B, T, D), dtype=jnp.float32), 'w_router': jax.random.normal(ks[1], (D, E), dtype=jnp.float32) * s, 'b_router': jnp.zeros((E,), dtype=jnp.float32), 'w1': jax.random.normal(ks[2], (E, D, F_FF), dtype=jnp.float32) * s, 'b1': jnp.zeros((E, F_FF), dtype=jnp.float32), 'w2': jax.random.normal(ks[3], (E, F_FF, D), dtype=jnp.float32) * s, 'b2': jnp.zeros((E, D), dtype=jnp.float32)}
    _L0_ffn_all = _L0_ffn_setup()
    _L0_ffn_in = {k: v for k, v in _L0_ffn_all.items() if k in ('w_router', 'b_router', 'w1', 'b1', 'w2', 'b2')}
    del _L0_ffn_all

    def _L1_xattn_setup():
        import jax, jax.numpy as jnp
        import numpy as np
        HEADS = 16
        DIM_HEAD = 64
        key = jax.random.key(seed)
        ks = jax.random.split(key, 8)
        B, S, D = (16, 512, 128)
        K, DE = (77, 96)
        inner = HEADS * DIM_HEAD
        hidden_states = jax.random.normal(ks[0], (B, S, D), dtype=jnp.float32)
        encoder_hidden_states = jax.random.normal(ks[1], (B, K, DE), dtype=jnp.float32)
        sc_q = 1.0 / np.sqrt(D)
        sc_kv = 1.0 / np.sqrt(DE)
        sc_o = 1.0 / np.sqrt(inner)
        Wq = jax.random.normal(ks[2], (D, inner), dtype=jnp.float32) * sc_q
        Wk = jax.random.normal(ks[3], (DE, inner), dtype=jnp.float32) * sc_kv
        Wv = jax.random.normal(ks[4], (DE, inner), dtype=jnp.float32) * sc_kv
        Wo = jax.random.normal(ks[5], (inner, D), dtype=jnp.float32) * sc_o
        bo = jax.random.normal(ks[6], (D,), dtype=jnp.float32) * 0.01
        return {'hidden_states': hidden_states, 'encoder_hidden_states': encoder_hidden_states, 'Wq': Wq, 'Wk': Wk, 'Wv': Wv, 'Wo': Wo, 'bo': bo}
    _L1_xattn_all = _L1_xattn_setup()
    _L1_xattn_in = {k: v for k, v in _L1_xattn_all.items() if k in ('Wq', 'Wk', 'Wv', 'Wo', 'bo')}
    del _L1_xattn_all

    def _L1_ffn_setup():
        import jax, jax.numpy as jnp
        import numpy as np
        DIM = 128
        HIDDEN = 384
        SCALE = 1.0 / 127.0

        def _dequant(w_int, dtype):
            return w_int.astype(dtype) * jnp.asarray(SCALE, dtype)
        key = jax.random.key(seed)
        k_x, k_g, k_u, k_d = jax.random.split(key, 4)
        x = jax.random.normal(k_x, (4, 256, DIM), dtype=jnp.float32)
        w_gate = jax.random.randint(k_g, (HIDDEN, DIM), -127, 128, dtype=jnp.int32)
        w_up = jax.random.randint(k_u, (HIDDEN, DIM), -127, 128, dtype=jnp.int32)
        w_down = jax.random.randint(k_d, (DIM, HIDDEN), -127, 128, dtype=jnp.int32)
        return {'x': x, 'w_gate': w_gate, 'w_up': w_up, 'w_down': w_down}
    _L1_ffn_all = _L1_ffn_setup()
    _L1_ffn_in = {k: v for k, v in _L1_ffn_all.items() if k in ('w_gate', 'w_up', 'w_down')}
    del _L1_ffn_all

    def _L2_xattn_setup():
        import jax, jax.numpy as jnp
        import numpy as np
        N_HEADS = 16
        key = jax.random.key(seed)
        ks = jax.random.split(key, 8)
        b, l, m = (8, 128, 128)
        d_embed, d_cross = (128, 96)
        s_q = 1.0 / np.sqrt(d_embed)
        s_kv = 1.0 / np.sqrt(d_cross)
        return {'x': jax.random.normal(ks[0], (b, l, d_embed), jnp.float32), 'y': jax.random.normal(ks[1], (b, m, d_cross), jnp.float32), 'Wq': jax.random.normal(ks[2], (d_embed, d_embed), jnp.float32) * s_q, 'bq': jax.random.normal(ks[3], (d_embed,), jnp.float32) * 0.01, 'Wkv': jax.random.normal(ks[4], (2 * d_embed, d_cross), jnp.float32) * s_kv, 'bkv': jax.random.normal(ks[5], (2 * d_embed,), jnp.float32) * 0.01, 'Wo': jax.random.normal(ks[6], (d_embed, d_embed), jnp.float32) * s_q, 'bo': jax.random.normal(ks[7], (d_embed,), jnp.float32) * 0.01}
    _L2_xattn_all = _L2_xattn_setup()
    _L2_xattn_in = {k: v for k, v in _L2_xattn_all.items() if k in ('Wq', 'bq', 'Wkv', 'bkv', 'Wo', 'bo')}
    del _L2_xattn_all

    def _L2_ffn_setup():
        import jax, jax.numpy as jnp
        import numpy as np
        D_MODEL = 128
        N_EXPERTS = 8
        TOP_K = 2
        HIDDEN = 4 * D_MODEL
        key = jax.random.key(seed)
        ks = jax.random.split(key, 6)
        B, S = (2, 256)
        x = jax.random.normal(ks[0], (B, S, D_MODEL), dtype=jnp.float32)
        shared_w1 = jax.random.normal(ks[1], (HIDDEN, D_MODEL), dtype=jnp.float32) * 0.02
        shared_w2 = jax.random.normal(ks[2], (D_MODEL, HIDDEN), dtype=jnp.float32) * 0.02
        experts_w1 = jax.random.normal(ks[3], (N_EXPERTS, HIDDEN, D_MODEL), dtype=jnp.float32) * 0.02
        experts_w2 = jax.random.normal(ks[4], (N_EXPERTS, D_MODEL, HIDDEN), dtype=jnp.float32) * 0.02
        gate_w = jax.random.normal(ks[5], (N_EXPERTS, D_MODEL), dtype=jnp.float32) * 0.02
        return {'x': x, 'shared_w1': shared_w1, 'shared_w2': shared_w2, 'experts_w1': experts_w1, 'experts_w2': experts_w2, 'gate_w': gate_w}
    _L2_ffn_all = _L2_ffn_setup()
    _L2_ffn_in = {k: v for k, v in _L2_ffn_all.items() if k in ('shared_w1', 'shared_w2', 'experts_w1', 'experts_w2', 'gate_w')}
    del _L2_ffn_all

    def _L3_xattn_setup():
        import jax, jax.numpy as jnp
        import numpy as np
        DIM = 128
        CTX_DIM = 96
        HEADS = 16
        key = jax.random.key(seed)
        ks = jax.random.split(key, 7)
        B, N, M = (4, 512, 32)
        x = jax.random.normal(ks[0], (B, N, DIM), dtype=jnp.float32)
        context = jax.random.normal(ks[1], (B, M, CTX_DIM), dtype=jnp.float32)
        context_mask = jnp.ones((B, M), dtype=bool)
        s_d = 1.0 / np.sqrt(DIM)
        s_c = 1.0 / np.sqrt(CTX_DIM)
        Wq = jax.random.normal(ks[2], (DIM, DIM), dtype=jnp.float32) * s_d
        Wk = jax.random.normal(ks[3], (CTX_DIM, DIM), dtype=jnp.float32) * s_c
        Wv = jax.random.normal(ks[4], (CTX_DIM, DIM), dtype=jnp.float32) * s_c
        Wo = jax.random.normal(ks[5], (DIM, DIM), dtype=jnp.float32) * s_d
        return {'x': x, 'context': context, 'context_mask': context_mask, 'Wq': Wq, 'Wk': Wk, 'Wv': Wv, 'Wo': Wo}
    _L3_xattn_all = _L3_xattn_setup()
    _L3_xattn_in = {k: v for k, v in _L3_xattn_all.items() if k in ('Wq', 'Wk', 'Wv', 'Wo')}
    del _L3_xattn_all

    def _L3_ffn_setup():
        import jax, jax.numpy as jnp
        from jax import lax
        import numpy as np
        D = 128
        N = 8
        K = 2
        KS = 1
        H = 2 * D
        B, S = (2, 128)

        def _moe(x_BSD, Wg_DN, Wl1_ND2H, Wl2_NHD):
            b, s, d = x_BSD.shape
            x_MD = x_BSD.reshape(b * s, d)
            Nr = N - KS
            s_raw_MN = x_MD @ Wg_DN
            routed = jax.nn.softmax(s_raw_MN[:, :Nr].astype(jnp.float32), axis=-1)
            shared = jax.nn.softmax(s_raw_MN[:, Nr:].astype(jnp.float32), axis=-1)
            _, idx_MK = lax.top_k(routed, K - KS)
            mask = jnp.sum(jax.nn.one_hot(idx_MK, Nr, dtype=jnp.float32), axis=1)
            sel = routed * mask
            routed_n = sel / jnp.sum(sel, axis=-1, keepdims=True)
            shared_n = shared / jnp.sum(shared, axis=-1, keepdims=True)
            gates_MN = jnp.concatenate([routed_n, shared_n], axis=-1).astype(x_MD.dtype)

            def step(y_MD, inp):
                w1_D2H, w2_HD, g_M = inp
                z = x_MD @ w1_D2H
                a, bgate = jnp.split(z, 2, axis=-1)
                h = jax.nn.silu(bgate) * a
                return (y_MD + g_M[:, None] * (h @ w2_HD), None)
            y0 = jnp.zeros_like(x_MD)
            y_MD, _ = lax.scan(step, y0, (Wl1_ND2H, Wl2_NHD, gates_MN.T))
            return y_MD.reshape(b, s, d)
        key = jax.random.key(seed)
        k1, k2, k3, k4 = jax.random.split(key, 4)
        scale = 1.0 / np.sqrt(D).astype(np.float32)
        x = jax.random.normal(k1, (B, S, D), dtype=jnp.float32)
        Wg = jax.random.normal(k2, (D, N), dtype=jnp.float32) * scale
        Wl1 = jax.random.normal(k3, (N, D, 2 * H), dtype=jnp.float32) * scale
        Wl2 = jax.random.normal(k4, (N, H, D), dtype=jnp.float32) * scale
        return {'x_BSD': x, 'Wg_DN': Wg, 'Wl1_ND2H': Wl1, 'Wl2_NHD': Wl2}
    _L3_ffn_all = _L3_ffn_setup()
    _L3_ffn_in = {k: v for k, v in _L3_ffn_all.items() if k in ('Wg_DN', 'Wl1_ND2H', 'Wl2_NHD')}
    del _L3_ffn_all
    return {'x': x, 'ctx_768': ctx_768, 'mask_BxS2_bf1': mask_BxS2_bf1, 'L0_xattn_Wq': _L0_xattn_in['Wq'], 'L0_xattn_Wkv': _L0_xattn_in['Wkv'], 'L0_xattn_Wproj': _L0_xattn_in['Wproj'], 'L0_xattn_bproj': _L0_xattn_in['bproj'], 'L0_ffn_w_router': _L0_ffn_in['w_router'], 'L0_ffn_b_router': _L0_ffn_in['b_router'], 'L0_ffn_w1': _L0_ffn_in['w1'], 'L0_ffn_b1': _L0_ffn_in['b1'], 'L0_ffn_w2': _L0_ffn_in['w2'], 'L0_ffn_b2': _L0_ffn_in['b2'], 'L1_xattn_Wq': _L1_xattn_in['Wq'], 'L1_xattn_Wk': _L1_xattn_in['Wk'], 'L1_xattn_Wv': _L1_xattn_in['Wv'], 'L1_xattn_Wo': _L1_xattn_in['Wo'], 'L1_xattn_bo': _L1_xattn_in['bo'], 'L1_ffn_w_gate': _L1_ffn_in['w_gate'], 'L1_ffn_w_up': _L1_ffn_in['w_up'], 'L1_ffn_w_down': _L1_ffn_in['w_down'], 'L2_xattn_Wq': _L2_xattn_in['Wq'], 'L2_xattn_bq': _L2_xattn_in['bq'], 'L2_xattn_Wkv': _L2_xattn_in['Wkv'], 'L2_xattn_bkv': _L2_xattn_in['bkv'], 'L2_xattn_Wo': _L2_xattn_in['Wo'], 'L2_xattn_bo': _L2_xattn_in['bo'], 'L2_ffn_shared_w1': _L2_ffn_in['shared_w1'], 'L2_ffn_shared_w2': _L2_ffn_in['shared_w2'], 'L2_ffn_experts_w1': _L2_ffn_in['experts_w1'], 'L2_ffn_experts_w2': _L2_ffn_in['experts_w2'], 'L2_ffn_gate_w': _L2_ffn_in['gate_w'], 'L3_xattn_Wq': _L3_xattn_in['Wq'], 'L3_xattn_Wk': _L3_xattn_in['Wk'], 'L3_xattn_Wv': _L3_xattn_in['Wv'], 'L3_xattn_Wo': _L3_xattn_in['Wo'], 'L3_ffn_Wg_DN': _L3_ffn_in['Wg_DN'], 'L3_ffn_Wl1_ND2H': _L3_ffn_in['Wl1_ND2H'], 'L3_ffn_Wl2_NHD': _L3_ffn_in['Wl2_NHD']}

def reference(x, ctx_768, mask_BxS2_bf1, L0_xattn_Wq, L0_xattn_Wkv, L0_xattn_Wproj, L0_xattn_bproj, L0_ffn_w_router, L0_ffn_b_router, L0_ffn_w1, L0_ffn_b1, L0_ffn_w2, L0_ffn_b2, L1_xattn_Wq, L1_xattn_Wk, L1_xattn_Wv, L1_xattn_Wo, L1_xattn_bo, L1_ffn_w_gate, L1_ffn_w_up, L1_ffn_w_down, L2_xattn_Wq, L2_xattn_bq, L2_xattn_Wkv, L2_xattn_bkv, L2_xattn_Wo, L2_xattn_bo, L2_ffn_shared_w1, L2_ffn_shared_w2, L2_ffn_experts_w1, L2_ffn_experts_w2, L2_ffn_gate_w, L3_xattn_Wq, L3_xattn_Wk, L3_xattn_Wv, L3_xattn_Wo, L3_ffn_Wg_DN, L3_ffn_Wl1_ND2H, L3_ffn_Wl2_NHD):
    import jax
    import jax.numpy as jnp

    def _L0_xattn_ref(x, y, Wq, Wkv, Wproj, bproj):
        import jax, jax.numpy as jnp
        import numpy as np
        B, LQ, LKV = (2, 256, 256)
        C, CTX, H, DK = (128, 96, 16, 64)
        SCALE = DK ** (-0.5)
        b, lq, _ = x.shape
        lkv = y.shape[1]
        q = (x @ Wq).reshape(b, lq, H, DK).transpose(0, 2, 1, 3)
        kv = (y @ Wkv).reshape(b, lkv, 2, H, DK).transpose(2, 0, 3, 1, 4)
        k, v = (kv[0], kv[1])
        atten = jax.nn.softmax(jnp.einsum('bhid,bhjd->bhij', q, k) * SCALE, axis=-1)
        res = jnp.einsum('bhij,bhjd->bhid', atten, v)
        res = res.transpose(0, 2, 1, 3).reshape(b, lq, H * DK)
        out = res @ Wproj + bproj
        return out

    def _L0_ffn_ref(x, w_router, b_router, w1, b1, w2, b2):
        import jax, jax.numpy as jnp
        import numpy as np
        B, T, D, F_FF, E, TOP_K = (8, 256, 128, 512, 8, 2)
        CAP_FACTOR = 1.25
        b, t, d = x.shape
        n = b * t
        e = w_router.shape[1]
        xf = x.reshape(n, d)
        logits = xf.astype(jnp.float32) @ w_router + b_router
        gates = jax.nn.softmax(logits, axis=-1)
        topv, topi = jax.lax.top_k(gates, TOP_K)
        cap = max(1, int(CAP_FACTOR * n / e))
        e_flat = topi.reshape(-1)
        g_flat = topv.reshape(-1)
        tok = jnp.repeat(jnp.arange(n), TOP_K)
        onehot = jax.nn.one_hot(e_flat, e, dtype=jnp.int32)
        pos = jnp.cumsum(onehot, axis=0)[jnp.arange(n * TOP_K), e_flat] - 1
        keep = pos < cap
        posc = jnp.minimum(pos, cap - 1)
        buf = jnp.zeros((e, cap, d), x.dtype).at[e_flat, posc].add(jnp.where(keep[:, None], xf[tok], 0.0))
        h = jax.nn.gelu(jnp.einsum('ecd,edf->ecf', buf, w1) + b1[:, None, :], approximate=False)
        out = jnp.einsum('ecf,efd->ecd', h, w2) + b2[:, None, :]
        og = out[e_flat, posc]
        w = jnp.where(keep, g_flat, 0.0).astype(x.dtype)
        y = jnp.zeros((n, d), x.dtype).at[tok].add(w[:, None] * og)
        ws = jnp.zeros((n,), x.dtype).at[tok].add(w)
        y = jnp.where((ws > 0.0)[:, None], y / jnp.maximum(ws, 1e-06)[:, None], y)
        return y.reshape(b, t, d)

    def _L1_xattn_ref(hidden_states, encoder_hidden_states, Wq, Wk, Wv, Wo, bo):
        import jax, jax.numpy as jnp
        import numpy as np
        HEADS = 16
        DIM_HEAD = 64
        B, S, D = hidden_states.shape
        K = encoder_hidden_states.shape[1]
        H, Dh = (HEADS, DIM_HEAD)
        scale = 1.0 / np.sqrt(Dh)
        q = hidden_states @ Wq
        k = encoder_hidden_states @ Wk
        v = encoder_hidden_states @ Wv
        q = q.reshape(B, S, H, Dh).transpose(0, 2, 1, 3)
        k = k.reshape(B, K, H, Dh).transpose(0, 2, 1, 3)
        v = v.reshape(B, K, H, Dh).transpose(0, 2, 1, 3)
        scores = jnp.einsum('bhsd,bhkd->bhsk', q, k) * scale
        probs = jax.nn.softmax(scores, axis=-1)
        out = jnp.einsum('bhsk,bhkd->bhsd', probs, v)
        out = out.transpose(0, 2, 1, 3).reshape(B, S, H * Dh)
        out = out @ Wo + bo
        return out

    def _L1_ffn_ref(x, w_gate, w_up, w_down):
        import jax, jax.numpy as jnp
        import numpy as np
        DIM = 128
        HIDDEN = 384
        SCALE = 1.0 / 127.0

        def _dequant(w_int, dtype):
            return w_int.astype(dtype) * jnp.asarray(SCALE, dtype)
        wg = _dequant(w_gate, x.dtype)
        wu = _dequant(w_up, x.dtype)
        wd = _dequant(w_down, x.dtype)
        gate = jnp.einsum('bsd,hd->bsh', x, wg)
        up = jnp.einsum('bsd,hd->bsh', x, wu)
        h = jax.nn.silu(gate) * up
        return jnp.einsum('bsh,dh->bsd', h, wd)

    def _L2_xattn_ref(x, y, Wq, bq, Wkv, bkv, Wo, bo):
        import jax, jax.numpy as jnp
        import numpy as np
        N_HEADS = 16
        b, l, d = x.shape
        m = y.shape[1]
        h = N_HEADS
        dh = d // h
        q = (jnp.einsum('bld,ed->ble', x, Wq) + bq).reshape(b, l, h, dh)
        kv = (jnp.einsum('bmc,ec->bme', y, Wkv) + bkv).reshape(b, m, h, 2 * dh)
        k, v = (kv[..., :dh], kv[..., dh:])
        scale = 1.0 / jnp.sqrt(jnp.asarray(dh, x.dtype))
        att = jax.nn.softmax(jnp.einsum('blhd,bmhd->blmh', q, k) * scale, axis=2)
        out = jnp.einsum('blmh,bmhd->blhd', att, v).reshape(b, l, d)
        return jnp.einsum('bld,ed->ble', out, Wo) + bo

    def _L2_ffn_ref(x, shared_w1, shared_w2, experts_w1, experts_w2, gate_w):
        import jax, jax.numpy as jnp
        import numpy as np
        D_MODEL = 128
        N_EXPERTS = 8
        TOP_K = 2
        HIDDEN = 4 * D_MODEL
        B, S, D = x.shape
        T = B * S
        x_flat = x.reshape(T, D)
        shared = jnp.einsum('td,dh->th', x_flat, shared_w1.T)
        shared = jnp.einsum('th,hd->td', jax.nn.silu(shared), shared_w2.T)
        gate_logits = x_flat @ gate_w.T
        top_k_gates, top_k_idx = jax.lax.top_k(gate_logits, TOP_K)
        top_k_gates = jax.nn.softmax(top_k_gates, axis=1)
        gates = jnp.zeros((T, N_EXPERTS), dtype=x.dtype)
        gates = gates.at[jnp.arange(T)[:, None], top_k_idx].set(top_k_gates)
        h = jnp.einsum('td,ehd->teh', x_flat, experts_w1)
        expert_out = jnp.einsum('teh,edh->ted', jax.nn.silu(h), experts_w2)
        selected = jnp.einsum('ted,te->td', expert_out, gates)
        return (shared + selected).reshape(B, S, D)

    def _L3_xattn_ref(x, context, context_mask, Wq, Wk, Wv, Wo):
        import jax, jax.numpy as jnp
        import numpy as np
        DIM = 128
        CTX_DIM = 96
        HEADS = 16
        B, N, _ = x.shape
        M = context.shape[1]
        hd = DIM // HEADS
        scale = hd ** (-0.5)
        q = (x @ Wq).reshape(B, N, HEADS, hd).transpose(0, 2, 1, 3)
        k = (context @ Wk).reshape(B, M, HEADS, hd).transpose(0, 2, 1, 3)
        v = (context @ Wv).reshape(B, M, HEADS, hd).transpose(0, 2, 1, 3)
        scores = jnp.einsum('bhid,bhjd->bhij', q, k) * scale
        max_neg = -jnp.finfo(scores.dtype).max
        scores = jnp.where(context_mask[:, None, None, :], scores, max_neg)
        attn = jax.nn.softmax(scores, axis=-1)
        out = jnp.einsum('bhij,bhjd->bhid', attn, v)
        out = out.transpose(0, 2, 1, 3).reshape(B, N, DIM)
        return out @ Wo

    def _L3_ffn_ref(x_BSD, Wg_DN, Wl1_ND2H, Wl2_NHD):
        import jax, jax.numpy as jnp
        from jax import lax
        import numpy as np
        D = 128
        N = 8
        K = 2
        KS = 1
        H = 2 * D
        B, S = (2, 128)

        def _moe(x_BSD, Wg_DN, Wl1_ND2H, Wl2_NHD):
            b, s, d = x_BSD.shape
            x_MD = x_BSD.reshape(b * s, d)
            Nr = N - KS
            s_raw_MN = x_MD @ Wg_DN
            routed = jax.nn.softmax(s_raw_MN[:, :Nr].astype(jnp.float32), axis=-1)
            shared = jax.nn.softmax(s_raw_MN[:, Nr:].astype(jnp.float32), axis=-1)
            _, idx_MK = lax.top_k(routed, K - KS)
            mask = jnp.sum(jax.nn.one_hot(idx_MK, Nr, dtype=jnp.float32), axis=1)
            sel = routed * mask
            routed_n = sel / jnp.sum(sel, axis=-1, keepdims=True)
            shared_n = shared / jnp.sum(shared, axis=-1, keepdims=True)
            gates_MN = jnp.concatenate([routed_n, shared_n], axis=-1).astype(x_MD.dtype)

            def step(y_MD, inp):
                w1_D2H, w2_HD, g_M = inp
                z = x_MD @ w1_D2H
                a, bgate = jnp.split(z, 2, axis=-1)
                h = jax.nn.silu(bgate) * a
                return (y_MD + g_M[:, None] * (h @ w2_HD), None)
            y0 = jnp.zeros_like(x_MD)
            y_MD, _ = lax.scan(step, y0, (Wl1_ND2H, Wl2_NHD, gates_MN.T))
            return y_MD.reshape(b, s, d)
        return _moe(x_BSD, Wg_DN, Wl1_ND2H, Wl2_NHD)
    x = x + _L0_xattn_ref(_layernorm(x, axis=-1), ctx_768, L0_xattn_Wq, L0_xattn_Wkv, L0_xattn_Wproj, L0_xattn_bproj)
    x = x + _L0_ffn_ref(_layernorm(x, axis=-1), L0_ffn_w_router, L0_ffn_b_router, L0_ffn_w1, L0_ffn_b1, L0_ffn_w2, L0_ffn_b2)
    x = x + _L1_xattn_ref(_layernorm(x, axis=-1), ctx_768, L1_xattn_Wq, L1_xattn_Wk, L1_xattn_Wv, L1_xattn_Wo, L1_xattn_bo)
    x = x + _L1_ffn_ref(_layernorm(x, axis=-1), L1_ffn_w_gate, L1_ffn_w_up, L1_ffn_w_down)
    x = x + _L2_xattn_ref(_layernorm(x, axis=-1), ctx_768, L2_xattn_Wq, L2_xattn_bq, L2_xattn_Wkv, L2_xattn_bkv, L2_xattn_Wo, L2_xattn_bo)
    x = x + _L2_ffn_ref(_layernorm(x, axis=-1), L2_ffn_shared_w1, L2_ffn_shared_w2, L2_ffn_experts_w1, L2_ffn_experts_w2, L2_ffn_gate_w)
    x = x + _L3_xattn_ref(_layernorm(x, axis=-1), ctx_768, mask_BxS2_bf1, L3_xattn_Wq, L3_xattn_Wk, L3_xattn_Wv, L3_xattn_Wo)
    x = x + _L3_ffn_ref(_layernorm(x, axis=-1), L3_ffn_Wg_DN, L3_ffn_Wl1_ND2H, L3_ffn_Wl2_NHD)
    return x

_drawn_inputs = setup_inputs


def setup_inputs(seed=0):
    import zlib

    import numpy as np

    out = dict(_drawn_inputs(seed))
    spreads = {'L0_ffn_b_router': (0.0, 0.1), 'L0_ffn_b1': (0.0, 0.437), 'L0_ffn_b2': (0.0, 0.1)}
    factors = {'L0_xattn_bproj': 3.09,
     'L1_xattn_bo': 4.973,
     'L2_xattn_Wq': 8.0,
     'L2_xattn_bq': 8.0,
     'L2_xattn_Wkv': 8.0,
     'L2_xattn_bkv': 8.0,
     'L2_xattn_Wo': 8.0,
     'L2_xattn_bo': 64.0,
     'L2_ffn_shared_w1': 8.0,
     'L2_ffn_shared_w2': 8.0,
     'L2_ffn_experts_w1': 8.0,
     'L2_ffn_experts_w2': 8.0,
     'L2_ffn_gate_w': 8.0,
     'L3_xattn_Wq': 8.0,
     'L3_xattn_Wk': 8.0,
     'L3_xattn_Wv': 8.0,
     'L3_xattn_Wo': 8.0,
     'L3_ffn_Wg_DN': 8.0,
     'L3_ffn_Wl1_ND2H': 8.0,
     'L3_ffn_Wl2_NHD': 8.0}
    for name, (base, spread) in spreads.items():
        noise = np.random.default_rng([zlib.crc32(name.encode()), seed]).standard_normal(out[name].shape)
        drawn = base * np.exp(spread * noise) if base else spread * noise
        out[name] = jnp.asarray(drawn.astype(out[name].dtype))
    for name, factor in factors.items():
        out[name] = (out[name] * factor).astype(out[name].dtype)
    return out
```

```python
import concourse.bass as bass
from concourse import mybir
from contextlib import ExitStack

F32 = mybir.dt.float32
I32 = mybir.dt.int32
U32 = mybir.dt.uint32
U8 = mybir.dt.uint8
ACT = mybir.ActivationFunctionType
ALU = mybir.AluOpType
AX = mybir.AxisListType
ds = bass.ds

P = 128
NB = 16
D = 128
NK = 77
C = 96
H = 16
UH = 4
NU = H // UH
UNITS = NB * NU
UW = UH * NK
KW = H * NK
E = 8
NT = NB * P
EPS = 1e-5
RSQRT_MAGIC = 1597463007.0
FLT_MAX = 3.4028234663852886e38
BELOW_ALL = -3.0e38
LAST = 8

CAP = int(1.25 * NT / E)
CAP_ROWS = E * CAP
TILES2 = (2 * NT + E * (P - 1)) // P
TILES2 += TILES2 % 2
TILES3 = (NT + (E - 1) * (P - 1)) // P
TILES3 += TILES3 % 2
F0 = 512
F1 = 384
F2 = 512
F3 = 256
T_CHUNKS = ((0, 6), (6, 11), (11, 16))
OB = 65


def spread(ap, dim, n):
    shape = list(ap.shape)
    assert shape[dim] == 1
    shape[dim] = n
    return ap.broadcast_to(shape)


class Attention:
    def __init__(self, n, wide, scale, bias, mask, wide_n=None, nar_n=None):
        self.n, self.unit0, self.batch0 = n, n * UNITS, n * NB
        self.wide, self.scale, self.bias, self.mask = wide, scale, bias, mask
        self.wide_n, self.nar_n = wide_n, nar_n
        self.x_out = None
        self.oT0 = self.v0 = self.q0 = self.c0 = self.b0 = 0


class Routing:
    def __init__(self, n, layer, k, experts, rows, outs, total, x_in):
        self.n, self.layer, self.k, self.experts = n, layer, k, experts
        self.rows, self.outs, self.total, self.x_in = rows, outs, total, x_in
        self.tiles = total // P
        self.scatter0 = 0


class MlpRun:
    def __init__(self, name, tiles, width, gated, w1, w2, expert, src, R=None):
        self.name, self.tiles, self.width, self.gated = name, tiles, width, gated
        self.w1, self.w2, self.expert, self.src, self.R = w1, w2, expert, src, R
        self.at = self.gates0 = self.in0 = self.rows0 = self.stored0 = 0


class Chain:

    def __init__(self, eng, sem):
        self.eng, self.sem, self.base, self.n = eng, sem, 0, 0

    def link(self, ins):
        ins.then_inc(self.sem, 1)
        self.n += 1
        self.eng.wait_ge(self.sem, self.base + self.n)

    def enter(self, it, steps):
        self.before, self.steps = self.base + self.n, steps
        self.resume(it)

    def resume(self, it):
        self.base, self.n = self.before + it * self.steps, 0

    def leave(self, count):
        assert self.n == self.steps, (self.n, self.steps)
        self.base, self.n = self.before + count * self.steps, 0


class Turns:

    def __init__(self, eng, filled, emptied, banks):
        self.eng, self.filled, self.emptied, self.banks, self.n = eng, filled, emptied, banks, 0

    def bank(self):
        return self.banks[self.n % len(self.banks)]

    def claim(self):
        if self.n >= len(self.banks):
            self.eng.wait_ge(self.emptied, self.n - len(self.banks) + 1)
        return self.bank()

    def fill(self, ins):
        ins.then_inc(self.filled, 1)
        self.n += 1

    def take(self):
        self.eng.wait_ge(self.filled, self.n + 1)
        return self.bank()

    def empty(self, ins):
        ins.then_inc(self.emptied, 1)
        self.n += 1

    def settle(self):
        self.eng.wait_ge(self.emptied, self.n)


def build(nc, A, out, last_layer=8):
    ctx = ExitStack()
    with ctx:
        def sb(name, shape, dt=F32):
            return ctx.enter_context(nc.sbuf_tensor(name, shape, dt))

        def sem(name):
            return ctx.enter_context(nc.semaphore(name))

        bank = [ctx.enter_context(nc.psum_tensor(f"bank{i}", [P, 512], F32)) for i in range(8)]
        S_BANK, PT_BANK = bank[0:2], bank[2:4]
        O_BANK, V_BANK, TR_BANK, Y_BANK = bank[4], bank[5], bank[6], bank[7]
        ON_BANK = bank[4:6]

        ident = sb("ident", [P, P])
        earlier = sb("earlier", [P, P])
        ones = sb("ones", [P, P])
        headmask = sb("headmask", [P, H])
        desc8 = sb("desc8", [P, NB, E])
        tileno = sb("tileno", [P, TILES2, E])
        steps128 = sb("steps128", [P, E, NB])
        trash = sb("trash", [P, 2, NB])
        X = sb("X", [P, NT])
        XN = sb("XN", [P, NT])
        CT = sb("CT", [C + 1, KW])
        R1 = sb("R1", [P, NB * KW])
        RP = sb("RP", [P, 3840])
        RV = sb("RV", [P, 2 * H * OB])
        RM = sb("RM", [P, H * D])
        RA = sb("RA", [P, 3296])
        RH = sb("RH", [P, 3072])
        RW = sb("RW", [P, 2304])
        wv = sb("wv", [C, H * 64])
        wo = sb("wo", [P, 8, D])
        nwq = [sb(f"nwq{i}", [P, D]) for i in range(2)]
        nwk = [sb(f"nwk{i}", [C + 1, D]) for i in range(2)]
        nwv = [sb(f"nwv{i}", [C + 1, D]) for i in range(2)]
        nwo = [sb(f"nwo{i}", [P, D]) for i in range(2)]
        bq2 = sb("bq2", [P, 1])
        bo_rows = [sb(f"bo_rows{i}", [P, D]) for i in range(3)]
        wr = [sb(f"wr{i}", [P, E]) for i in range(3)]
        br_rows = sb("br_rows", [P, E])
        b1c = sb("b1c", [P, E * 4])
        mask8 = sb("mask8", [P, KW], U8)
        qT = [sb(f"qT{i}", [P, P]) for i in range(2)]
        mxT = [sb(f"mxT{i}", [P, P]) for i in range(2)]
        ln_stats = sb("ln_stats", [P, 2, 6])
        ln_mv = sb("ln_mv", [P, 2, 2])
        ln_ve = sb("ln_ve", [P, 2])
        ln_r = sb("ln_r", [P, 2])
        ln_t = sb("ln_t", [P, 2])
        xn = [sb(f"xn{i}", [P, D]) for i in range(2)]
        xnT = [sb(f"xnT{i}", [P, P]) for i in range(2)]
        cts = [sb(f"cts{i}", [C, NK]) for i in range(2)]
        mx = [sb(f"mx{i}", [P, UH]) for i in range(2)]
        rsum = [sb(f"rsum{i}", [P, UH]) for i in range(2)]
        rt = {n: sb(f"rt_{n}", [P, NB, E]) for n in
              "score work pick1 pick2 both pos tot cum cum2".split()}
        rc = {n: sb(f"rc_{n}", [P, NB]) for n in
              "best1 best2 first1 first2 place1 place2 keep1 keep2 gate1 gate2 sum inv diff".split()}
        to_row = [sb(f"to_row{k}", [P, NB], U32) for k in range(2)]
        from_row = [sb(f"from_row{k}", [P, NB], U32) for k in range(2)]
        ec = {n: sb(f"ec_{n}", [P, E]) for n in "count tiles end end2 start".split()}
        ecmp = sb("ecmp", [P, E * NB])
        tcmp = sb("tcmp", [P, TILES2 * E])
        texp = sb("texp", [P, TILES2])
        texp_i = sb("texp_i", [P, TILES2], I32)
        got = [sb(f"got{i}", [P, D]) for i in range(4)]

        T_all = R1
        wq_nat = RP[:, 0:1024]
        wk_nat = RP[0:C, 1024:2048]
        wqT = RP[:, 2048:3072].rearrange("p (j d) -> p j d", j=8)
        wkT = RP[:, 3072:3840].rearrange("p (j c) -> p j c", j=8)
        bufT = RP[:, 0:CAP_ROWS]
        kbd = [RP[:, i * KW:(i + 1) * KW] for i in range(2)]
        vw = [RV[0:NK, i * H * OB:(i + 1) * H * OB].rearrange("k (h e) -> k h e", h=H) for i in range(2)]
        v_narrow = RV[0:NK, 0:NB * D]
        MT = RM[0:C, :].rearrange("c (h d) -> c h d", h=H)
        kT_all = RM[:, 0:KW]
        ctx_nat = R1[0:NK, 0:NB * C].rearrange("k (b c) -> k b c", b=NB)

        def ra(at, n):
            return RA[:, at:at + n]
        Z = [ra(i * UW, UW) for i in range(2)]
        PR = [ra(2 * UW + i * UW, UW) for i in range(2)]
        PT = [RA[0:NK, 4 * UW + i * 512:4 * UW + (i + 1) * 512].rearrange("k (h q) -> k h q", h=UH) for i in range(2)]
        ON = [ra(4 * UW + 1024 + i * 256, 256) for i in range(2)]
        OT = [ra(4 * UW + 1536 + i * 256, 256).rearrange("p (j q) -> p j q", j=2) for i in range(2)]
        OTn = [ra(4 * UW + 1024 + i * P, P) for i in range(2)]
        rden = ra(4 * UW + 1280, P)
        SM = [XN[:, i * UW:(i + 1) * UW] for i in range(2)]
        rows0 = RA[:, 0:CAP_ROWS].rearrange("p (t d) -> p t d", d=D)

        w1s = [RW[:, i * 512:(i + 1) * 512] for i in range(2)]
        w2s = [RW[:, 1024 + i * 512:1024 + (i + 1) * 512].rearrange("p (f d) -> p f d", f=4) for i in range(2)]
        hT0 = [RH[:, i * 1280:(i + 1) * 1280].rearrange("p (f t) -> p f t", f=4) for i in range(2)]
        o0 = [RA[:, i * 384:(i + 1) * 384].rearrange("p (r d) -> p r d", r=3) for i in range(2)]
        b2_rows = RA[:, 768:768 + E * D]
        w1n = RW[:, 0:1152]
        wgu1 = RW[:, 1152:1152 + 768]
        wd1 = RW[:, 1920:2304].rearrange("p (j d) -> p j d", j=3)
        notmask = RW[:, 0:KW]
        hid = [RH[:, i * 512:(i + 1) * 512] for i in range(2)]
        gate = [RH[:, 1024 + i * 384:1024 + (i + 1) * 384] for i in range(2)]
        hidT = [RH[:, 1792 + i * 512:1792 + (i + 1) * 512].rearrange("p (j t) -> p j t", j=4) for i in range(2)]
        vbd = [R[0:NK, at:at + 16 * 136] for R, at in ((RH, 0), (R1, 34 * 512))]
        vbd_steps = [v_.rearrange("k (h x) -> k h x", x=136) for v_ in vbd]
        row_in = [sb(f"row_in{i}", [P, D]) for i in range(2)]
        row_out = [sb(f"row_out{i}", [P, D]) for i in range(2)]
        w1_2 = R1[:, 0:9 * 512]
        w2_2 = R1[:, 9 * 512:18 * 512]
        nat2 = [R1[:, (18 + i) * 512:(19 + i) * 512] for i in range(4)]
        w1_3 = R1[:, 22 * 512:30 * 512]
        w2_3 = R1[:, 30 * 512:34 * 512]

        rows_d = [nc.dram_tensor(f"rows{i}", [n + (2 * NT if i == 0 else 0), D], F32, kind="Internal")
                  for i, n in enumerate((CAP_ROWS, TILES2 * P, TILES3 * P))]
        outs_d = [nc.dram_tensor(f"outs{i}", [n, D], F32, kind="Internal")
                  for i, n in enumerate((CAP_ROWS, TILES2 * P, TILES3 * P))]
        zero_tile = sb("zero_tile", [P, D])

        const_step = sem("const_step")
        const_done = sem("const_done")
        loaded = {}

        def arrives(name):
            loaded[name] = sem("loaded_" + name)
            return loaded[name]
        for n in ("x ctx wqk0 wvo0 wqk1 wvo1 narrow2 narrow3 rowsof misc b2 mlp1 mlp3").split():
            arrives(n)
        zeroed, xn_kept = sem("zeroed"), sem("xn_kept")
        filled, emptied = sem("stage_filled"), sem("stage_emptied")
        dve_step = sem("dve_step")
        dve_prepared = sem("dve_prepared")
        xn_ready, xnT_psum, xnT_ready = sem("xn_ready"), sem("xnT_psum"), sem("xnT_ready")
        q_psum, q_ready = sem("q_psum"), sem("q_ready")
        cts_ready, kbd_ready, bias_added = sem("cts_ready"), sem("kbd_ready"), sem("bias_added")
        vbd_ready = sem("vbd_ready")
        v_psum, v_ready = sem("v_psum"), sem("v_ready")
        s_psum, z_ready, p_ready = sem("s_psum"), sem("z_ready"), sem("p_ready")
        pT_psum, pT_ready = sem("pT_psum"), sem("pT_ready")
        o_psum, on_ready = sem("o_psum"), sem("on_ready")
        oT_psum, oT_ready, y_psum = sem("oT_psum"), sem("oT_ready"), sem("y_psum")
        x_done = [sem(f"x_done{i}") for i in range(4)]
        rn_ready, rnT_psum, rnT_ready, logits_psum = sem("rn_ready"), sem("rnT_psum"), sem("rnT_ready"), sem("logits_psum")
        exps_in, exps_out = sem("exps_in"), sem("exps_out")
        picked, ranked = sem("picked"), sem("ranked")
        routed = sem("routed")
        scattered = sem("scattered")
        rows_loaded = [sem(f"rows_loaded{i}") for i in range(2)]
        gathered = [sem(f"gathered{i}") for i in range(4)]
        combined = sem("combined")
        stored = [sem(f"stored{i}") for i in range(2)]
        w_loaded = [sem(f"w_loaded{i}") for i in range(2)]
        h0_psum, h0_ready, o0_psum, o0_ready = sem("h0_psum"), sem("h0_ready"), sem("o0_psum"), sem("o0_ready")
        m_in, mT_psum, mT_ready = sem("m_in"), sem("mT_psum"), sem("mT_ready")
        m1_psum, g_ready, h_ready = sem("m1_psum"), sem("g_ready"), sem("h_ready")
        hT_psum, hT_ready, m2_psum, m2_done = sem("hT_psum"), sem("hT_ready"), sem("m2_psum"), sem("m2_done")
        nat_loaded = [sem(f"nat_loaded{i}") for i in range(4)]
        written = sem("written")

        def attention(n, **k):
            return Attention(n, **k)
        ATT = [attention(0, wide=True, scale=64 ** -0.5, bias=0, mask=False, wide_n=0),
               attention(1, wide=True, scale=64 ** -0.5, bias=1, mask=False, wide_n=1),
               attention(2, wide=False, scale=8 ** -0.5, bias=2, mask=False, nar_n=0),
               attention(3, wide=False, scale=8 ** -0.5, bias=None, mask=True, nar_n=1)]
        for L in ATT:
            L.x_out = x_done[L.n]
            L.oT0 = sum(UNITS if K.wide else 0 for K in ATT[:L.n])
            L.on0 = sum(UNITS if K.wide else 2 * NB for K in ATT[:L.n])
            L.v0 = sum(2 * NB if K.wide else 0 for K in ATT[:L.n])
            L.q0 = sum(0 if K.wide else NB for K in ATT[:L.n])
            L.c0 = sum(NB if K.wide else 0 for K in ATT[:L.n])
            L.b0 = sum(NB if K.bias is not None else 0 for K in ATT[:L.n])
        RT = [Routing(n=0, layer=0, k=2, experts=8, rows=rows_d[0], outs=outs_d[0], total=CAP_ROWS, x_in=0),
              Routing(n=1, layer=2, k=2, experts=8, rows=rows_d[1], outs=outs_d[1], total=TILES2 * P, x_in=4),
              Routing(n=2, layer=3, k=1, experts=7, rows=rows_d[2], outs=outs_d[2], total=TILES3 * P, x_in=6)]
        for R in RT:
            R.tiles = R.total // P
            R.scatter0 = sum(16 * NB * K.k for K in RT[:R.n])
        runs = [MlpRun(name="mlp1", tiles=NB, width=F1, gated=True, w1=wgu1, w2=wd1, expert=None, src="norm"),
                MlpRun(name="shared2", tiles=NB, width=F2, gated=False, w1=w1_2, w2=w2_2, expert=8, src="norm"),
                MlpRun(name="routed2", tiles=TILES2, width=F2, gated=False, w1=w1_2, w2=w2_2, expert="table", src="rows", R=RT[1]),
                MlpRun(name="shared3", tiles=NB, width=F3, gated=True, w1=w1_3, w2=w2_3, expert=7, src="norm"),
                MlpRun(name="routed3", tiles=TILES3, width=F3, gated=True, w1=w1_3, w2=w2_3, expert="table", src="rows", R=RT[2])]
        MLP1, SH2, RO2, SH3, RO3 = runs
        at = gated = entered = 0
        for r in runs:
            r.at, r.gates0, r.in0 = at, gated, entered
            at += r.tiles
            gated += r.tiles if r.gated else 0
            entered += r.tiles if r.src == "norm" else 0
        RO2.rows0, RO2.stored0 = 1, 32 * (E // 2)
        RO3.rows0, RO3.stored0 = 1 + TILES2 // 2, 32 * (E // 2) + 16 * (TILES2 // 2)
        STORED_END = [RO2.stored0, RO3.stored0, RO3.stored0 + 16 * (TILES3 // 2)]
        COMBINE0 = [0, 2 * NB, 4 * NB]

        def x_ready(layer, n):
            if layer % 2 == 0:
                return x_done[layer // 2], n
            if layer == 3:
                return m2_done, MLP1.at + n
            return combined, COMBINE0[layer // 3 if layer < 7 else 2] + n * (1 if layer == 7 else 2)

        STAGE_END, filled_n = {}, 0
        for name, n, layer in (("ct", 4, 1), ("small", 2, 1), ("m0", 8, 1), ("t0", 48, 1), ("m1", 8, 3), ("narrow2", 4, 1),
                               ("t1", 48, 3), ("rows", CAP_ROWS // 512, 2), ("mlp1", 3, 4), ("kv2", 7, 5),
                               ("nat2", 18, 6), ("kv3", 7, 7)):
            if last_layer >= layer:
                filled_n += n
            STAGE_END[name] = filled_n

        block = ctx.enter_context(nc.Block())

        def bcast(src, n):
            return bass.AP(src.tensor, src.offset, [[0, P], [1, n]])

        @block.sync
        def _(sp):
            def load(dst, src, name):
                sp.dma_start(dst, src).then_inc(loaded[name], 16)

            sp.dma_start(X[:, :].rearrange("p (b d) -> p b d", b=NB), A["x"].rearrange("b s d -> s b d")).then_inc(loaded["x"], 16)
            load(ctx_nat, A["ctx_768"].rearrange("b k c -> k b c"), "ctx")
            load(wq_nat, A["L0_xattn_Wq"], "wqk0")
            load(wk_nat, A["L0_xattn_Wkv"][:, 0:1024], "wqk0")
            load(wv[:, :], A["L0_xattn_Wkv"][:, 1024:2048], "wvo0")
            load(wo[:, :, :], A["L0_xattn_Wproj"].rearrange("(j p) d -> p j d", p=P), "wvo0")
            for i, name in enumerate(("L0_xattn_bproj", "L1_xattn_bo", "L2_xattn_bo")):
                load(bo_rows[i][:, :], bcast(A[name], D), "rowsof")
            load(br_rows[:, :], bcast(A["L0_ffn_b_router"], E), "rowsof")
            load(mask8[:, :], bcast(A["mask_BxS2_bf1"], KW), "rowsof")
            load(wr[0][:, :], A["L0_ffn_w_router"], "misc")
            load(wr[2][:, :], A["L3_ffn_Wg_DN"], "misc")
            load(row_in[0][0:32, :], A["L0_ffn_b1"].rearrange("e (f p) -> (e f) p", p=P), "misc")
            load(row_in[1][0:E, :], A["L2_ffn_gate_w"], "misc")
            sp.wait_ge(emptied, STAGE_END["m0"])
            load(wq_nat, A["L1_xattn_Wq"], "wqk1")
            load(wk_nat, A["L1_xattn_Wk"], "wqk1")
            load(got[0][:, :], A["L2_xattn_Wq"], "narrow2")
            load(got[1][:, :], A["L2_xattn_Wo"], "narrow2")
            load(got[2][:, 0:C], A["L2_xattn_Wkv"][0:P, :], "narrow2")
            load(got[3][:, 0:C], A["L2_xattn_Wkv"][P:2 * P, :], "narrow2")
            load(bq2[:, :], A["L2_xattn_bq"].rearrange("(p o) -> p o", o=1), "narrow2")
            bkv = A["L2_xattn_bkv"].rearrange("(o h t e) -> t o h e", o=1, t=2, e=8)
            load(nwk[0][C:C + 1, :].rearrange("o (h e) -> o h e", e=8), bkv[0], "narrow2")
            load(nwv[0][C:C + 1, :].rearrange("o (h e) -> o h e", e=8), bkv[1], "narrow2")
            load(nwq[1][:, :], A["L3_xattn_Wq"], "narrow3")
            load(nwk[1][0:C, :], A["L3_xattn_Wk"], "narrow3")
            load(nwv[1][0:C, :], A["L3_xattn_Wv"], "narrow3")
            load(nwo[1][:, :], A["L3_xattn_Wo"], "narrow3")

            if last_layer >= 2:
                if last_layer >= 3:
                    sp.wait_ge(x_done[0], NB)
                    load(wv[:, :], A["L1_xattn_Wv"], "wvo1")
                    load(wo[:, :, :], A["L1_xattn_Wo"].rearrange("(j p) d -> p j d", p=P), "wvo1")
                sp.wait_ge(zeroed, 16 * 3)
                sp.wait_ge(scattered, RT[0].scatter0 + 16 * NB * RT[0].k)
                half = RT[0].tiles // 2
                for i in range(2):
                    sp.dma_start(rows0[:, i * half:(i + 1) * half, :],
                                 rows_d[0][i * half * P:(i + 1) * half * P, :].rearrange("(t p) d -> p t d", p=P))\
                        .then_inc(rows_loaded[i], 16)

                sp.wait_ge(emptied, STAGE_END["rows"])
                load(b2_rows, bcast(A["L0_ffn_b2"], E * D), "b2")

                def load_expert(it, s):
                    e = 2 * it + s
                    if not isinstance(it, int) or it > 0:
                        sp.wait_ge(o0_psum, 2 * it + s - 1)
                    sp.dma_start(w1s[s], A["L0_ffn_w1"].rearrange("e p f -> p e f")[:, ds(e, 1), :]
                                 .rearrange("p o f -> p (o f)")).then_inc(w_loaded[s], 16)
                    sp.dma_start(w2s[s], A["L0_ffn_w2"].rearrange("e (f p) d -> p e f d", p=P)[:, ds(e, 1), :, :]
                                 .rearrange("p o f d -> p (o f) d")).then_inc(w_loaded[s], 16)
                load_expert(0, 0)
                load_expert(0, 1)
                with sp.Fori(1, E // 2) as it:
                    load_expert(it, 0)
                    load_expert(it, 1)
            if last_layer >= 4:
                sp.wait_ge(o0_psum, E)
                load(w1n.bitcast(I32)[:, 0:384].rearrange("p (j d) -> p j d", j=3), A["L1_ffn_w_gate"].rearrange("(j p) d -> p j d", p=P), "mlp1")
                load(w1n.bitcast(I32)[:, 384:768].rearrange("p (j d) -> p j d", j=3), A["L1_ffn_w_up"].rearrange("(j p) d -> p j d", p=P), "mlp1")
                load(w1n.bitcast(I32)[:, 768:1152], A["L1_ffn_w_down"], "mlp1")
            if last_layer >= 6:
                sp.wait_ge(s_psum, 2 * UNITS)
                for n in range(18):
                    if n >= 4:
                        sp.wait_ge(emptied, STAGE_END["nat2"] - 18 + n - 3)
                    e, second = n // 2, n % 2
                    if second:
                        src = A["L2_ffn_shared_w2"] if e == 8 else A["L2_ffn_experts_w2"][e]
                        sp.dma_start(nat2[n % 4], src).then_inc(nat_loaded[n % 4], 16)
                    else:
                        src = A["L2_ffn_shared_w1"] if e == 8 else A["L2_ffn_experts_w1"][e]
                        sp.dma_start(nat2[n % 4].rearrange("p (j d) -> p j d", j=4),
                                     src.rearrange("(j p) d -> p j d", p=P)).then_inc(nat_loaded[n % 4], 16)
                load(w1_3.rearrange("p (e f) -> p e f", e=E), A["L3_ffn_Wl1_ND2H"].rearrange("e p f -> p e f"), "mlp3")
                load(w2_3.rearrange("p (e j d) -> p e j d", e=E, j=2), A["L3_ffn_Wl2_NHD"].rearrange("e (j p) d -> p e j d", p=P), "mlp3")

            def load_rows(r):
                R = r.R
                sp.wait_ge(scattered, R.scatter0 + 16 * NB * R.k)

                def one(it, s):
                    sp.wait_ge(mT_psum, r.at + 2 * it + s - 1)
                    sp.dma_start(row_in[s][:, :], R.rows[ds((2 * it + s) * P, P), :]).then_inc(rows_loaded[s], 16)
                with sp.Fori(0, r.tiles // 2) as it:
                    one(it, 0)
                    one(it, 1)
            if last_layer >= 6:
                load_rows(RO2)
            if last_layer >= 8:
                load_rows(RO3)

            with sp.Fori(0, NB) as b:
                sp.wait_ge(*x_ready(last_layer - 1, b + 1))
                sp.dma_start(out.rearrange("b s d -> s b d")[:, ds(b, 1), :].rearrange("s o d -> s (o d)"), X[:, ds(b * D, D)]).then_inc(written, 16)
            sp.wait_ge(written, 16 * NB)

        @block.gpsimd
        def _(pool):
            g = nc.gpsimd
            c = Chain(pool, const_step)
            c.link(g.memset(zero_tile[:, :], 0.0))
            for i, n in enumerate((CAP_ROWS, TILES2 * P, TILES3 * P)):
                view = rows_d[i][0:n, :].rearrange("(t p) d -> p t d", p=P)
                z = spread(zero_tile[:, :].rearrange("p (o d) -> p o d", o=1), 1, n // P)
                pool.dma_start(view, z).then_inc(zeroed, 16)
            c.link(g.memset(ones[:, :], 1.0))
            c.link(g.memset(CT[C:C + 1, :], 1.0))
            c.link(g.memset(ident[:, :], 0.0))
            c.link(g.affine_select(out=ident[:, :], in_=ident[:, :], compare_op=ALU.not_equal, fill=1.0,
                                   base=0, pattern=[[-1, P]], channel_multiplier=1))
            c.link(g.memset(earlier[:, :], 0.0))
            c.link(g.affine_select(out=earlier[:, :], in_=earlier[:, :], compare_op=ALU.is_ge, fill=1.0,
                                   base=0, pattern=[[-1, P]], channel_multiplier=1))
            c.link(g.memset(headmask[:, :], 1.0))
            c.link(g.affine_select(out=headmask[:, :], in_=headmask[:, :], compare_op=ALU.is_ge, fill=0.0,
                                   base=0, pattern=[[-8, H]], channel_multiplier=1))
            c.link(g.affine_select(out=headmask[:, :], in_=headmask[:, :], compare_op=ALU.is_ge, fill=0.0,
                                   base=7, pattern=[[8, H]], channel_multiplier=-1))
            scratch_i = texp_i
            c.link(g.iota(tcmp[:, 0:NB * E].bitcast(I32).rearrange("p (t e) -> p t e", e=E), pattern=[[0, NB], [-1, E]], base=8, channel_multiplier=0))
            c.link(g.tensor_copy(desc8[:, :, :], tcmp[:, 0:NB * E].bitcast(I32).rearrange("p (t e) -> p t e", e=E)))
            c.link(g.iota(tcmp[:, :].bitcast(I32).rearrange("p (t e) -> p t e", e=E), pattern=[[1, TILES2], [0, E]], base=0, channel_multiplier=0))
            c.link(g.tensor_copy(tileno[:, :, :], tcmp[:, :].bitcast(I32).rearrange("p (t e) -> p t e", e=E)))
            c.link(g.iota(ecmp[:, :].bitcast(I32).rearrange("p (e j) -> p e j", e=E), pattern=[[0, E], [P, NB]], base=0, channel_multiplier=0))
            c.link(g.tensor_copy(steps128[:, :, :], ecmp[:, :].bitcast(I32).rearrange("p (e j) -> p e j", e=E)))
            picks = scratch_i[:, 0:2 * NB].rearrange("p (k t) -> p k t", k=2)
            c.link(g.iota(picks, pattern=[[NT, 2], [P, NB]], base=CAP_ROWS, channel_multiplier=1))
            g.tensor_copy(trash[:, :, :], picks).then_inc(const_done, 1)

            def pool_attention(L):
                def one(it, s, first):
                    b = 2 * it + s
                    if L.wide:
                        if not first:
                            pool.wait_ge(v_psum, L.v0 + 2 * (b - 2) + 2)
                        g.tensor_copy(cts[s][:, :], CT[0:C, ds(b * NK, NK)]).then_inc(cts_ready, 1)
                    else:
                        if not first:
                            pool.wait_ge(s_psum, L.unit0 + NU * (b - 2) + NU)
                        g.tensor_tensor(kbd[s].rearrange("p (h k) -> p h k", h=H),
                                        spread(kT_all[:, ds(b * NK, NK)].rearrange("p (o k) -> p o k", o=1), 1, H),
                                        spread(headmask[:, :].rearrange("p (h o) -> p h o", o=1), 2, NK),
                                        ALU.mult).then_inc(kbd_ready, 1)
                        if not first:
                            pool.wait_ge(o_psum, L.unit0 + NU * (b - 2) + NU)
                        g.tensor_copy(vbd_steps[s][:, :, 0:8], v_narrow[:, ds(b * D, D)].rearrange("k (h e) -> k h e", e=8))\
                            .then_inc(vbd_ready, 1)

                def bias(b):
                    pool.wait_ge(xn_ready, L.batch0 + b + 1)
                    g.tensor_tensor(X[:, ds(b * D, D)], X[:, ds(b * D, D)], bo_rows[L.bias][:, :], ALU.add).then_inc(bias_added, 1)
                if L.wide:
                    pool.wait_ge(emptied, STAGE_END["ct"])
                else:
                    pool.wait_ge(emptied, STAGE_END[f"kv{L.n}"])
                    for s in range(2):
                        c.link(g.memset(vbd[s], 0.0))
                        c.link(g.memset(vbd_steps[s][:, 0:8, 64:72], 1.0))
                        c.link(g.memset(vbd_steps[s][:, 7:15, 72:80], 1.0))
                one(0, 0, True)
                one(0, 1, True)
                if L.bias is not None:
                    bias(0)
                    bias(1)
                with pool.Fori(1, NB // 2) as it:
                    one(it, 0, False)
                    one(it, 1, False)
                    if L.bias is not None:
                        bias(2 * it)
                        bias(2 * it + 1)

            def scatter(R):
                pool.wait_ge(zeroed, 16 * 3)
                pool.wait_ge(routed, R.n + 1)
                for t in range(NB):
                    for k in range(R.k):
                        g.indirect_dma_start(R.rows[:, :], bass.IndirectOffsetOnAxis(ap=to_row[k][:, t:t + 1], axis=0),
                                             XN[:, t * D:(t + 1) * D], None).then_inc(scattered, 16)
                pool.wait_ge(scattered, R.scatter0 + 16 * NB * R.k)

            def gather(R):
                for s in range(2):
                    pool.wait_ge(stored[s], STORED_END[R.n])
                n = 0
                for t in range(NB):
                    for k in range(R.k):
                        s = n % 4
                        if n >= 4:
                            pool.wait_ge(combined, COMBINE0[R.n] + n - 3)
                        g.indirect_dma_start(got[s][:, :], None, R.outs[0:R.total, :],
                                             bass.IndirectOffsetOnAxis(ap=from_row[k][:, t:t + 1], axis=0)).then_inc(gathered[s], 16)
                        n += 1

            def copy_in(r):
                def one(it, s, first):
                    if not first:
                        pool.wait_ge(mT_psum, r.at + 2 * it + s - 1)
                    g.tensor_copy(row_in[s][:, :], XN[:, ds((2 * it + s) * D, D)]).then_inc(m_in, 1)
                one(0, 0, False)
                one(0, 1, False)
                with pool.Fori(1, NB // 2) as it:
                    one(it, 0, False)
                    one(it, 1, False)

            def store_rows(r):
                def one(it, s):
                    pool.wait_ge(m2_done, r.at + 2 * it + s + 1)
                    pool.dma_start(r.R.outs[ds((2 * it + s) * P, P), :], row_out[s][:, :]).then_inc(stored[s], 16)
                with pool.Fori(0, r.tiles // 2) as it:
                    one(it, 0)
                    one(it, 1)

            pool_attention(ATT[0])
            if last_layer >= 2:
                scatter(RT[0])
                def store0(it, s):
                    e = 2 * it + s
                    pool.wait_ge(o0_ready, e + 1)
                    pool.dma_start(outs_d[0][ds(e * CAP, 2 * P), :].rearrange("(r p) d -> p r d", p=P), o0[s][:, 0:2, :]).then_inc(stored[s], 16)
                    pool.dma_start(outs_d[0][ds(e * CAP + 2 * P, CAP - 2 * P), :], o0[s][0:CAP - 2 * P, 2, :]).then_inc(stored[s], 16)
                with pool.Fori(0, E // 2) as it:
                    store0(it, 0)
                    store0(it, 1)
                gather(RT[0])
            if last_layer >= 3:
                pool_attention(ATT[1])
            if last_layer >= 5:
                pool_attention(ATT[2])
            if last_layer >= 6:
                scatter(RT[1])
                copy_in(SH2)
                store_rows(RO2)
                gather(RT[1])
            if last_layer >= 7:
                pool_attention(ATT[3])
            if last_layer >= 8:
                scatter(RT[2])
                copy_in(SH3)
                store_rows(RO3)
                gather(RT[2])

        @block.tensor
        def _(pe):
            st = Turns(pe, filled, emptied, bank[0:4])
            mm, tp = nc.tensor.matmul, nc.tensor.transpose

            def prepare_m(n):
                pe.wait_ge(loaded[f"wqk{n}"], 32)
                for half in range(2):
                    b = st.claim()
                    for i in range(4):
                        j = 4 * half + i
                        last = tp(b[:, i * P:(i + 1) * P], wq_nat[:, j * P:(j + 1) * P], ident[:, :])
                    st.fill(last)
                for half in range(2):
                    b = st.claim()
                    for i in range(4):
                        j = 4 * half + i
                        last = tp(b[:, i * C:(i + 1) * C], wk_nat[:, j * P:(j + 1) * P], ident[0:C, 0:C])
                    st.fill(last)
                st.settle()
                for q in range(4):
                    b = st.claim()
                    for i in range(4):
                        h = 8 * (q // 2) + 2 * i + q % 2
                        at = 64 * (h % 2)
                        last = mm(b[0:C, i * D:(i + 1) * D], wkT[at:at + 64, h // 2, :], wqT[at:at + 64, h // 2, :],
                                  start=True, stop=True)
                    st.fill(last)
                st.settle()

            def make_t():
                for h in range(H):
                    for b0, b1 in T_CHUNKS:
                        b = st.claim()
                        st.fill(mm(b[:, 0:(b1 - b0) * NK], MT[:, h, :], CT[0:C, b0 * NK:b1 * NK], start=True, stop=True))
                st.settle()

            def pe_attention(L):
                wide = L.wide

                def turn_x(b, s):
                    pe.wait_ge(xn_ready, L.batch0 + b + 1)
                    if not isinstance(b, int) or b > 0:
                        pe.wait_ge(xnT_ready, L.batch0 + b)
                    tp(TR_BANK[:, 0:P], xn[s][:, :], ident[:, :]).then_inc(xnT_psum, 1)

                def query(b, s):
                    pe.wait_ge(xnT_ready, L.batch0 + b + 1)
                    mm(TR_BANK[:, 0:P], nwq[L.nar_n][:, :], xnT[s][:, :], start=True, stop=True).then_inc(q_psum, 1)

                def values(b, s, half):
                    if half == 0:
                        pe.wait_ge(cts_ready, L.c0 + b + 1)
                    n = 2 * b + half
                    if not isinstance(b, int) or b > 0 or half:
                        pe.wait_ge(v_ready, L.v0 + n)
                    mm(V_BANK[0:NK, :], cts[s][:, :], wv[:, half * 512:(half + 1) * 512],
                       start=True, stop=True).then_inc(v_psum, 1)

                def scores(U, b, s, u):
                    if u == 0:
                        if wide:
                            pe.wait_ge(xnT_ready, L.batch0 + b + 1)
                        else:
                            pe.wait_ge(q_ready, L.q0 + b + 1)
                            pe.wait_ge(kbd_ready, L.q0 + b + 1)
                    if not isinstance(U, int) or U >= 2:
                        pe.wait_ge(z_ready, L.unit0 + U - 1)
                    rhs = T_all[:, ds(b * KW + u * UW, UW)] if wide else kbd[s][:, u * UW:(u + 1) * UW]
                    lhs = xnT[s] if wide else qT[s]
                    mm(S_BANK[u % 2][:, 0:UW], lhs[:, :], rhs, start=True, stop=True).then_inc(s_psum, 1)

                def turn_p(U, u):
                    pe.wait_ge(p_ready, L.unit0 + U + 1)
                    if not isinstance(U, int) or U >= 2:
                        pe.wait_ge(pT_ready, L.unit0 + U - 1)
                    for i in range(UH):
                        last = tp(PT_BANK[u % 2][0:NK, i * P:(i + 1) * P], PR[u % 2][:, i * NK:(i + 1) * NK], ident[:, :])
                    last.then_inc(pT_psum, 1)

                def weigh(U, b, s, u):
                    pe.wait_ge(pT_ready, L.unit0 + U + 1)
                    if wide and u == 0:
                        pe.wait_ge(v_ready, L.v0 + 2 * b + 2)
                    if not wide:
                        if u == 0:
                            pe.wait_ge(vbd_ready, L.q0 + b + 1)
                        if u % 2 == 0 and (not isinstance(b, int) or b > 0):
                            pe.wait_ge(on_ready, L.on0 + 2 * (b - 1) + u // 2 + 1)
                    elif not isinstance(U, int) or U >= 1:
                        pe.wait_ge(on_ready, L.on0 + U)
                    for i in range(UH):
                        h = u * UH + i
                        if wide:
                            last = mm(O_BANK[:, i * OB:(i + 1) * OB], PT[u % 2][:, i, :], vw[s][:, h, :], start=True, stop=True)
                        else:
                            last = mm(ON_BANK[u // 2][:, 0:P], vbd[s][:, h * P:(h + 1) * P], PT[u % 2][:, i, :],
                                      start=(h % 8 == 0), stop=(h % 8 == 7))
                    last.then_inc(o_psum, 1)

                def project(U, b, s, u):
                    if wide:
                        pe.wait_ge(oT_ready, L.oT0 + U + 1)
                        if u == 0 and (not isinstance(b, int) or b > 0):
                            pe.wait_ge(L.x_out, b)
                        for j in range(2):
                            last = mm(Y_BANK[:, 0:D], OT[u % 2][:, j, :], wo[:, 2 * u + j, :],
                                      start=(u == 0 and j == 0), stop=(u == NU - 1 and j == 1))
                        if u == NU - 1:
                            last.then_inc(y_psum, 1)
                    elif u == NU - 1:
                        pe.wait_ge(on_ready, L.on0 + 2 * b + 2)
                        if not isinstance(b, int) or b > 0:
                            pe.wait_ge(L.x_out, b)
                        mm(Y_BANK[:, 0:D], OTn[s][:, :], nwo[L.nar_n][:, :], start=True, stop=True).then_inc(y_psum, 1)

                def steps(it):
                    for k in range(2 * NU):
                        U = 2 * NU * it + k

                        def stage(lag):
                            V = U - lag
                            kk = k - lag
                            bb = 2 * it + kk // NU
                            if isinstance(V, int) and not 0 <= V < UNITS:
                                return None
                            return V, bb, (kk // NU) % 2, kk % NU
                        if a := stage(0):
                            scores(*a)
                        if a := stage(1):
                            turn_p(a[0], a[3])
                        if a := stage(2):
                            weigh(*a)
                        if wide and (a := stage(3)):
                            V, b, s, u = a
                            pe.wait_ge(on_ready, L.on0 + V + 1)
                            nb = 2 * it + (k - 2) // NU + 2
                            if isinstance(nb, int):
                                nb = min(max(nb, 1), NB)
                            pe.wait_ge(xnT_ready, L.batch0 + nb)
                            if not isinstance(V, int) or V >= 1:
                                pe.wait_ge(oT_ready, L.oT0 + V)
                            for j in range(2):
                                last = tp(TR_BANK[:, j * P:(j + 1) * P], ON[u % 2][:, j * P:(j + 1) * P], ident[:, :])
                            last.then_inc(oT_psum, 1)
                        if a := stage(4):
                            project(*a)
                        b1 = 2 * it + k // NU + 1
                        if isinstance(b1, int) and b1 >= NB:
                            continue
                        s1 = (k // NU + 1) % 2
                        u = k % NU
                        if u == 1:
                            if wide:
                                done = 2 * NU * it + k - 2
                                if not isinstance(done, int) or done >= 1:
                                    pe.wait_ge(oT_ready, L.oT0 + done)
                            else:
                                pe.wait_ge(q_ready, L.q0 + b1)
                            turn_x(b1, s1)
                        if wide and u >= 2:
                            values(b1, s1, u - 2)
                        if not wide and u == 3:
                            query(b1, s1)

                turn_x(0, 0)
                if wide:
                    pe.wait_ge(loaded[f"wvo{L.wide_n}"], 32)
                    values(0, 0, 0)
                    values(0, 0, 1)
                else:
                    query(0, 0)
                steps(0)
                with pe.Fori(1, NB // 2 - 1) as it:
                    steps(it)
                steps(NB // 2 - 1)
                steps(NB // 2)

            def pe_route(R):
                nr = R.n * NB
                LG = bank[0]

                def one(it, s):
                    b = 2 * it + s
                    tr = (TR_BANK, V_BANK)[s]
                    pe.wait_ge(rn_ready, nr + b + 1)
                    tp(tr[:, 0:P], xn[s][:, :], ident[:, :]).then_inc(rnT_psum, 1)

                def two(it, s):
                    b = 2 * it + s
                    pe.wait_ge(rnT_ready, nr + b + 1)
                    mm(LG[:, ds(b * E, E)], xnT[s][:, :], wr[R.n][:, :], start=True, stop=True).then_inc(logits_psum, 1)
                with pe.Fori(0, NB // 2) as it:
                    one(it, 0)
                    one(it, 1)
                    two(it, 0)
                    two(it, 1)

            def pe_rank(R):
                pe.wait_ge(picked, R.n + 1)
                both = rt["both"][:, :, :].rearrange("p t e -> p (t e)")
                mm(bank[4][:, 0:NB * E], earlier[:, :], both, start=True, stop=True)
                mm(bank[5][:, 0:NB * E], ones[:, :], both, start=True, stop=True).then_inc(ranked, 1)

            def pe_mlp(r):
                w, nj = r.width, r.width // P
                tr, out_b = TR_BANK, Y_BANK
                h_bank = [[bank[0], bank[1]], [bank[2], bank[3]]]
                t_bank = [bank[4], bank[5]]
                table = r.expert == "table"

                def turn(it, s):
                    i = 2 * it + s
                    if r.src == "rows":
                        pe.wait_ge(rows_loaded[s], 16 * (r.rows0 + it + 1))
                    else:
                        pe.wait_ge(m_in, r.in0 + i + 1)
                    src = row_in[s] if r is not MLP1 else xn[s]
                    if r.at or not isinstance(it, int) or i > 0:
                        pe.wait_ge(mT_ready, r.at + i)
                    tp(tr[:, 0:P], src[:, :], ident[:, :]).then_inc(mT_psum, 1)

                def expert(it, s):
                    if not table:
                        return r.expert or 0
                    return pe.value_load(texp_i[0:1, ds(2 * it + s, 1)], min_val=0, max_val=E - 1)

                def first(it, s, e):
                    i = 2 * it + s
                    pe.wait_ge(mT_ready, r.at + i + 1)
                    if not isinstance(it, int) or it > 0:
                        pe.wait_ge(h_ready, r.at + i - 1)
                    if r.gated and w == F1:
                        for k in range(2):
                            last = mm(h_bank[s][k][:, 0:w], mxT[s][:, :], r.w1[:, k * w:(k + 1) * w], start=True, stop=True)
                    elif table:
                        last = mm(h_bank[s][0][:, :], mxT[s][:, :], r.w1[:, ds(e * 512, 512)], start=True, stop=True)
                    else:
                        last = mm(h_bank[s][0][:, :], mxT[s][:, :], r.w1[:, e * 512:(e + 1) * 512], start=True, stop=True)
                    last.then_inc(m1_psum, 1)

                def turn_h(it, s):
                    i = 2 * it + s
                    pe.wait_ge(h_ready, r.at + i + 1)
                    if not isinstance(it, int) or it > 0:
                        pe.wait_ge(hT_ready, r.at + i - 1)
                    for j in range(nj):
                        last = tp(t_bank[s][:, j * P:(j + 1) * P], hid[s][:, j * P:(j + 1) * P], ident[:, :])
                    last.then_inc(hT_psum, 1)

                def second(it, s, e):
                    i = 2 * it + s
                    pe.wait_ge(hT_ready, r.at + i + 1)
                    if not isinstance(it, int) or i > 0:
                        pe.wait_ge(m2_done, r.at + i)
                    for j in range(nj):
                        if r is MLP1:
                            rhs = r.w2[:, j, :]
                        elif table:
                            rhs = r.w2[:, ds(e * w + j * P, P)]
                        else:
                            rhs = r.w2[:, e * w + j * P:e * w + (j + 1) * P]
                        last = mm(out_b[:, 0:D], hidT[s][:, j, :], rhs, start=(j == 0), stop=(j == nj - 1))
                    last.then_inc(m2_psum, 1)

                n2 = r.tiles // 2

                def steps(it):
                    for s in range(2):
                        i = 2 * it + s
                        if not isinstance(i, int) or i < r.tiles:
                            first(it, s, expert(it, s))
                        if not isinstance(i, int) or i + 1 < r.tiles:
                            turn(*((it, 1) if s == 0 else (it + 1, 0)))
                        if not isinstance(i, int) or 1 <= i <= r.tiles:
                            turn_h(*((it - 1, 1) if s == 0 else (it, 0)))
                        if not isinstance(i, int) or 2 <= i <= r.tiles + 1:
                            second(it - 1, s, expert(it - 1, s))
                turn(0, 0)
                steps(0)
                with pe.Fori(1, n2 - 1) as it:
                    steps(it)
                steps(n2 - 1)
                steps(n2)

            def narrow_kv(L):
                n, rows = L.nar_n, C + 1 if L.n == 2 else C
                if L.n == 3:
                    pe.wait_ge(loaded["narrow3"], 64)
                pe.wait_ge(const_done, 1)
                for b0, b1 in T_CHUNKS:
                    b = st.claim()
                    st.fill(mm(b[:, 0:(b1 - b0) * NK], nwk[n][0:rows, :], CT[0:rows, b0 * NK:b1 * NK], start=True, stop=True))
                for q in range(4):
                    b = st.claim()
                    for i in range(4):
                        last = mm(b[0:NK, i * D:(i + 1) * D], CT[0:rows, (4 * q + i) * NK:(4 * q + i + 1) * NK],
                                  nwv[n][0:rows, :], start=True, stop=True)
                    st.fill(last)
                st.settle()

            pe.wait_ge(const_done, 1)
            pe.wait_ge(loaded["ctx"], 16)
            for q in range(4):
                b = st.claim()
                for i in range(4):
                    last = tp(b[0:C, i * NK:(i + 1) * NK], ctx_nat[:, 4 * q + i, :], ident[0:NK, 0:NK])
                st.fill(last)
            pe.wait_ge(loaded["misc"], 16 * 4)
            b = st.claim()
            st.fill(tp(b[:, 0:32], row_in[0][0:32, :], ident[0:32, 0:32]))
            b = st.claim()
            st.fill(tp(b[:, 0:E], row_in[1][0:E, :], ident[0:E, 0:E]))
            prepare_m(0)
            make_t()
            if last_layer >= 3:
                prepare_m(1)
            pe.wait_ge(loaded["narrow2"], 16 * 7)
            for src in (got[0], got[1]):
                b = st.claim()
                st.fill(tp(b[:, 0:P], src[:, :], ident[:, :]))
            for src in (got[2], got[3]):
                b = st.claim()
                st.fill(tp(b[0:C, 0:P], src[:, 0:C], ident[:, :]))
            st.settle()
            pe.wait_ge(dve_prepared, 1)
            pe_attention(ATT[0])
            if last_layer >= 2:
                pe_route(RT[0])
                pe_rank(RT[0])
                if last_layer >= 3:
                    make_t()
                for q in range(RT[0].tiles // 4):
                    if q == 0:
                        pe.wait_ge(rows_loaded[0], 16)
                    if (q + 1) * 4 > RT[0].tiles // 2:
                        pe.wait_ge(rows_loaded[1], 16)
                    b = st.claim()
                    for i in range(4):
                        last = tp(b[:, i * P:(i + 1) * P], rows0[:, 4 * q + i, :], ident[:, :])
                    st.fill(last)
                st.settle()

                def hidden(it, s):
                    e = 2 * it + s
                    pe.wait_ge(w_loaded[s], 32 * (it + 1))
                    for f in range(4):
                        if not isinstance(e, int) or e > 0:
                            pe.wait_ge(h0_ready, 4 * e + f - 3)
                        mm(bank[f][:, 0:CAP], w1s[s][:, f * P:(f + 1) * P], bufT[:, ds(e * CAP, CAP)],
                           start=True, stop=True).then_inc(h0_psum, 1)

                def outputs(it, s):
                    e = 2 * it + s
                    pe.wait_ge(h0_ready, 4 * e + 4)
                    if not isinstance(e, int) or e >= 2:
                        pe.wait_ge(o0_ready, e - 1)
                    ob = bank[4 + s]
                    for q in range(3):
                        n = min(P, CAP - q * P)
                        for f in range(4):
                            last = mm(ob[0:n, q * D:(q + 1) * D], hT0[s][:, f, q * P:q * P + n], w2s[s][:, f, :],
                                      start=(f == 0), stop=(f == 3))
                    last.then_inc(o0_psum, 1)
                hidden(0, 0)
                hidden(0, 1)
                outputs(0, 0)
                with pe.Fori(1, E // 2) as it:
                    hidden(it, 0)
                    outputs(it - 1, 1)
                    hidden(it, 1)
                    outputs(it, 0)
                outputs(E // 2 - 1, 1)
                pe.wait_ge(o0_ready, E)
            if last_layer >= 3:
                pe_attention(ATT[1])
            if last_layer >= 4:
                pe.wait_ge(dve_prepared, 2)
                for k in range(2):
                    b = st.claim()
                    for j in range(3):
                        last = tp(b[:, j * P:(j + 1) * P], w1n[:, k * 384 + j * P:k * 384 + (j + 1) * P], ident[:, :])
                    st.fill(last)
                b = st.claim()
                for j in range(3):
                    last = tp(b[:, j * P:(j + 1) * P], w1n[:, 768 + j * P:768 + (j + 1) * P], ident[:, :])
                st.fill(last)
                st.settle()
                pe_mlp(MLP1)
            if last_layer >= 5:
                narrow_kv(ATT[2])
                pe_attention(ATT[2])
            if last_layer >= 6:
                pe_route(RT[1])
                pe_rank(RT[1])
                pe.wait_ge(routed, 2)
                for n in range(18):
                    pe.wait_ge(nat_loaded[n % 4], 16 * (n // 4 + 1))
                    b = st.claim()
                    for j in range(4):
                        last = tp(b[:, j * P:(j + 1) * P], nat2[n % 4][:, j * P:(j + 1) * P], ident[:, :])
                    st.fill(last)
                st.settle()
                pe_mlp(SH2)
                pe_mlp(RO2)
            if last_layer >= 7:
                pe.wait_ge(m2_done, RO2.at + RO2.tiles)
                narrow_kv(ATT[3])
                pe_attention(ATT[3])
            if last_layer >= 8:
                pe_route(RT[2])
                pe_rank(RT[2])
                pe.wait_ge(routed, 3)
                pe.wait_ge(loaded["mlp3"], 32)
                pe_mlp(SH3)
                pe_mlp(RO3)

        @block.scalar
        def _(act):
            st = Turns(act, filled, emptied, bank[0:4])
            a = nc.scalar.activation

            def copy(o, i):
                return a(o, i, ACT.Copy)

            def prepare_m(n):
                for half in range(2):
                    b = st.take()
                    st.empty(copy(wqT[:, 4 * half:4 * half + 4, :], b[:, :].rearrange("p (j d) -> p j d", j=4)))
                for half in range(2):
                    b = st.take()
                    st.empty(copy(wkT[:, 4 * half:4 * half + 4, :], b[:, 0:4 * C].rearrange("p (j c) -> p j c", j=4)))
                for q in range(4):
                    b = st.take()
                    heads = MT[:, 8 * (q // 2):8 * (q // 2) + 8, :].rearrange("c (i two) d -> c i two d", two=2)
                    st.empty(copy(heads[:, :, q % 2, :], b[0:C, :].rearrange("p (j d) -> p j d", j=4)))

            def make_t():
                for h in range(H):
                    for b0, b1 in T_CHUNKS:
                        b = st.take()
                        o = T_all[:, b0 * KW:b1 * KW].rearrange("p (b h k) -> p b h k", h=H, k=NK)[:, :, h, :]
                        st.empty(copy(o, b[:, 0:(b1 - b0) * NK].rearrange("p (b k) -> p b k", k=NK)))

            def act_attention(L):
                wide = L.wide

                def turned_x(b, s):
                    act.wait_ge(xnT_psum, L.batch0 + b + 1)
                    copy(xnT[s][:, :], TR_BANK[:, 0:P]).then_inc(xnT_ready, 1)

                def query(b, s):
                    act.wait_ge(q_psum, L.q0 + b + 1)
                    if L.n == 2:
                        a(qT[s][:, :], TR_BANK[:, 0:P], ACT.Identity, bias=bq2[:, 0:1]).then_inc(q_ready, 1)
                    else:
                        copy(qT[s][:, :], TR_BANK[:, 0:P]).then_inc(q_ready, 1)

                def values(b, s, half):
                    act.wait_ge(v_psum, L.v0 + 2 * b + half + 1)
                    copy(vw[s][:, half * 8:half * 8 + 8, 0:64], V_BANK[0:NK, :].rearrange("k (h e) -> k h e", h=8)).then_inc(v_ready, 1)

                def steps(it):
                    for k in range(2 * NU):
                        U = 2 * NU * it + k

                        def stage(lag):
                            V = U - lag
                            kk = k - lag
                            if isinstance(V, int) and not 0 <= V < UNITS:
                                return None
                            return V, 2 * it + kk // NU, kk % NU
                        if t := stage(1):
                            V, b, u = t
                            act.wait_ge(pT_psum, L.unit0 + V + 1)
                            copy(PT[u % 2], PT_BANK[u % 2][0:NK, :].rearrange("k (h q) -> k h q", h=UH)).then_inc(pT_ready, 1)
                        if wide and (t := stage(3)):
                            V, b, u = t
                            act.wait_ge(oT_psum, L.oT0 + V + 1)
                            copy(OT[u % 2], TR_BANK[:, 0:256].rearrange("p (j q) -> p j q", j=2)).then_inc(oT_ready, 1)
                        if t := stage(0):
                            V, b, u = t
                            act.wait_ge(z_ready, L.unit0 + V + 1)
                            a(PR[u % 2], Z[u % 2], ACT.Exp, scale=L.scale).then_inc(p_ready, 1)
                        b1 = 2 * it + k // NU + 1
                        if isinstance(b1, int) and b1 >= NB:
                            continue
                        s1 = (k // NU + 1) % 2
                        u = k % NU
                        if u == 1:
                            turned_x(b1, s1)
                        if wide and u >= 2:
                            values(b1, s1, u - 2)
                        if not wide and u == 3:
                            query(b1, s1)
                act.preload_act_table(ACT.Exp)
                turned_x(0, 0)
                if wide:
                    values(0, 0, 0)
                    values(0, 0, 1)
                else:
                    query(0, 0)
                steps(0)
                with act.Fori(1, NB // 2 - 1) as it:
                    steps(it)
                steps(NB // 2 - 1)
                steps(NB // 2)

            def act_route(R):
                nr = R.n * NB

                def one(it, s):
                    b = 2 * it + s
                    act.wait_ge(rnT_psum, nr + b + 1)
                    if not isinstance(it, int) or b >= 2:
                        act.wait_ge(logits_psum, nr + b - 1)
                    copy(xnT[s][:, :], (TR_BANK, V_BANK)[s][:, 0:P]).then_inc(rnT_ready, 1)
                one(0, 0)
                one(0, 1)
                with act.Fori(1, NB // 2) as it:
                    one(it, 0)
                    one(it, 1)
                act.wait_ge(exps_in, R.n + 1)
                if R.n == 1:
                    a(rc["gate2"][:, :], rc["diff"][:, :], ACT.Exp).then_inc(exps_out, 1)
                else:
                    a(rt["score"][:, :, :], rt["work"][:, :, :], ACT.Exp).then_inc(exps_out, 1)

            def act_mlp(r):
                w, nj = r.width, r.width // P
                h_bank = [[bank[0], bank[1]], [bank[2], bank[3]]]

                def turned(it, s):
                    i = 2 * it + s
                    act.wait_ge(mT_psum, r.at + i + 1)
                    if not isinstance(it, int) or it > 0:
                        act.wait_ge(m1_psum, r.at + i - 1)
                    copy(mxT[s][:, :], TR_BANK[:, 0:P]).then_inc(mT_ready, 1)

                def bend(it, s):
                    i = 2 * it + s
                    act.wait_ge(m1_psum, r.at + i + 1)
                    if r.gated:
                        if not isinstance(it, int) or it > 0:
                            act.wait_ge(h_ready, r.at + i - 1)
                        src = h_bank[s][0][:, 0:w] if r is MLP1 else h_bank[s][0][:, w:2 * w]
                        a(gate[s][:, 0:w], src, ACT.Silu).then_inc(g_ready, 1)
                    else:
                        if not isinstance(it, int) or it > 0:
                            act.wait_ge(hT_psum, r.at + i - 1)
                        a(hid[s][:, 0:w], h_bank[s][0][:, 0:w], ACT.Silu).then_inc(h_ready, 1)
                act.preload_act_table(ACT.Silu)

                def steps(it):
                    for s in range(2):
                        i = 2 * it + s
                        bend(it, s)
                        if not isinstance(i, int) or i + 1 < r.tiles:
                            turned(*((it, 1) if s == 0 else (it + 1, 0)))
                turned(0, 0)
                steps(0)
                with act.Fori(1, r.tiles // 2 - 1) as it:
                    steps(it)
                steps(r.tiles // 2 - 1)

            def narrow_kv(L):
                if L.q0:
                    act.wait_ge(vbd_ready, L.q0)
                for b0, b1 in T_CHUNKS:
                    b = st.take()
                    st.empty(copy(kT_all[:, b0 * NK:b1 * NK], b[:, 0:(b1 - b0) * NK]))
                for q in range(4):
                    b = st.take()
                    st.empty(copy(v_narrow[:, q * 512:(q + 1) * 512], b[0:NK, :]))

            for q in range(4):
                b = st.take()
                st.empty(copy(CT[0:C, 4 * q * NK:(4 * q + 4) * NK], b[0:C, 0:4 * NK]))
            b = st.take()
            st.empty(copy(b1c[:, :], b[:, 0:32]))
            b = st.take()
            st.empty(copy(wr[1][:, :], b[:, 0:E]))
            prepare_m(0)
            make_t()
            if last_layer >= 3:
                prepare_m(1)
            b = st.take()
            st.empty(copy(nwq[0][:, :], b[:, 0:P]))
            b = st.take()
            st.empty(copy(nwo[0][:, :], b[:, 0:P]))
            for half in range(2):
                b = st.take()
                v = b[0:C, 0:P].rearrange("c (h e) -> c h e", e=16)
                copy(nwk[0][0:C, half * 64:half * 64 + 64].rearrange("c (h e) -> c h e", e=8), v[:, :, 0:8])
                st.empty(copy(nwv[0][0:C, half * 64:half * 64 + 64].rearrange("c (h e) -> c h e", e=8), v[:, :, 8:16]))
            act_attention(ATT[0])
            if last_layer >= 2:
                act_route(RT[0])
                if last_layer >= 3:
                    make_t()
                for q in range(RT[0].tiles // 4):
                    b = st.take()
                    st.empty(copy(bufT[:, q * 512:(q + 1) * 512], b[:, :]))
                act.preload_act_table(ACT.Gelu)

                def bend0(it, s):
                    e = 2 * it + s
                    for f in range(4):
                        act.wait_ge(h0_psum, 4 * e + f + 1)
                        if f == 0 and (not isinstance(e, int) or e >= 2):
                            act.wait_ge(o0_psum, e - 1)
                        a(hT0[s][:, f, :], bank[f][:, 0:CAP], ACT.Gelu, bias=b1c[:, ds(4 * e + f, 1)]).then_inc(h0_ready, 1)
                bend0(0, 0)
                bend0(0, 1)
                with act.Fori(1, E // 2) as it:
                    bend0(it, 0)
                    bend0(it, 1)
            if last_layer >= 3:
                act_attention(ATT[1])
            if last_layer >= 4:
                for k in range(2):
                    b = st.take()
                    st.empty(copy(wgu1[:, k * 384:(k + 1) * 384], b[:, 0:384]))
                b = st.take()
                st.empty(copy(wd1, b[:, 0:384].rearrange("p (j d) -> p j d", j=3)))
                act_mlp(MLP1)
            if last_layer >= 5:
                narrow_kv(ATT[2])
                act_attention(ATT[2])
            if last_layer >= 6:
                act_route(RT[1])
                for n in range(18):
                    b = st.take()
                    dst = (w2_2 if n % 2 else w1_2)[:, (n // 2) * 512:(n // 2 + 1) * 512]
                    st.empty(copy(dst, b[:, :]))
                act_mlp(SH2)
                act_mlp(RO2)
            if last_layer >= 7:
                narrow_kv(ATT[3])
                act_attention(ATT[3])
            if last_layer >= 8:
                act_route(RT[2])
                act_mlp(SH3)
                act_mlp(RO3)

        @block.vector
        def _(dve):
            v = nc.vector
            c = Chain(dve, dve_step)
            tt, ts, stt = v.tensor_tensor, v.tensor_scalar, v.scalar_tensor_tensor

            def flat(t):
                return t[:, :, :].rearrange("p a b -> p (a b)")

            LN_STEPS = 14

            def norm_stats(it, ready):
                ready(2 * it + 1)
                for s in range(2):
                    xb = X[:, ds((2 * it + s) * D, D)]
                    ins = v.bn_stats(ln_stats[:, s, :], xb)
                    if s == 0:
                        ins.then_inc(dve_step, 1)
                        c.n += 1
                    else:
                        c.link(ins)
                v.tensor_copy(ln_t[:, 0:1], ln_stats[:, 0, 0:1])
                for s in range(2):
                    ins = v.bn_aggr(ln_mv[:, s, :], ln_stats[:, s, :])
                    if s == 0:
                        ins.then_inc(dve_step, 1)
                        c.n += 1
                    else:
                        c.link(ins)

            def norm_guess():
                c.link(ts(ln_ve[:, :], ln_mv[:, :, 1], EPS, None, ALU.add))
                c.link(ts(ln_r[:, :].bitcast(I32), ln_ve[:, :].bitcast(I32), -0.5, RSQRT_MAGIC, ALU.mult, ALU.add))

            def norm_newton():
                c.link(stt(ln_t[:, :], ln_r[:, :], -0.5, ln_r[:, :], ALU.mult, ALU.mult))
                c.link(tt(ln_t[:, :], ln_t[:, :], ln_ve[:, :], ALU.mult))
                c.link(stt(ln_r[:, :], ln_t[:, :], 1.5, ln_r[:, :], ALU.add, ALU.mult))

            def norm_apply(it, free, to):
                free()
                for s in range(2):
                    xb = X[:, ds((2 * it + s) * D, D)]
                    for dst, done in to(it, s):
                        ins = ts(dst, xb, ln_mv[:, s, 0:1], ln_r[:, s:s + 1], ALU.subtract, ALU.mult)
                        ins.then_inc(done, 1)

            def norm_pair(it, ready, free, to):
                norm_stats(it, ready)
                norm_guess()
                for _ in range(3):
                    norm_newton()
                norm_apply(it, free, to)
            LN_LINKS = 2 + 2 + 2 + 9

            def dve_attention(L):
                wide = L.wide
                sl = L.unit0

                def norm(it, part=None):
                    def ready(n):
                        if L.n > 0:
                            dve.wait_ge(*x_ready(2 * L.n - 1, n + 1))

                    def free():
                        if not isinstance(it, int) or it > 0:
                            dve.wait_ge(xnT_psum, L.batch0 + 2 * it)
                    if part in (None, 0):
                        norm_stats(it, ready)
                        norm_guess()
                    if part in (None, 1):
                        norm_newton()
                    if part in (None, 2):
                        norm_newton()
                    if part in (None, 3):
                        norm_newton()
                        norm_apply(it, free, lambda it, s: [(xn[s][:, :], xn_ready)])

                def add_y(b):
                    dve.wait_ge(y_psum, L.batch0 + b + 1)
                    if L.bias is not None:
                        dve.wait_ge(bias_added, L.b0 + b + 1)
                    xb = X[:, ds(b * D, D)]
                    tt(xb, xb, Y_BANK[:, 0:D], ALU.add).then_inc(L.x_out, 1)

                per = 0

                def steps(it):
                    for k in range(2 * NU):
                        U = 2 * NU * it + k
                        u = k % NU
                        if u == 0:
                            b = 2 * it + k // NU - 2
                            if not isinstance(b, int) or 0 <= b < NB:
                                add_y(b)
                        if not isinstance(U, int) or U < UNITS:
                            b = 2 * it + k // NU
                            dve.wait_ge(s_psum, sl + U + 1)
                            src = S_BANK[u % 2][:, 0:UW].rearrange("p (h k) -> p h k", h=UH)
                            if L.mask:
                                sm = SM[u % 2].rearrange("p (h k) -> p h k", h=UH)
                                c.link(tt(sm, src, spread(notmask[:, ds(b * NK, NK)].rearrange("p (o k) -> p o k", o=1), 1, UH), ALU.add))
                                src = sm
                            c.link(v.tensor_reduce(mx[u % 2][:, :], src, AX.X, ALU.max))
                            tt(Z[u % 2].rearrange("p (h k) -> p h k", h=UH), src,
                               spread(mx[u % 2][:, :].rearrange("p (h o) -> p h o", o=1), 2, NK), ALU.subtract).then_inc(z_ready, 1)
                        V = U - 2
                        if not wide and (k - 2) % 2 == 1 and (not isinstance(V, int) or 0 <= V < UNITS):
                            half = (k - 2) % NU // 2
                            rows_o, rows_d_ = (slice(0, 64), slice(64, P))[::1 - 2 * half]
                            ob = ON_BANK[half]
                            dve.wait_ge(o_psum, sl + V + 1)
                            c.link(v.reciprocal(rden[rows_o, :], ob[rows_d_, 0:P]))
                            tt(OTn[(k - 2) // NU % 2][rows_o, :], ob[rows_o, 0:P], rden[rows_o, :], ALU.mult).then_inc(on_ready, 1)
                        elif wide and (not isinstance(V, int) or 0 <= V < UNITS):
                            uu = (k - 2) % NU
                            dve.wait_ge(o_psum, sl + V + 1)
                            e = OB
                            o = O_BANK[:, 0:UH * e].rearrange("p (h e) -> p h e", h=UH)
                            c.link(v.reciprocal(rsum[uu % 2][:, :], o[:, :, e - 1]))
                            dst = ON[uu % 2].rearrange("p (h e) -> p h e", h=UH)
                            tt(dst, o[:, :, 0:e - 1], spread(rsum[uu % 2][:, :].rearrange("p (h o) -> p h o", o=1), 2, e - 1),
                               ALU.mult).then_inc(on_ready, 1)
                        if k < 4:
                            if not isinstance(it, int) or it + 1 < NB // 2:
                                norm(it + 1, k)

                links = 2 * NU * (1 + (1 if L.mask else 0)) + 2 * (NU if wide else 2) + LN_LINKS
                norm(0)
                steps(0)
                c.enter(0, links)
                with dve.Fori(1, NB // 2 - 1) as it:
                    c.resume(it - 1)
                    steps(it)
                c.leave(NB // 2 - 2)
                steps(NB // 2 - 1)
                steps(NB // 2)

            def route(R):
                n = R.n
                nr = n * NB

                def ready(k):
                    dve.wait_ge(*x_ready(R.x_in, k + 1))

                def norm(it):
                    def free():
                        if not isinstance(it, int) or it > 0:
                            dve.wait_ge(rnT_psum, nr + 2 * it)
                    norm_pair(it, ready, free, lambda it, s: [(XN[:, ds((2 * it + s) * D, D)], xn_kept), (xn[s][:, :], rn_ready)])
                norm(0)
                c.enter(0, LN_LINKS)
                with dve.Fori(1, NB // 2) as it:
                    c.resume(it - 1)
                    norm(it)
                c.leave(NB // 2 - 1)
                dve.wait_ge(const_done, 1)
                dve.wait_ge(logits_psum, nr + NB)
                score, work, pick1, pick2, both, pos, tot, cum, cum2 = (rt[k] for k in "score work pick1 pick2 both pos tot cum cum2".split())
                X_ = R.experts

                def rows(t):
                    return spread(t[:, :].rearrange("p (t o) -> p t o", o=1), 2, E)

                def per_expert(t):
                    return spread(t[:, :].rearrange("p (o e) -> p o e", o=1), 1, NB)
                lg = bank[0][:, 0:NB * E].rearrange("p (t e) -> p t e", e=E)
                if n == 0:
                    c.link(tt(score[:, :, :], lg, per_expert(br_rows), ALU.add))
                else:
                    c.link(v.tensor_copy(score[:, :, :], lg))
                if X_ < E:
                    c.link(v.memset(score[:, :, X_:E], BELOW_ALL))
                if n != 1:
                    c.link(v.tensor_reduce(rc["best1"][:, :], score[:, :, :], AX.X, ALU.max))
                    tt(work[:, :, :], score[:, :, :], rows(rc["best1"]), ALU.subtract).then_inc(exps_in, 1)
                    dve.wait_ge(exps_out, n + 1)
                    c.link(v.tensor_reduce(rc["sum"][:, :], score[:, :, :], AX.X, ALU.add))
                    c.link(v.reciprocal(rc["inv"][:, :], rc["sum"][:, :]))
                    c.link(tt(score[:, :, :], score[:, :, :], rows(rc["inv"]), ALU.mult))
                    if X_ < E:
                        c.link(v.memset(score[:, :, X_:E], -1.0))

                def pick(src, best, first, out_):
                    c.link(v.tensor_reduce(best[:, :], src[:, :, :], AX.X, ALU.max))
                    c.link(tt(work[:, :, :], src[:, :, :], rows(best), ALU.is_equal))
                    c.link(tt(work[:, :, :], work[:, :, :], desc8[:, :, :], ALU.mult))
                    c.link(v.tensor_reduce(first[:, :], work[:, :, :], AX.X, ALU.max))
                    c.link(tt(out_[:, :, :], desc8[:, :, :], rows(first), ALU.is_equal))
                pick(score, rc["best1"], rc["first1"], pick1)
                if R.k == 2:
                    c.link(stt(cum[:, :, :], pick1[:, :, :], BELOW_ALL, score[:, :, :], ALU.mult, ALU.add))
                    pick(cum, rc["best2"], rc["first2"], pick2)
                    tt(both[:, :, :], pick1[:, :, :], pick2[:, :, :], ALU.add).then_inc(picked, 1)
                else:
                    v.tensor_copy(both[:, :, :], pick1[:, :, :]).then_inc(picked, 1)
                if n == 1:
                    tt(rc["diff"][:, :], rc["best2"][:, :], rc["best1"][:, :], ALU.subtract).then_inc(exps_in, 1)
                    dve.wait_ge(exps_out, n + 1)
                    c.link(ts(rc["sum"][:, :], rc["gate2"][:, :], 1.0, None, ALU.add))
                    c.link(v.reciprocal(rc["gate1"][:, :], rc["sum"][:, :]))
                    c.link(tt(rc["gate2"][:, :], rc["gate2"][:, :], rc["gate1"][:, :], ALU.mult))
                dve.wait_ge(ranked, n + 1)
                c.link(v.tensor_copy(tot[:, :, :], bank[5][:, 0:NB * E].rearrange("p (t e) -> p t e", e=E)))
                src, dst = tot, cum
                for sh in (1, 2, 4, 8):
                    c.link(v.tensor_copy(dst[:, 0:sh, :], src[:, 0:sh, :]))
                    c.link(tt(dst[:, sh:NB, :], src[:, sh:NB, :], src[:, 0:NB - sh, :], ALU.add))
                    src, dst = dst, (cum2 if dst is cum else cum)
                total = src
                c.link(tt(pos[:, :, :], bank[4][:, 0:NB * E].rearrange("p (t e) -> p t e", e=E), total[:, :, :], ALU.add))
                c.link(tt(pos[:, :, :], pos[:, :, :], tot[:, :, :], ALU.subtract))
                if n > 0:
                    ecm = ecmp[:, :].rearrange("p (e j) -> p e j", e=E)
                    c.link(tt(ecm, spread(total[:, NB - 1, :].rearrange("p (e o) -> p e o", o=1), 2, NB), steps128[:, :, :], ALU.is_gt))
                    c.link(v.tensor_reduce(ec["tiles"][:, :], ecm, AX.X, ALU.add))
                    s_, d_ = ec["tiles"], ec["end"]
                    for sh in (1, 2, 4):
                        c.link(v.tensor_copy(d_[:, 0:sh], s_[:, 0:sh]))
                        c.link(tt(d_[:, sh:E], s_[:, sh:E], s_[:, 0:E - sh], ALU.add))
                        s_, d_ = d_, (ec["end2"] if d_ is ec["end"] else ec["end"])
                    end = s_
                    c.link(tt(ec["start"][:, :], end[:, :], ec["tiles"][:, :], ALU.subtract))
                    c.link(ts(ec["start"][:, :], ec["start"][:, :], float(P), None, ALU.mult))
                    c.link(tt(pos[:, :, :], pos[:, :, :], per_expert(ec["start"]), ALU.add))
                    tc_ = tcmp[:, 0:TILES2 * E].rearrange("p (t e) -> p t e", e=E)
                    c.link(tt(tc_, tileno[:, :, :], spread(end[:, :].rearrange("p (o e) -> p o e", o=1), 1, TILES2), ALU.is_ge))
                    c.link(v.tensor_reduce(texp[:, :], tc_, AX.X, ALU.add))
                    c.link(ts(texp[:, :], texp[:, :], float(X_ - 1), None, ALU.min))
                    c.link(v.tensor_copy(texp_i[:, :], texp[:, :]))
                for k, (pk, first, best) in enumerate(((pick1, "first1", "best1"), (pick2, "first2", "best2"))[:R.k]):
                    place, keep = rc[f"place{k + 1}"], rc[f"keep{k + 1}"]
                    c.link(tt(work[:, :, :], pk[:, :, :], pos[:, :, :], ALU.mult))
                    c.link(v.tensor_reduce(place[:, :], work[:, :, :], AX.X, ALU.add))
                    if n == 0:
                        c.link(ts(keep[:, :], place[:, :], float(CAP), None, ALU.is_lt))
                        c.link(ts(place[:, :], place[:, :], float(CAP - 1), None, ALU.min))
                        c.link(stt(place[:, :], rc[first][:, :], -float(CAP), place[:, :], ALU.mult, ALU.add))
                        c.link(ts(place[:, :], place[:, :], float(E * CAP), None, ALU.add))
                        c.link(v.tensor_copy(from_row[k][:, :], place[:, :]))
                        c.link(tt(place[:, :], place[:, :], trash[:, k, :], ALU.subtract))
                        c.link(tt(place[:, :], place[:, :], keep[:, :], ALU.mult))
                        c.link(tt(place[:, :], place[:, :], trash[:, k, :], ALU.add))
                        c.link(v.tensor_copy(to_row[k][:, :], place[:, :]))
                        c.link(tt(rc[f"gate{k + 1}"][:, :], rc[best][:, :], keep[:, :], ALU.mult))
                    else:
                        c.link(v.tensor_copy(from_row[k][:, :], place[:, :]))
                        c.link(v.tensor_copy(to_row[k][:, :], place[:, :]))
                if n == 0:
                    c.link(tt(rc["sum"][:, :], rc["gate1"][:, :], rc["gate2"][:, :], ALU.add))
                    c.link(ts(rc["sum"][:, :], rc["sum"][:, :], 1e-6, None, ALU.max))
                    c.link(v.reciprocal(rc["inv"][:, :], rc["sum"][:, :]))
                    for g_ in ("gate1", "gate2"):
                        c.link(tt(rc[g_][:, :], rc[g_][:, :], rc["inv"][:, :], ALU.mult))
                v.tensor_copy(texp[:, 0:1], place[:, 0:1]).then_inc(routed, 1)

            counts = [0, 0, 0, 0]

            def combine(R):
                i = 0
                for t in range(NB):
                    for k in range(R.k):
                        s = i % 4
                        counts[s] += 16
                        dve.wait_ge(gathered[s], counts[s])
                        xb = X[:, t * D:(t + 1) * D]
                        if R.k == 1:
                            ins = tt(xb, got[s][:, :], xb, ALU.add)
                        else:
                            ins = stt(xb, got[s][:, :], rc[f"gate{k + 1}"][:, t:t + 1], xb, ALU.mult, ALU.add)
                        ins.then_inc(combined, 1)
                        i += 1
                        dve.wait_ge(combined, COMBINE0[R.n] + i)

            def dve_mlp(r):
                w, nj = r.width, r.width // P
                h_bank = [[bank[0], bank[1]], [bank[2], bank[3]]]
                t_bank = [bank[4], bank[5]]

                def norm(it):
                    def ready(n):
                        dve.wait_ge(*x_ready(2, n + 1))

                    def free():
                        if not isinstance(it, int) or it > 0:
                            dve.wait_ge(mT_psum, r.at + 2 * it)
                    norm_pair(it, ready, free, lambda it, s: [(xn[s][:, :], m_in)])

                def multiply(it, s):
                    i = 2 * it + s
                    dve.wait_ge(g_ready, r.gates0 + i + 1)
                    if not isinstance(it, int) or it > 0:
                        dve.wait_ge(hT_psum, r.at + i - 1)
                    up = h_bank[s][1][:, 0:w] if r is MLP1 else h_bank[s][0][:, 0:w]
                    tt(hid[s][:, 0:w], up, gate[s][:, 0:w], ALU.mult).then_inc(h_ready, 1)

                def turned(it, s):
                    i = 2 * it + s
                    dve.wait_ge(hT_psum, r.at + i + 1)
                    if not isinstance(it, int) or it > 0:
                        dve.wait_ge(m2_psum, r.at + i - 1)
                    v.tensor_copy(hidT[s][:, 0:nj, :], t_bank[s][:, 0:w].rearrange("p (j t) -> p j t", j=nj)).then_inc(hT_ready, 1)

                def finish(it, s):
                    i = 2 * it + s
                    dve.wait_ge(m2_psum, r.at + i + 1)
                    if r.src == "rows":
                        if not isinstance(it, int) or it > 0:
                            dve.wait_ge(stored[s], r.stored0 + 16 * it)
                        v.tensor_copy(row_out[s][:, :], Y_BANK[:, 0:D]).then_inc(m2_done, 1)
                    else:
                        xb = X[:, ds(i * D, D)]
                        tt(xb, xb, Y_BANK[:, 0:D], ALU.add).then_inc(m2_done, 1)

                def steps(it):
                    for s in range(2):
                        i = 2 * it + s
                        if not isinstance(i, int) or 1 <= i <= r.tiles:
                            turned(*((it - 1, 1) if s == 0 else (it, 0)))
                        if r.gated and (not isinstance(i, int) or i < r.tiles):
                            multiply(it, s)
                        if not isinstance(i, int) or 2 <= i <= r.tiles + 1:
                            finish(it - 1, s)
                        if r is MLP1 and s == 0 and (not isinstance(it, int) or it + 1 < r.tiles // 2):
                            norm(it + 1)
                if r is MLP1:
                    norm(0)
                steps(0)
                c.enter(0, LN_LINKS if r is MLP1 else 0)
                last = r.tiles // 2 - (1 if r is MLP1 else 0)
                with dve.Fori(1, last) as it:
                    c.resume(it - 1)
                    steps(it)
                c.leave(last - 1)
                for it in range(last, r.tiles // 2 + 1):
                    steps(it)

            for s in range(2):
                v.memset(vw[s][:, :, 64:65], 1.0).then_inc(dve_prepared if s else dve_step, 1)
            c.n += 1
            dve.wait_ge(loaded["rowsof"], 16 * 5)
            dve.wait_ge(loaded["x"], 16)
            dve_attention(ATT[0])
            if last_layer >= 2:
                route(RT[0])

                def finish0(it, s):
                    e = 2 * it + s
                    dve.wait_ge(o0_psum, e + 1)
                    if not isinstance(it, int) or it > 0:
                        dve.wait_ge(stored[s], 32 * it)
                    b2 = b2_rows[:, ds(e * D, D)].rearrange("p (o d) -> p o d", o=1)
                    c.link(tt(o0[s][:, 0:2, :], bank[4 + s][:, 0:256].rearrange("p (r d) -> p r d", r=2), spread(b2, 1, 2), ALU.add))
                    n = CAP - 2 * P
                    tt(o0[s][0:n, 2, :], bank[4 + s][0:n, 256:384], b2_rows[0:n, ds(e * D, D)], ALU.add).then_inc(o0_ready, 1)
                dve.wait_ge(loaded["b2"], 16)
                finish0(0, 0)
                finish0(0, 1)
                c.enter(0, 2)
                with dve.Fori(1, E // 2) as it:
                    c.resume(it - 1)
                    finish0(it, 0)
                    finish0(it, 1)
                c.leave(E // 2 - 1)
                combine(RT[0])
            if last_layer >= 3:
                dve_attention(ATT[1])
            if last_layer >= 4:
                dve.wait_ge(loaded["mlp1"], 48)
                c.link(v.tensor_copy(w1n, w1n.bitcast(I32)))
                ts(w1n, w1n, 1.0 / 127.0, None, ALU.mult).then_inc(dve_prepared, 1)
                dve_mlp(MLP1)
            if last_layer >= 5:
                c.link(ts(notmask, mask8[:, :], -1.0, FLT_MAX, ALU.add, ALU.mult))
                dve_attention(ATT[2])
            if last_layer >= 6:
                route(RT[1])
                dve_mlp(SH2)
                dve_mlp(RO2)
                combine(RT[1])
            if last_layer >= 7:
                dve_attention(ATT[3])
            if last_layer >= 8:
                route(RT[2])
                dve_mlp(SH3)
                dve_mlp(RO3)
                combine(RT[2])


_INS = ['x', 'ctx_768', 'mask_BxS2_bf1', 'L0_xattn_Wq', 'L0_xattn_Wkv', 'L0_xattn_Wproj', 'L0_xattn_bproj',
        'L0_ffn_w_router', 'L0_ffn_b_router', 'L0_ffn_w1', 'L0_ffn_b1', 'L0_ffn_w2', 'L0_ffn_b2',
        'L1_xattn_Wq', 'L1_xattn_Wk', 'L1_xattn_Wv', 'L1_xattn_Wo', 'L1_xattn_bo',
        'L1_ffn_w_gate', 'L1_ffn_w_up', 'L1_ffn_w_down',
        'L2_xattn_Wq', 'L2_xattn_bq', 'L2_xattn_Wkv', 'L2_xattn_bkv', 'L2_xattn_Wo', 'L2_xattn_bo',
        'L2_ffn_shared_w1', 'L2_ffn_shared_w2', 'L2_ffn_experts_w1', 'L2_ffn_experts_w2', 'L2_ffn_gate_w',
        'L3_xattn_Wq', 'L3_xattn_Wk', 'L3_xattn_Wv', 'L3_xattn_Wo', 'L3_ffn_Wg_DN', 'L3_ffn_Wl1_ND2H', 'L3_ffn_Wl2_NHD']


def kernel(**inputs):
    import numpy as _np
    import concourse.bacc as _bacc
    from concourse import mybir as _mybir
    from concourse.bass_utils import run_bass_kernel_spmd as _run

    nc = _bacc.Bacc("TRN2", target_bir_lowering=False, num_devices=1)
    arrays, args = {}, {}
    for name in _INS:
        a = _np.ascontiguousarray(inputs[name])
        if a.dtype == bool:
            a = a.view(_np.uint8)
        arrays[f"in_{name}_dram"] = a
        args[name] = nc.dram_tensor(f"in_{name}_dram", a.shape, _mybir.dt.from_np(a.dtype), kind="ExternalInput").ap()
    out = nc.dram_tensor("out_0_dram", (NB, P, D), F32, kind="ExternalOutput").ap()
    build(nc, args, out, LAST)
    r = _run(nc, [arrays], core_ids=[0])
    return r.results[0]["out_0_dram"]
```

```python
import concourse.bass as bass
from concourse import mybir
from contextlib import ExitStack

F32 = mybir.dt.float32
I32 = mybir.dt.int32
U32 = mybir.dt.uint32
U8 = mybir.dt.uint8
ACT = mybir.ActivationFunctionType
ALU = mybir.AluOpType
AX = mybir.AxisListType
ds = bass.ds

P = 128
NB = 16
D = 128
NK = 77
C = 96
H = 16
UH = 4
NU = H // UH
UNITS = NB * NU
UW = UH * NK
KW = H * NK
E = 8
NT = NB * P
EPS = 1e-5
RSQRT_MAGIC = 1597463007.0
FLT_MAX = 3.4028234663852886e38
BELOW_ALL = -3.0e38
LAST = 8

CAP = int(1.25 * NT / E)
CAP_ROWS = E * CAP
TILES2 = (2 * NT + E * (P - 1)) // P
TILES2 += TILES2 % 2
TILES3 = (NT + (E - 1) * (P - 1)) // P
TILES3 += TILES3 % 2
F0 = 512
F1 = 384
F2 = 512
F3 = 256
T_CHUNKS = ((0, 6), (6, 11), (11, 16))
OB = 65


def spread(ap, dim, n):
    shape = list(ap.shape)
    assert shape[dim] == 1
    shape[dim] = n
    return ap.broadcast_to(shape)


class Attention:
    def __init__(self, n, wide, scale, bias, mask, wide_n=None, nar_n=None):
        self.n, self.unit0, self.batch0 = n, n * UNITS, n * NB
        self.wide, self.scale, self.bias, self.mask = wide, scale, bias, mask
        self.wide_n, self.nar_n = wide_n, nar_n
        self.x_out = None
        self.oT0 = self.v0 = self.q0 = self.c0 = self.b0 = 0


class Routing:
    def __init__(self, n, layer, k, experts, rows, outs, total, x_in):
        self.n, self.layer, self.k, self.experts = n, layer, k, experts
        self.rows, self.outs, self.total, self.x_in = rows, outs, total, x_in
        self.tiles = total // P
        self.scatter0 = 0


class MlpRun:
    def __init__(self, tiles, width, gated, w1, w2, R):
        self.tiles, self.width, self.gated = tiles, width, gated
        self.w1, self.w2, self.R = w1, w2, R
        self.at = self.gates0 = self.rows0 = self.stored0 = 0


class SharedMlp:
    def __init__(self, nf, w1, gate, w2):
        self.nf, self.w1, self.gate, self.w2 = nf, w1, gate, w2
        self.products0 = self.gates0 = self.parts0 = self.groups0 = 0


class Chain:

    def __init__(self, eng, sem):
        self.eng, self.sem, self.base, self.n = eng, sem, 0, 0

    def link(self, ins):
        ins.then_inc(self.sem, 1)
        self.n += 1
        self.eng.wait_ge(self.sem, self.base + self.n)

    def enter(self, it, steps):
        self.before, self.steps = self.base + self.n, steps
        self.resume(it)

    def resume(self, it):
        self.base, self.n = self.before + it * self.steps, 0

    def leave(self, count):
        assert self.n == self.steps, (self.n, self.steps)
        self.base, self.n = self.before + count * self.steps, 0


class Turns:

    def __init__(self, eng, filled, emptied, banks):
        self.eng, self.filled, self.emptied, self.banks, self.n = eng, filled, emptied, banks, 0

    def bank(self):
        return self.banks[self.n % len(self.banks)]

    def claim(self):
        if self.n >= len(self.banks):
            self.eng.wait_ge(self.emptied, self.n - len(self.banks) + 1)
        return self.bank()

    def fill(self, ins):
        ins.then_inc(self.filled, 1)
        self.n += 1

    def take(self):
        self.eng.wait_ge(self.filled, self.n + 1)
        return self.bank()

    def empty(self, ins):
        ins.then_inc(self.emptied, 1)
        self.n += 1

    def settle(self):
        self.eng.wait_ge(self.emptied, self.n)


def build(nc, A, out, last_layer=8):
    ctx = ExitStack()
    with ctx:
        def sb(name, shape, dt=F32):
            return ctx.enter_context(nc.sbuf_tensor(name, shape, dt))

        def sem(name):
            return ctx.enter_context(nc.semaphore(name))

        bank = [ctx.enter_context(nc.psum_tensor(f"bank{i}", [P, 512], F32)) for i in range(8)]
        S_BANK, PT_BANK = bank[0:2], bank[2:4]
        O_BANK, V_BANK, TR_BANK, Y_BANK = bank[4], bank[5], bank[6], bank[7]
        ON_BANK = bank[4:6]

        ident = sb("ident", [P, P])
        earlier = sb("earlier", [P, P])
        ones = sb("ones", [P, P])
        headmask = sb("headmask", [P, H])
        desc8 = sb("desc8", [P, NB, E])
        tileno = sb("tileno", [P, TILES2, E])
        steps128 = sb("steps128", [P, E, NB])
        trash = sb("trash", [P, 2, NB])
        X = sb("X", [P, NT])
        XN = sb("XN", [P, NT])
        CT = sb("CT", [C + 1, KW])
        R1 = sb("R1", [P, NB * KW])
        RP = sb("RP", [P, 3840])
        RV = sb("RV", [P, 2 * H * OB])
        RM = sb("RM", [P, H * D])
        RA = sb("RA", [P, 3296])
        RH = sb("RH", [P, 3072])
        RW = sb("RW", [P, 2304])
        wv = sb("wv", [C, H * 64])
        wo = sb("wo", [P, 8, D])
        nwq = [sb(f"nwq{i}", [P, D]) for i in range(2)]
        nwk = [sb(f"nwk{i}", [C + 1, D]) for i in range(2)]
        nwv = [sb(f"nwv{i}", [C + 1, D]) for i in range(2)]
        nwo = [sb(f"nwo{i}", [P, D]) for i in range(2)]
        bq2 = sb("bq2", [P, 1])
        bo_rows = [sb(f"bo_rows{i}", [P, D]) for i in range(3)]
        wr = [sb(f"wr{i}", [P, E]) for i in range(3)]
        br_rows = sb("br_rows", [P, E])
        b1c = sb("b1c", [P, E * 4])
        mask8 = sb("mask8", [P, KW], U8)
        qT = [sb(f"qT{i}", [P, P]) for i in range(2)]
        mxT = [sb(f"mxT{i}", [P, P]) for i in range(2)]
        ln_stats = sb("ln_stats", [P, 2, 6])
        ln_mv = sb("ln_mv", [P, 2, 2])
        ln_ve = sb("ln_ve", [P, 2])
        ln_r = sb("ln_r", [P, 2])
        ln_t = sb("ln_t", [P, 2])
        all_stats = sb("all_stats", [P, NB, 6])
        carry = sb("carry", [P, 1])
        all_mv = sb("all_mv", [P, NB, 2])
        all_ve, all_r, all_t = sb("all_ve", [P, NB]), sb("all_r", [P, NB]), sb("all_t", [P, NB])
        xn = [sb(f"xn{i}", [P, D]) for i in range(2)]
        xnT = [sb(f"xnT{i}", [P, P]) for i in range(2)]
        cts = [sb(f"cts{i}", [C, NK]) for i in range(2)]
        mx = [sb(f"mx{i}", [P, UH]) for i in range(2)]
        rsum = [sb(f"rsum{i}", [P, UH]) for i in range(2)]
        rt = {n: sb(f"rt_{n}", [P, NB, E]) for n in
              "score work pick1 pick2 both pos tot cum cum2".split()}
        rc = {n: sb(f"rc_{n}", [P, NB]) for n in
              "best1 best2 first1 first2 place1 place2 keep1 keep2 gate1 gate2 sum inv diff".split()}
        to_row = [sb(f"to_row{k}", [P, NB], U32) for k in range(2)]
        from_row = [sb(f"from_row{k}", [P, NB], U32) for k in range(2)]
        ec = {n: sb(f"ec_{n}", [P, E]) for n in "count tiles end end2 start".split()}
        ecmp = sb("ecmp", [P, E * NB])
        tcmp = sb("tcmp", [P, TILES2 * E])
        texp = sb("texp", [P, TILES2])
        texp_i = sb("texp_i", [P, TILES2], I32)
        got = [sb(f"got{i}", [P, D]) for i in range(4)]

        T_all = R1
        wq_nat = RP[:, 0:1024]
        wk_nat = RP[0:C, 1024:2048]
        wqT = RP[:, 2048:3072].rearrange("p (j d) -> p j d", j=8)
        wkT = RP[:, 3072:3840].rearrange("p (j c) -> p j c", j=8)
        bufT = RP[:, 0:CAP_ROWS]
        kbd = [RP[:, i * KW:(i + 1) * KW] for i in range(2)]
        vw = [RV[0:NK, i * H * OB:(i + 1) * H * OB].rearrange("k (h e) -> k h e", h=H) for i in range(2)]
        v_narrow = RV[0:NK, 0:NB * D]
        MT = RM[0:C, :].rearrange("c (h d) -> c h d", h=H)
        kT_all = RM[:, 0:KW]
        ctx_nat = R1[0:NK, 0:NB * C].rearrange("k (b c) -> k b c", b=NB)

        def ra(at, n):
            return RA[:, at:at + n]
        Z = [ra(i * UW, UW) for i in range(2)]
        PR = [ra(2 * UW + i * UW, UW) for i in range(2)]
        PT = [RA[0:NK, 4 * UW + i * 512:4 * UW + (i + 1) * 512].rearrange("k (h q) -> k h q", h=UH) for i in range(2)]
        ON = [ra(4 * UW + 1024 + i * 256, 256) for i in range(2)]
        OT = [ra(4 * UW + 1536 + i * 256, 256).rearrange("p (j q) -> p j q", j=2) for i in range(2)]
        OTn = [ra(4 * UW + 1024 + i * P, P) for i in range(2)]
        rden = ra(4 * UW + 1280, P)
        SM = [XN[:, i * UW:(i + 1) * UW] for i in range(2)]
        rows0 = RA[:, 0:CAP_ROWS].rearrange("p (t d) -> p t d", d=D)

        w1s = [RW[:, i * 512:(i + 1) * 512] for i in range(2)]
        w2s = [RW[:, 1024 + i * 512:1024 + (i + 1) * 512].rearrange("p (f d) -> p f d", f=4) for i in range(2)]
        hT0 = [RH[:, i * 1280:(i + 1) * 1280].rearrange("p (f t) -> p f t", f=4) for i in range(2)]
        o0 = [RA[:, i * 384:(i + 1) * 384].rearrange("p (r d) -> p r d", r=3) for i in range(2)]
        b2_rows = RA[:, 768:768 + E * D]
        w1n = RW[:, 0:1152]
        wg1, wu1 = RW[:, 1152:1152 + F1], RW[:, 1152 + F1:1152 + 2 * F1]
        wd1 = RW[:, 1920:2304].rearrange("p (j d) -> p j d", j=3)
        notmask = RW[:, 0:KW]
        hid = [RH[:, i * 512:(i + 1) * 512] for i in range(2)]
        gate = [RH[:, 1024 + i * 384:1024 + (i + 1) * 384] for i in range(2)]
        hidT = [RH[:, 1792 + i * 512:1792 + (i + 1) * 512].rearrange("p (j t) -> p j t", j=4) for i in range(2)]
        vbd = [R[0:NK, at:at + 16 * 136] for R, at in ((RH, 0), (R1, 34 * 512))]
        vbd_steps = [v_.rearrange("k (h x) -> k h x", x=136) for v_ in vbd]
        row_in = [sb(f"row_in{i}", [P, D]) for i in range(2)]
        row_out = [sb(f"row_out{i}", [P, D]) for i in range(2)]
        xnT_all = RA[:, 0:NT]
        shT = [R[:, 0:2048].rearrange("p (f t) -> p f t", f=4) for R in (RP, RH)]
        sh_gate = [RH[:, 2048 + i * 512:2048 + (i + 1) * 512] for i in range(2)]
        w1_2 = R1[:, 0:9 * 512]
        w2_2 = R1[:, 9 * 512:18 * 512]
        nat2 = [R1[:, (18 + i) * 512:(19 + i) * 512] for i in range(4)]
        w1_3 = R1[:, 22 * 512:30 * 512]
        w2_3 = R1[:, 30 * 512:34 * 512]

        rows_d = [nc.dram_tensor(f"rows{i}", [n + (2 * NT if i == 0 else 0), D], F32, kind="Internal")
                  for i, n in enumerate((CAP_ROWS, TILES2 * P, TILES3 * P))]
        outs_d = [nc.dram_tensor(f"outs{i}", [n, D], F32, kind="Internal")
                  for i, n in enumerate((CAP_ROWS, TILES2 * P, TILES3 * P))]
        zero_tile = sb("zero_tile", [P, D])

        const_step = sem("const_step")
        const_done = sem("const_done")
        loaded = {}

        def arrives(name):
            loaded[name] = sem("loaded_" + name)
            return loaded[name]
        for n in ("x ctx wqk0 wvo0 wqk1 wvo1 narrow2 narrow3 rowsof misc b2 mlp1 mlp3").split():
            arrives(n)
        zeroed, xn_kept = sem("zeroed"), sem("xn_kept")
        filled, emptied = sem("stage_filled"), sem("stage_emptied")
        dve_step = sem("dve_step")
        dve_prepared = sem("dve_prepared")
        xn_ready, xnT_psum, xnT_ready = sem("xn_ready"), sem("xnT_psum"), sem("xnT_ready")
        q_psum, q_ready = sem("q_psum"), sem("q_ready")
        cts_ready, kbd_ready, bias_added = sem("cts_ready"), sem("kbd_ready"), sem("bias_added")
        vbd_ready = sem("vbd_ready")
        v_psum, v_ready = sem("v_psum"), sem("v_ready")
        s_psum, z_ready, p_ready = sem("s_psum"), sem("z_ready"), sem("p_ready")
        pT_psum, pT_ready = sem("pT_psum"), sem("pT_ready")
        o_psum, on_ready = sem("o_psum"), sem("on_ready")
        oT_psum, oT_ready, y_psum = sem("oT_psum"), sem("oT_ready"), sem("y_psum")
        x_done = [sem(f"x_done{i}") for i in range(4)]
        stats_ready, vbd_blank = sem("stats_ready"), sem("vbd_blank")
        logits_psum = sem("logits_psum")
        exps_in, exps_out = sem("exps_in"), sem("exps_out")
        picked, ranked = sem("picked"), sem("ranked")
        routed = sem("routed")
        scattered = sem("scattered")
        rows_loaded = [sem(f"rows_loaded{i}") for i in range(2)]
        gathered = [sem(f"gathered{i}") for i in range(4)]
        combined = sem("combined")
        stored = [sem(f"stored{i}") for i in range(2)]
        w_loaded = [sem(f"w_loaded{i}") for i in range(2)]
        h0_psum, h0_ready, o0_psum, o0_ready = sem("h0_psum"), sem("h0_ready"), sem("o0_psum"), sem("o0_ready")
        sh_psum, sh_gated, sh_ready, so_psum, shared_done = (sem(n) for n in
                                                             "sh_psum sh_gated sh_ready so_psum shared_done".split())
        mT_psum, mT_ready = sem("mT_psum"), sem("mT_ready")
        m1_psum, g_ready, h_ready = sem("m1_psum"), sem("g_ready"), sem("h_ready")
        hT_psum, hT_ready, m2_psum, m2_done = sem("hT_psum"), sem("hT_ready"), sem("m2_psum"), sem("m2_done")
        nat_loaded = [sem(f"nat_loaded{i}") for i in range(4)]
        written = sem("written")

        def attention(n, **k):
            return Attention(n, **k)
        ATT = [attention(0, wide=True, scale=64 ** -0.5, bias=0, mask=False, wide_n=0),
               attention(1, wide=True, scale=64 ** -0.5, bias=1, mask=False, wide_n=1),
               attention(2, wide=False, scale=8 ** -0.5, bias=2, mask=False, nar_n=0),
               attention(3, wide=False, scale=8 ** -0.5, bias=None, mask=True, nar_n=1)]
        for L in ATT:
            L.x_out = x_done[L.n]
            L.oT0 = sum(UNITS if K.wide else 0 for K in ATT[:L.n])
            L.on0 = sum(UNITS if K.wide else 2 * NB for K in ATT[:L.n])
            L.v0 = sum(2 * NB if K.wide else 0 for K in ATT[:L.n])
            L.q0 = sum(0 if K.wide else NB for K in ATT[:L.n])
            L.c0 = sum(NB if K.wide else 0 for K in ATT[:L.n])
            L.b0 = sum(NB if K.bias is not None else 0 for K in ATT[:L.n])
        RT = [Routing(n=0, layer=0, k=2, experts=8, rows=rows_d[0], outs=outs_d[0], total=CAP_ROWS, x_in=0),
              Routing(n=1, layer=2, k=2, experts=8, rows=rows_d[1], outs=outs_d[1], total=TILES2 * P, x_in=4),
              Routing(n=2, layer=3, k=1, experts=7, rows=rows_d[2], outs=outs_d[2], total=TILES3 * P, x_in=6)]
        for R in RT:
            R.tiles = R.total // P
            R.scatter0 = sum(16 * NB * K.k for K in RT[:R.n])
        def parts(w, f0):
            return lambda f: w[:, f0 + f * P:f0 + (f + 1) * P]
        SH1 = SharedMlp(3, parts(wu1, 0), parts(wg1, 0), lambda f: wd1[:, f, :])
        SH2 = SharedMlp(4, parts(w1_2, 8 * 512), None, parts(w2_2, 8 * 512))
        SH3 = SharedMlp(2, parts(w1_3, 7 * 512), parts(w1_3, 7 * 512 + F3), parts(w2_3, 7 * F3))
        products = gates = parts_n = 0
        for n, S in enumerate((SH1, SH2, SH3)):
            S.products0, S.gates0, S.parts0, S.groups0 = products, gates, parts_n, 4 * n
            products += 4 * S.nf * (2 if S.gate else 1)
            gates += 4 * S.nf if S.gate else 0
            parts_n += 4 * S.nf
        RO2 = MlpRun(TILES2, F2, False, w1_2, w2_2, RT[1])
        RO3 = MlpRun(TILES3, F3, True, w1_3, w2_3, RT[2])
        RO3.at = TILES2
        RO2.rows0, RO2.stored0 = 1, 32 * (E // 2)
        RO3.rows0, RO3.stored0 = 1 + TILES2 // 2, 32 * (E // 2) + 16 * (TILES2 // 2)
        STORED_END = [RO2.stored0, RO3.stored0, RO3.stored0 + 16 * (TILES3 // 2)]
        COMBINE0 = [0, 2 * NB, 4 * NB]

        def x_ready(layer, n):
            if layer % 2 == 0:
                return x_done[layer // 2], n
            if layer == 3:
                return shared_done, n
            return combined, COMBINE0[layer // 3 if layer < 7 else 2] + n * (1 if layer == 7 else 2)

        STAGE_END, filled_n = {}, 0
        for name, n, layer in (("ct", 4, 1), ("small", 2, 1), ("m0", 8, 1), ("t0", 48, 1), ("m1", 8, 3), ("narrow2", 4, 1),
                               ("xn0", 4, 2), ("t1", 48, 3), ("rows", CAP_ROWS // 512, 2), ("xn1", 4, 4), ("mlp1", 3, 4),
                               ("kv2", 7, 5), ("xn2", 4, 6), ("nat2", 18, 6), ("kv3", 7, 7), ("xn3", 4, 8)):
            if last_layer >= layer:
                filled_n += n
            STAGE_END[name] = filled_n

        block = ctx.enter_context(nc.Block())

        def bcast(src, n):
            return bass.AP(src.tensor, src.offset, [[0, P], [1, n]])

        @block.sync
        def _(sp):
            def load(dst, src, name):
                sp.dma_start(dst, src).then_inc(loaded[name], 16)

            sp.dma_start(X[:, :].rearrange("p (b d) -> p b d", b=NB), A["x"].rearrange("b s d -> s b d")).then_inc(loaded["x"], 16)
            load(ctx_nat, A["ctx_768"].rearrange("b k c -> k b c"), "ctx")
            load(wq_nat, A["L0_xattn_Wq"], "wqk0")
            load(wk_nat, A["L0_xattn_Wkv"][:, 0:1024], "wqk0")
            load(wv[:, :], A["L0_xattn_Wkv"][:, 1024:2048], "wvo0")
            load(wo[:, :, :], A["L0_xattn_Wproj"].rearrange("(j p) d -> p j d", p=P), "wvo0")
            for i, name in enumerate(("L0_xattn_bproj", "L1_xattn_bo", "L2_xattn_bo")):
                load(bo_rows[i][:, :], bcast(A[name], D), "rowsof")
            load(br_rows[:, :], bcast(A["L0_ffn_b_router"], E), "rowsof")
            load(mask8[:, :], bcast(A["mask_BxS2_bf1"], KW), "rowsof")
            load(wr[0][:, :], A["L0_ffn_w_router"], "misc")
            load(wr[2][:, :], A["L3_ffn_Wg_DN"], "misc")
            load(row_in[0][0:32, :], A["L0_ffn_b1"].rearrange("e (f p) -> (e f) p", p=P), "misc")
            load(row_in[1][0:E, :], A["L2_ffn_gate_w"], "misc")
            sp.wait_ge(emptied, STAGE_END["m0"])
            load(wq_nat, A["L1_xattn_Wq"], "wqk1")
            load(wk_nat, A["L1_xattn_Wk"], "wqk1")
            load(got[0][:, :], A["L2_xattn_Wq"], "narrow2")
            load(got[1][:, :], A["L2_xattn_Wo"], "narrow2")
            load(got[2][:, 0:C], A["L2_xattn_Wkv"][0:P, :], "narrow2")
            load(got[3][:, 0:C], A["L2_xattn_Wkv"][P:2 * P, :], "narrow2")
            load(bq2[:, :], A["L2_xattn_bq"].rearrange("(p o) -> p o", o=1), "narrow2")
            bkv = A["L2_xattn_bkv"].rearrange("(o h t e) -> t o h e", o=1, t=2, e=8)
            load(nwk[0][C:C + 1, :].rearrange("o (h e) -> o h e", e=8), bkv[0], "narrow2")
            load(nwv[0][C:C + 1, :].rearrange("o (h e) -> o h e", e=8), bkv[1], "narrow2")
            load(nwq[1][:, :], A["L3_xattn_Wq"], "narrow3")
            load(nwk[1][0:C, :], A["L3_xattn_Wk"], "narrow3")
            load(nwv[1][0:C, :], A["L3_xattn_Wv"], "narrow3")
            load(nwo[1][:, :], A["L3_xattn_Wo"], "narrow3")

            if last_layer >= 2:
                if last_layer >= 3:
                    sp.wait_ge(x_done[0], NB)
                    load(wv[:, :], A["L1_xattn_Wv"], "wvo1")
                    load(wo[:, :, :], A["L1_xattn_Wo"].rearrange("(j p) d -> p j d", p=P), "wvo1")
                sp.wait_ge(zeroed, 16 * 3)
                sp.wait_ge(scattered, RT[0].scatter0 + 16 * NB * RT[0].k)
                half = RT[0].tiles // 2
                for i in range(2):
                    sp.dma_start(rows0[:, i * half:(i + 1) * half, :],
                                 rows_d[0][i * half * P:(i + 1) * half * P, :].rearrange("(t p) d -> p t d", p=P))\
                        .then_inc(rows_loaded[i], 16)

                sp.wait_ge(emptied, STAGE_END["rows"])
                load(b2_rows, bcast(A["L0_ffn_b2"], E * D), "b2")

                def load_expert(it, s):
                    e = 2 * it + s
                    if not isinstance(it, int) or it > 0:
                        sp.wait_ge(o0_psum, 2 * it + s - 1)
                    sp.dma_start(w1s[s], A["L0_ffn_w1"].rearrange("e p f -> p e f")[:, ds(e, 1), :]
                                 .rearrange("p o f -> p (o f)")).then_inc(w_loaded[s], 16)
                    sp.dma_start(w2s[s], A["L0_ffn_w2"].rearrange("e (f p) d -> p e f d", p=P)[:, ds(e, 1), :, :]
                                 .rearrange("p o f d -> p (o f) d")).then_inc(w_loaded[s], 16)
                load_expert(0, 0)
                load_expert(0, 1)
                with sp.Fori(1, E // 2) as it:
                    load_expert(it, 0)
                    load_expert(it, 1)
            if last_layer >= 4:
                sp.wait_ge(o0_psum, E)
                load(w1n.bitcast(I32)[:, 0:384].rearrange("p (j d) -> p j d", j=3), A["L1_ffn_w_gate"].rearrange("(j p) d -> p j d", p=P), "mlp1")
                load(w1n.bitcast(I32)[:, 384:768].rearrange("p (j d) -> p j d", j=3), A["L1_ffn_w_up"].rearrange("(j p) d -> p j d", p=P), "mlp1")
                load(w1n.bitcast(I32)[:, 768:1152], A["L1_ffn_w_down"], "mlp1")
            if last_layer >= 6:
                sp.wait_ge(s_psum, 2 * UNITS)
                for n in range(18):
                    if n >= 4:
                        sp.wait_ge(emptied, STAGE_END["nat2"] - 18 + n - 3)
                    e, second = n // 2, n % 2
                    if second:
                        src = A["L2_ffn_shared_w2"] if e == 8 else A["L2_ffn_experts_w2"][e]
                        sp.dma_start(nat2[n % 4], src).then_inc(nat_loaded[n % 4], 16)
                    else:
                        src = A["L2_ffn_shared_w1"] if e == 8 else A["L2_ffn_experts_w1"][e]
                        sp.dma_start(nat2[n % 4].rearrange("p (j d) -> p j d", j=4),
                                     src.rearrange("(j p) d -> p j d", p=P)).then_inc(nat_loaded[n % 4], 16)
                load(w1_3.rearrange("p (e f) -> p e f", e=E), A["L3_ffn_Wl1_ND2H"].rearrange("e p f -> p e f"), "mlp3")
                load(w2_3.rearrange("p (e j d) -> p e j d", e=E, j=2), A["L3_ffn_Wl2_NHD"].rearrange("e (j p) d -> p e j d", p=P), "mlp3")

            def load_rows(r):
                R = r.R
                sp.wait_ge(scattered, R.scatter0 + 16 * NB * R.k)

                def one(it, s):
                    if r.at or not isinstance(it, int):
                        sp.wait_ge(mT_psum, r.at + 2 * it + s - 1)
                    sp.dma_start(row_in[s][:, :], R.rows[ds((2 * it + s) * P, P), :]).then_inc(rows_loaded[s], 16)
                one(0, 0)
                one(0, 1)
                with sp.Fori(1, r.tiles // 2) as it:
                    one(it, 0)
                    one(it, 1)
            if last_layer >= 6:
                load_rows(RO2)
            if last_layer >= 8:
                load_rows(RO3)

            with sp.Fori(0, NB) as b:
                sp.wait_ge(*x_ready(last_layer - 1, b + 1))
                sp.dma_start(out.rearrange("b s d -> s b d")[:, ds(b, 1), :].rearrange("s o d -> s (o d)"), X[:, ds(b * D, D)]).then_inc(written, 16)
            sp.wait_ge(written, 16 * NB)

        @block.gpsimd
        def _(pool):
            g = nc.gpsimd
            c = Chain(pool, const_step)
            c.link(g.memset(zero_tile[:, :], 0.0))
            for i, n in enumerate((CAP_ROWS, TILES2 * P, TILES3 * P)):
                view = rows_d[i][0:n, :].rearrange("(t p) d -> p t d", p=P)
                z = spread(zero_tile[:, :].rearrange("p (o d) -> p o d", o=1), 1, n // P)
                pool.dma_start(view, z).then_inc(zeroed, 16)
            c.link(g.memset(ones[:, :], 1.0))
            c.link(g.memset(CT[C:C + 1, :], 1.0))
            c.link(g.memset(ident[:, :], 0.0))
            c.link(g.affine_select(out=ident[:, :], in_=ident[:, :], compare_op=ALU.not_equal, fill=1.0,
                                   base=0, pattern=[[-1, P]], channel_multiplier=1))
            c.link(g.memset(earlier[:, :], 0.0))
            c.link(g.affine_select(out=earlier[:, :], in_=earlier[:, :], compare_op=ALU.is_ge, fill=1.0,
                                   base=0, pattern=[[-1, P]], channel_multiplier=1))
            c.link(g.memset(headmask[:, :], 1.0))
            c.link(g.affine_select(out=headmask[:, :], in_=headmask[:, :], compare_op=ALU.is_ge, fill=0.0,
                                   base=0, pattern=[[-8, H]], channel_multiplier=1))
            c.link(g.affine_select(out=headmask[:, :], in_=headmask[:, :], compare_op=ALU.is_ge, fill=0.0,
                                   base=7, pattern=[[8, H]], channel_multiplier=-1))
            scratch_i = texp_i
            c.link(g.iota(tcmp[:, 0:NB * E].bitcast(I32).rearrange("p (t e) -> p t e", e=E), pattern=[[0, NB], [-1, E]], base=8, channel_multiplier=0))
            c.link(g.tensor_copy(desc8[:, :, :], tcmp[:, 0:NB * E].bitcast(I32).rearrange("p (t e) -> p t e", e=E)))
            c.link(g.iota(tcmp[:, :].bitcast(I32).rearrange("p (t e) -> p t e", e=E), pattern=[[1, TILES2], [0, E]], base=0, channel_multiplier=0))
            c.link(g.tensor_copy(tileno[:, :, :], tcmp[:, :].bitcast(I32).rearrange("p (t e) -> p t e", e=E)))
            c.link(g.iota(ecmp[:, :].bitcast(I32).rearrange("p (e j) -> p e j", e=E), pattern=[[0, E], [P, NB]], base=0, channel_multiplier=0))
            c.link(g.tensor_copy(steps128[:, :, :], ecmp[:, :].bitcast(I32).rearrange("p (e j) -> p e j", e=E)))
            picks = scratch_i[:, 0:2 * NB].rearrange("p (k t) -> p k t", k=2)
            c.link(g.iota(picks, pattern=[[NT, 2], [P, NB]], base=CAP_ROWS, channel_multiplier=1))
            g.tensor_copy(trash[:, :, :], picks).then_inc(const_done, 1)

            def pool_attention(L, R=None):
                def one(it, s, first):
                    b = 2 * it + s
                    if L.wide:
                        if not first:
                            pool.wait_ge(v_psum, L.v0 + 2 * (b - 2) + 2)
                        g.tensor_copy(cts[s][:, :], CT[0:C, ds(b * NK, NK)]).then_inc(cts_ready, 1)
                    else:
                        if not first:
                            pool.wait_ge(s_psum, L.unit0 + NU * (b - 2) + NU)
                        g.tensor_tensor(kbd[s].rearrange("p (h k) -> p h k", h=H),
                                        spread(kT_all[:, ds(b * NK, NK)].rearrange("p (o k) -> p o k", o=1), 1, H),
                                        spread(headmask[:, :].rearrange("p (h o) -> p h o", o=1), 2, NK),
                                        ALU.mult).then_inc(kbd_ready, 1)
                        if not first:
                            pool.wait_ge(o_psum, L.unit0 + NU * (b - 2) + NU)
                        g.tensor_copy(vbd_steps[s][:, :, 0:8], v_narrow[:, ds(b * D, D)].rearrange("k (h e) -> k h e", e=8))\
                            .then_inc(vbd_ready, 1)

                def bias(b):
                    pool.wait_ge(xn_ready, L.batch0 + b + 1)
                    g.tensor_tensor(X[:, ds(b * D, D)], X[:, ds(b * D, D)], bo_rows[L.bias][:, :], ALU.add).then_inc(bias_added, 1)
                if L.wide:
                    pool.wait_ge(emptied, STAGE_END["ct"])
                else:
                    pool.wait_ge(vbd_blank, 2 * L.nar_n + 2)
                    pool.wait_ge(emptied, STAGE_END[f"kv{L.n}"])
                def pair(it):
                    for s in range(2):
                        one(it, s, False)
                        if L.bias is not None:
                            bias(2 * it + s - 2)
                if R is not None:
                    gather(R, 0)
                    gather(R, 1)
                one(0, 0, True)
                one(0, 1, True)
                if R is not None:
                    gather(R, 2)
                    for it in range(1, NB // 2):
                        pair(it)
                        if it + 2 < NB // 2:
                            gather(R, it + 2)
                else:
                    with pool.Fori(1, NB // 2) as it:
                        pair(it)
                if L.bias is not None:
                    bias(NB - 2)
                    bias(NB - 1)

            def scatter(R):
                pool.wait_ge(zeroed, 16 * 3)
                pool.wait_ge(routed, R.n + 1)
                for t in range(NB):
                    for k in range(R.k):
                        g.indirect_dma_start(R.rows[:, :], bass.IndirectOffsetOnAxis(ap=to_row[k][:, t:t + 1], axis=0),
                                             XN[:, t * D:(t + 1) * D], None).then_inc(scattered, 16)
                pool.wait_ge(scattered, R.scatter0 + 16 * NB * R.k)

            def gather(R, pair):
                if pair == 0:
                    for s in range(2):
                        pool.wait_ge(stored[s], STORED_END[R.n])
                for n in range(2 * R.k * pair, 2 * R.k * (pair + 1)):
                    t, k, s = n // R.k, n % R.k, n % 4
                    if n >= 4:
                        pool.wait_ge(combined, COMBINE0[R.n] + n - 3)
                    g.indirect_dma_start(got[s][:, :], None, R.outs[0:R.total, :],
                                         bass.IndirectOffsetOnAxis(ap=from_row[k][:, t:t + 1], axis=0)).then_inc(gathered[s], 16)

            def store_rows(r):
                def one(it, s):
                    pool.wait_ge(m2_done, r.at + 2 * it + s + 1)
                    pool.dma_start(r.R.outs[ds((2 * it + s) * P, P), :], row_out[s][:, :]).then_inc(stored[s], 16)
                with pool.Fori(0, r.tiles // 2) as it:
                    one(it, 0)
                    one(it, 1)

            pool_attention(ATT[0])
            if last_layer >= 2:
                scatter(RT[0])
                def store0(it, s):
                    e = 2 * it + s
                    pool.wait_ge(o0_ready, e + 1)
                    pool.dma_start(outs_d[0][ds(e * CAP, 2 * P), :].rearrange("(r p) d -> p r d", p=P), o0[s][:, 0:2, :]).then_inc(stored[s], 16)
                    pool.dma_start(outs_d[0][ds(e * CAP + 2 * P, CAP - 2 * P), :], o0[s][0:CAP - 2 * P, 2, :]).then_inc(stored[s], 16)
                with pool.Fori(0, E // 2) as it:
                    store0(it, 0)
                    store0(it, 1)
            if last_layer >= 3:
                pool_attention(ATT[1], RT[0])
            if last_layer >= 5:
                pool_attention(ATT[2])
            if last_layer >= 6:
                scatter(RT[1])
                store_rows(RO2)
            if last_layer >= 7:
                pool_attention(ATT[3], RT[1])
            if last_layer >= 8:
                scatter(RT[2])
                store_rows(RO3)
                for pair in range(NB // 2):
                    gather(RT[2], pair)

        @block.tensor
        def _(pe):
            st = Turns(pe, filled, emptied, bank[0:4])
            mm, tp = nc.tensor.matmul, nc.tensor.transpose

            def prepare_m(n):
                pe.wait_ge(loaded[f"wqk{n}"], 32)
                for half in range(2):
                    b = st.claim()
                    for i in range(4):
                        j = 4 * half + i
                        last = tp(b[:, i * P:(i + 1) * P], wq_nat[:, j * P:(j + 1) * P], ident[:, :])
                    st.fill(last)
                for half in range(2):
                    b = st.claim()
                    for i in range(4):
                        j = 4 * half + i
                        last = tp(b[:, i * C:(i + 1) * C], wk_nat[:, j * P:(j + 1) * P], ident[0:C, 0:C])
                    st.fill(last)
                st.settle()
                for q in range(4):
                    b = st.claim()
                    for i in range(4):
                        h = 8 * (q // 2) + 2 * i + q % 2
                        at = 64 * (h % 2)
                        last = mm(b[0:C, i * D:(i + 1) * D], wkT[at:at + 64, h // 2, :], wqT[at:at + 64, h // 2, :],
                                  start=True, stop=True)
                    st.fill(last)
                st.settle()

            def make_t(h0, h1):
                for h in range(h0, h1):
                    for b0, b1 in T_CHUNKS:
                        b = st.claim()
                        st.fill(mm(b[:, 0:(b1 - b0) * NK], MT[:, h, :], CT[0:C, b0 * NK:b1 * NK], start=True, stop=True))
                if h1 == H:
                    st.settle()

            def pe_attention(L):
                wide = L.wide

                def turn_x(b, s):
                    pe.wait_ge(xn_ready, L.batch0 + b + 1)
                    if not isinstance(b, int) or b > 0:
                        pe.wait_ge(xnT_ready, L.batch0 + b)
                    tp(TR_BANK[:, 0:P], xn[s][:, :], ident[:, :]).then_inc(xnT_psum, 1)

                def query(b, s):
                    pe.wait_ge(xnT_ready, L.batch0 + b + 1)
                    mm(TR_BANK[:, 0:P], nwq[L.nar_n][:, :], xnT[s][:, :], start=True, stop=True).then_inc(q_psum, 1)

                def values(b, s, half):
                    if half == 0:
                        pe.wait_ge(cts_ready, L.c0 + b + 1)
                    n = 2 * b + half
                    if not isinstance(b, int) or b > 0 or half:
                        pe.wait_ge(v_ready, L.v0 + n)
                    mm(V_BANK[0:NK, :], cts[s][:, :], wv[:, half * 512:(half + 1) * 512],
                       start=True, stop=True).then_inc(v_psum, 1)

                def scores(U, b, s, u):
                    if u == 0:
                        if wide:
                            pe.wait_ge(xnT_ready, L.batch0 + b + 1)
                        else:
                            pe.wait_ge(q_ready, L.q0 + b + 1)
                            pe.wait_ge(kbd_ready, L.q0 + b + 1)
                    if not isinstance(U, int) or U >= 2:
                        pe.wait_ge(z_ready, L.unit0 + U - 1)
                    rhs = T_all[:, ds(b * KW + u * UW, UW)] if wide else kbd[s][:, u * UW:(u + 1) * UW]
                    lhs = xnT[s] if wide else qT[s]
                    mm(S_BANK[u % 2][:, 0:UW], lhs[:, :], rhs, start=True, stop=True).then_inc(s_psum, 1)

                def turn_p(U, u):
                    pe.wait_ge(p_ready, L.unit0 + U + 1)
                    if not isinstance(U, int) or U >= 2:
                        pe.wait_ge(pT_ready, L.unit0 + U - 1)
                    for i in range(UH):
                        last = tp(PT_BANK[u % 2][0:NK, i * P:(i + 1) * P], PR[u % 2][:, i * NK:(i + 1) * NK], ident[:, :])
                    last.then_inc(pT_psum, 1)

                def weigh(U, b, s, u):
                    pe.wait_ge(pT_ready, L.unit0 + U + 1)
                    if wide and u == 0:
                        pe.wait_ge(v_ready, L.v0 + 2 * b + 2)
                    if not wide:
                        if u == 0:
                            pe.wait_ge(vbd_ready, L.q0 + b + 1)
                        if u % 2 == 0 and (not isinstance(b, int) or b > 0):
                            pe.wait_ge(on_ready, L.on0 + 2 * (b - 1) + u // 2 + 1)
                    elif not isinstance(U, int) or U >= 1:
                        pe.wait_ge(on_ready, L.on0 + U)
                    for i in range(UH):
                        h = u * UH + i
                        if wide:
                            last = mm(O_BANK[:, i * OB:(i + 1) * OB], PT[u % 2][:, i, :], vw[s][:, h, :], start=True, stop=True)
                        else:
                            last = mm(ON_BANK[u // 2][:, 0:P], vbd[s][:, h * P:(h + 1) * P], PT[u % 2][:, i, :],
                                      start=(h % 8 == 0), stop=(h % 8 == 7))
                    last.then_inc(o_psum, 1)

                def project(U, b, s, u):
                    if wide:
                        pe.wait_ge(oT_ready, L.oT0 + U + 1)
                        if u == 0 and (not isinstance(b, int) or b > 0):
                            pe.wait_ge(L.x_out, b)
                        for j in range(2):
                            last = mm(Y_BANK[:, 0:D], OT[u % 2][:, j, :], wo[:, 2 * u + j, :],
                                      start=(u == 0 and j == 0), stop=(u == NU - 1 and j == 1))
                        if u == NU - 1:
                            last.then_inc(y_psum, 1)
                    elif u == NU - 1:
                        pe.wait_ge(on_ready, L.on0 + 2 * b + 2)
                        if not isinstance(b, int) or b > 0:
                            pe.wait_ge(L.x_out, b)
                        mm(Y_BANK[:, 0:D], OTn[s][:, :], nwo[L.nar_n][:, :], start=True, stop=True).then_inc(y_psum, 1)

                def steps(it):
                    for k in range(2 * NU):
                        U = 2 * NU * it + k

                        def stage(lag):
                            V = U - lag
                            kk = k - lag
                            bb = 2 * it + kk // NU
                            if isinstance(V, int) and not 0 <= V < UNITS:
                                return None
                            return V, bb, (kk // NU) % 2, kk % NU
                        if a := stage(0):
                            scores(*a)
                        if a := stage(1):
                            turn_p(a[0], a[3])
                        if a := stage(2):
                            weigh(*a)
                        if wide and (a := stage(3)):
                            V, b, s, u = a
                            pe.wait_ge(on_ready, L.on0 + V + 1)
                            nb = 2 * it + (k - 2) // NU + 2
                            if isinstance(nb, int):
                                nb = min(max(nb, 1), NB)
                            pe.wait_ge(xnT_ready, L.batch0 + nb)
                            if not isinstance(V, int) or V >= 1:
                                pe.wait_ge(oT_ready, L.oT0 + V)
                            for j in range(2):
                                last = tp(TR_BANK[:, j * P:(j + 1) * P], ON[u % 2][:, j * P:(j + 1) * P], ident[:, :])
                            last.then_inc(oT_psum, 1)
                        if a := stage(4):
                            project(*a)
                        b1 = 2 * it + k // NU + 1
                        if isinstance(b1, int) and b1 >= NB:
                            continue
                        s1 = (k // NU + 1) % 2
                        u = k % NU
                        if u == 1:
                            if wide:
                                done = 2 * NU * it + k - 2
                                if not isinstance(done, int) or done >= 1:
                                    pe.wait_ge(oT_ready, L.oT0 + done)
                            else:
                                pe.wait_ge(q_ready, L.q0 + b1)
                            turn_x(b1, s1)
                        if wide and u >= 2:
                            values(b1, s1, u - 2)
                        if not wide and u == 3:
                            query(b1, s1)

                turn_x(0, 0)
                if wide:
                    pe.wait_ge(loaded[f"wvo{L.wide_n}"], 32)
                    values(0, 0, 0)
                    values(0, 0, 1)
                else:
                    query(0, 0)
                steps(0)
                with pe.Fori(1, NB // 2 - 1) as it:
                    steps(it)
                steps(NB // 2 - 1)
                steps(NB // 2)

            def turn_all(n):
                for q in range(4):
                    b = st.claim()
                    for i in range(4):
                        t = 4 * q + i
                        pe.wait_ge(xn_kept, NB * n + t + 1)
                        last = tp(b[:, i * P:(i + 1) * P], XN[:, t * D:(t + 1) * D], ident[:, :])
                    st.fill(last)

            def pe_route(R, n):
                turn_all(n)
                for t in range(NB):
                    if t % 4 == 0:
                        pe.wait_ge(emptied, STAGE_END[f"xn{n}"] - 3 + t // 4)
                    last = mm(TR_BANK[:, t * E:(t + 1) * E], xnT_all[:, t * P:(t + 1) * P], wr[R.n][:, :], start=True, stop=True)
                last.then_inc(logits_psum, 1)

            def pe_shared(S):
                def first(g):
                    for f in range(S.nf):
                        p = S.nf * g + f
                        rhs = xnT_all[:, g * 512:(g + 1) * 512]
                        if S.gate:
                            if p >= 2:
                                pe.wait_ge(sh_ready, S.parts0 + p - 1)
                            mm(bank[2 * (p % 2)][:, :], S.gate(f), rhs, start=True, stop=True).then_inc(sh_psum, 1)
                            mm(bank[2 * (p % 2) + 1][:, :], S.w1(f), rhs, start=True, stop=True).then_inc(sh_psum, 1)
                        else:
                            if p >= 4:
                                pe.wait_ge(sh_ready, S.parts0 + p - 3)
                            mm(bank[p % 4][:, :], S.w1(f), rhs, start=True, stop=True).then_inc(sh_psum, 1)

                def second(g):
                    pe.wait_ge(sh_ready, S.parts0 + S.nf * (g + 1))
                    if g >= 2:
                        pe.wait_ge(shared_done, 4 * (S.groups0 + g - 1))
                    for t in range(4):
                        for f in range(S.nf):
                            last = mm(bank[6 + g % 2][:, t * D:(t + 1) * D], shT[g % 2][:, f, t * P:(t + 1) * P], S.w2(f),
                                      start=(f == 0), stop=(f == S.nf - 1))
                    last.then_inc(so_psum, 1)
                first(0)
                for g in range(4):
                    if g < 3:
                        first(g + 1)
                    second(g)
                pe.wait_ge(shared_done, 4 * (S.groups0 + 4))

            def pe_rank(R):
                pe.wait_ge(picked, R.n + 1)
                both = rt["both"][:, :, :].rearrange("p t e -> p (t e)")
                mm(bank[4][:, 0:NB * E], earlier[:, :], both, start=True, stop=True)
                mm(bank[5][:, 0:NB * E], ones[:, :], both, start=True, stop=True).then_inc(ranked, 1)

            def pe_mlp(r):
                w, nj = r.width, r.width // P
                tr, out_b = TR_BANK, Y_BANK
                h_bank = [[bank[0], bank[1]], [bank[2], bank[3]]]
                t_bank = [bank[4], bank[5]]
                def turn(it, s):
                    i = 2 * it + s
                    pe.wait_ge(rows_loaded[s], 16 * (r.rows0 + it + 1))
                    if r.at or not isinstance(it, int) or i > 0:
                        pe.wait_ge(mT_ready, r.at + i)
                    tp(tr[:, 0:P], row_in[s][:, :], ident[:, :]).then_inc(mT_psum, 1)

                def expert(it, s):
                    return pe.value_load(texp_i[0:1, ds(2 * it + s, 1)], min_val=0, max_val=E - 1)

                def first(it, s, e):
                    i = 2 * it + s
                    pe.wait_ge(mT_ready, r.at + i + 1)
                    if not isinstance(it, int) or it > 0:
                        pe.wait_ge(h_ready, r.at + i - 1)
                    mm(h_bank[s][0][:, :], mxT[s][:, :], r.w1[:, ds(e * 512, 512)], start=True, stop=True).then_inc(m1_psum, 1)

                def turn_h(it, s):
                    i = 2 * it + s
                    pe.wait_ge(h_ready, r.at + i + 1)
                    if not isinstance(it, int) or it > 0:
                        pe.wait_ge(hT_ready, r.at + i - 1)
                    for j in range(nj):
                        last = tp(t_bank[s][:, j * P:(j + 1) * P], hid[s][:, j * P:(j + 1) * P], ident[:, :])
                    last.then_inc(hT_psum, 1)

                def second(it, s, e):
                    i = 2 * it + s
                    pe.wait_ge(hT_ready, r.at + i + 1)
                    if not isinstance(it, int) or i > 0:
                        pe.wait_ge(m2_done, r.at + i)
                    for j in range(nj):
                        last = mm(out_b[:, 0:D], hidT[s][:, j, :], r.w2[:, ds(e * w + j * P, P)], start=(j == 0), stop=(j == nj - 1))
                    last.then_inc(m2_psum, 1)

                n2 = r.tiles // 2

                def steps(it):
                    for s in range(2):
                        i = 2 * it + s
                        if not isinstance(i, int) or i < r.tiles:
                            first(it, s, expert(it, s))
                        if not isinstance(i, int) or i + 1 < r.tiles:
                            turn(*((it, 1) if s == 0 else (it + 1, 0)))
                        if not isinstance(i, int) or 1 <= i <= r.tiles:
                            turn_h(*((it - 1, 1) if s == 0 else (it, 0)))
                        if not isinstance(i, int) or 2 <= i <= r.tiles + 1:
                            second(it - 1, s, expert(it - 1, s))
                turn(0, 0)
                steps(0)
                with pe.Fori(1, n2 - 1) as it:
                    steps(it)
                steps(n2 - 1)
                steps(n2)

            def narrow_kv(L):
                n, rows = L.nar_n, C + 1 if L.n == 2 else C
                if L.n == 3:
                    pe.wait_ge(loaded["narrow3"], 64)
                pe.wait_ge(const_done, 1)
                for b0, b1 in T_CHUNKS:
                    b = st.claim()
                    st.fill(mm(b[:, 0:(b1 - b0) * NK], nwk[n][0:rows, :], CT[0:rows, b0 * NK:b1 * NK], start=True, stop=True))
                for q in range(4):
                    b = st.claim()
                    for i in range(4):
                        last = mm(b[0:NK, i * D:(i + 1) * D], CT[0:rows, (4 * q + i) * NK:(4 * q + i + 1) * NK],
                                  nwv[n][0:rows, :], start=True, stop=True)
                    st.fill(last)
                st.settle()

            pe.wait_ge(const_done, 1)
            pe.wait_ge(loaded["ctx"], 16)
            for q in range(4):
                b = st.claim()
                for i in range(4):
                    last = tp(b[0:C, i * NK:(i + 1) * NK], ctx_nat[:, 4 * q + i, :], ident[0:NK, 0:NK])
                st.fill(last)
            pe.wait_ge(loaded["misc"], 16 * 4)
            b = st.claim()
            st.fill(tp(b[:, 0:32], row_in[0][0:32, :], ident[0:32, 0:32]))
            b = st.claim()
            st.fill(tp(b[:, 0:E], row_in[1][0:E, :], ident[0:E, 0:E]))
            prepare_m(0)
            make_t(0, H)
            if last_layer >= 3:
                prepare_m(1)
            pe.wait_ge(loaded["narrow2"], 16 * 7)
            for src in (got[0], got[1]):
                b = st.claim()
                st.fill(tp(b[:, 0:P], src[:, :], ident[:, :]))
            for src in (got[2], got[3]):
                b = st.claim()
                st.fill(tp(b[0:C, 0:P], src[:, 0:C], ident[:, :]))
            st.settle()
            pe.wait_ge(dve_prepared, 1)
            pe_attention(ATT[0])
            if last_layer >= 2:
                pe_route(RT[0], 0)
                if last_layer >= 3:
                    make_t(0, 3)
                pe_rank(RT[0])
                if last_layer >= 3:
                    make_t(3, H)
                for q in range(RT[0].tiles // 4):
                    if q == 0:
                        pe.wait_ge(rows_loaded[0], 16)
                    if (q + 1) * 4 > RT[0].tiles // 2:
                        pe.wait_ge(rows_loaded[1], 16)
                    b = st.claim()
                    for i in range(4):
                        last = tp(b[:, i * P:(i + 1) * P], rows0[:, 4 * q + i, :], ident[:, :])
                    st.fill(last)
                st.settle()

                def hidden(it, s):
                    e = 2 * it + s
                    pe.wait_ge(w_loaded[s], 32 * (it + 1))
                    for f in range(4):
                        if not isinstance(e, int) or e > 0:
                            pe.wait_ge(h0_ready, 4 * e + f - 3)
                        mm(bank[f][:, 0:CAP], w1s[s][:, f * P:(f + 1) * P], bufT[:, ds(e * CAP, CAP)],
                           start=True, stop=True).then_inc(h0_psum, 1)

                def outputs(it, s):
                    e = 2 * it + s
                    pe.wait_ge(h0_ready, 4 * e + 4)
                    if not isinstance(e, int) or e >= 2:
                        pe.wait_ge(o0_ready, e - 1)
                    ob = bank[4 + s]
                    for q in range(3):
                        n = min(P, CAP - q * P)
                        for f in range(4):
                            last = mm(ob[0:n, q * D:(q + 1) * D], hT0[s][:, f, q * P:q * P + n], w2s[s][:, f, :],
                                      start=(f == 0), stop=(f == 3))
                    last.then_inc(o0_psum, 1)
                hidden(0, 0)
                hidden(0, 1)
                outputs(0, 0)
                with pe.Fori(1, E // 2) as it:
                    hidden(it, 0)
                    outputs(it - 1, 1)
                    hidden(it, 1)
                    outputs(it, 0)
                outputs(E // 2 - 1, 1)
                pe.wait_ge(o0_ready, E)
            if last_layer >= 3:
                pe_attention(ATT[1])
            if last_layer >= 4:
                turn_all(1)
                pe.wait_ge(dve_prepared, 2)
                for k in range(2):
                    b = st.claim()
                    for j in range(3):
                        last = tp(b[:, j * P:(j + 1) * P], w1n[:, k * 384 + j * P:k * 384 + (j + 1) * P], ident[:, :])
                    st.fill(last)
                b = st.claim()
                for j in range(3):
                    last = tp(b[:, j * P:(j + 1) * P], w1n[:, 768 + j * P:768 + (j + 1) * P], ident[:, :])
                st.fill(last)
                st.settle()
                pe_shared(SH1)
            if last_layer >= 5:
                narrow_kv(ATT[2])
                pe_attention(ATT[2])
            if last_layer >= 6:
                pe_route(RT[1], 2)
                for n in range(18):
                    if n == 8:
                        pe_rank(RT[1])
                    pe.wait_ge(nat_loaded[n % 4], 16 * (n // 4 + 1))
                    b = st.claim()
                    for j in range(4):
                        last = tp(b[:, j * P:(j + 1) * P], nat2[n % 4][:, j * P:(j + 1) * P], ident[:, :])
                    st.fill(last)
                st.settle()
                pe_shared(SH2)
                pe.wait_ge(routed, 2)
                pe_mlp(RO2)
            if last_layer >= 7:
                pe.wait_ge(m2_done, RO2.at + RO2.tiles)
                narrow_kv(ATT[3])
                pe_attention(ATT[3])
            if last_layer >= 8:
                pe_route(RT[2], 3)
                pe_rank(RT[2])
                pe.wait_ge(loaded["mlp3"], 32)
                pe_shared(SH3)
                pe.wait_ge(routed, 3)
                pe_mlp(RO3)

        @block.scalar
        def _(act):
            st = Turns(act, filled, emptied, bank[0:4])
            a = nc.scalar.activation

            def copy(o, i):
                return a(o, i, ACT.Copy)

            def prepare_m(n):
                for half in range(2):
                    b = st.take()
                    st.empty(copy(wqT[:, 4 * half:4 * half + 4, :], b[:, :].rearrange("p (j d) -> p j d", j=4)))
                for half in range(2):
                    b = st.take()
                    st.empty(copy(wkT[:, 4 * half:4 * half + 4, :], b[:, 0:4 * C].rearrange("p (j c) -> p j c", j=4)))
                for q in range(4):
                    b = st.take()
                    heads = MT[:, 8 * (q // 2):8 * (q // 2) + 8, :].rearrange("c (i two) d -> c i two d", two=2)
                    st.empty(copy(heads[:, :, q % 2, :], b[0:C, :].rearrange("p (j d) -> p j d", j=4)))

            def make_t():
                for h in range(H):
                    for b0, b1 in T_CHUNKS:
                        b = st.take()
                        o = T_all[:, b0 * KW:b1 * KW].rearrange("p (b h k) -> p b h k", h=H, k=NK)[:, :, h, :]
                        st.empty(copy(o, b[:, 0:(b1 - b0) * NK].rearrange("p (b k) -> p b k", k=NK)))

            def act_attention(L):
                wide = L.wide

                def turned_x(b, s):
                    act.wait_ge(xnT_psum, L.batch0 + b + 1)
                    copy(xnT[s][:, :], TR_BANK[:, 0:P]).then_inc(xnT_ready, 1)

                def query(b, s):
                    act.wait_ge(q_psum, L.q0 + b + 1)
                    if L.n == 2:
                        a(qT[s][:, :], TR_BANK[:, 0:P], ACT.Identity, bias=bq2[:, 0:1]).then_inc(q_ready, 1)
                    else:
                        copy(qT[s][:, :], TR_BANK[:, 0:P]).then_inc(q_ready, 1)

                def values(b, s, half):
                    act.wait_ge(v_psum, L.v0 + 2 * b + half + 1)
                    copy(vw[s][:, half * 8:half * 8 + 8, 0:64], V_BANK[0:NK, :].rearrange("k (h e) -> k h e", h=8)).then_inc(v_ready, 1)

                def steps(it):
                    for k in range(2 * NU):
                        U = 2 * NU * it + k

                        def stage(lag):
                            V = U - lag
                            kk = k - lag
                            if isinstance(V, int) and not 0 <= V < UNITS:
                                return None
                            return V, 2 * it + kk // NU, kk % NU
                        if t := stage(1):
                            V, b, u = t
                            act.wait_ge(pT_psum, L.unit0 + V + 1)
                            copy(PT[u % 2], PT_BANK[u % 2][0:NK, :].rearrange("k (h q) -> k h q", h=UH)).then_inc(pT_ready, 1)
                        if wide and (t := stage(3)):
                            V, b, u = t
                            act.wait_ge(oT_psum, L.oT0 + V + 1)
                            copy(OT[u % 2], TR_BANK[:, 0:256].rearrange("p (j q) -> p j q", j=2)).then_inc(oT_ready, 1)
                        if t := stage(0):
                            V, b, u = t
                            act.wait_ge(z_ready, L.unit0 + V + 1)
                            a(PR[u % 2], Z[u % 2], ACT.Exp, scale=L.scale).then_inc(p_ready, 1)
                        b1 = 2 * it + k // NU + 1
                        if isinstance(b1, int) and b1 >= NB:
                            continue
                        s1 = (k // NU + 1) % 2
                        u = k % NU
                        if u == 1:
                            turned_x(b1, s1)
                        if wide and u >= 2:
                            values(b1, s1, u - 2)
                        if not wide and u == 3:
                            query(b1, s1)
                act.preload_act_table(ACT.Exp)
                turned_x(0, 0)
                if wide:
                    values(0, 0, 0)
                    values(0, 0, 1)
                else:
                    query(0, 0)
                steps(0)
                with act.Fori(1, NB // 2 - 1) as it:
                    steps(it)
                steps(NB // 2 - 1)
                steps(NB // 2)

            def turned_all():
                for q in range(4):
                    b = st.take()
                    st.empty(copy(xnT_all[:, q * 512:(q + 1) * 512], b[:, :]))

            def act_route(R):
                turned_all()
                act.wait_ge(exps_in, R.n + 1)
                if R.n == 1:
                    a(rc["gate2"][:, :], rc["diff"][:, :], ACT.Exp).then_inc(exps_out, 1)
                else:
                    a(rt["score"][:, :, :], rt["work"][:, :, :], ACT.Exp).then_inc(exps_out, 1)

            def act_shared(S):
                act.preload_act_table(ACT.Silu)
                for p in range(4 * S.nf):
                    g, f = p // S.nf, p % S.nf
                    if S.gate:
                        act.wait_ge(sh_psum, S.products0 + 2 * p + 1)
                        a(sh_gate[p % 2], bank[2 * (p % 2)][:, :], ACT.Silu).then_inc(sh_gated, 1)
                    else:
                        act.wait_ge(sh_psum, S.products0 + p + 1)
                        if g >= 2 and f == 0:
                            act.wait_ge(so_psum, S.groups0 + g - 1)
                        a(shT[g % 2][:, f, :], bank[p % 4][:, :], ACT.Silu).then_inc(sh_ready, 1)

            def act_mlp(r):
                w, nj = r.width, r.width // P
                h_bank = [[bank[0], bank[1]], [bank[2], bank[3]]]

                def turned(it, s):
                    i = 2 * it + s
                    act.wait_ge(mT_psum, r.at + i + 1)
                    if not isinstance(it, int) or it > 0:
                        act.wait_ge(m1_psum, r.at + i - 1)
                    copy(mxT[s][:, :], TR_BANK[:, 0:P]).then_inc(mT_ready, 1)

                def bend(it, s):
                    i = 2 * it + s
                    act.wait_ge(m1_psum, r.at + i + 1)
                    if r.gated:
                        if not isinstance(it, int) or it > 0:
                            act.wait_ge(h_ready, r.at + i - 1)
                        a(gate[s][:, 0:w], h_bank[s][0][:, w:2 * w], ACT.Silu).then_inc(g_ready, 1)
                    else:
                        if not isinstance(it, int) or it > 0:
                            act.wait_ge(hT_psum, r.at + i - 1)
                        a(hid[s][:, 0:w], h_bank[s][0][:, 0:w], ACT.Silu).then_inc(h_ready, 1)
                act.preload_act_table(ACT.Silu)

                def steps(it):
                    for s in range(2):
                        i = 2 * it + s
                        bend(it, s)
                        if not isinstance(i, int) or i + 1 < r.tiles:
                            turned(*((it, 1) if s == 0 else (it + 1, 0)))
                turned(0, 0)
                steps(0)
                with act.Fori(1, r.tiles // 2 - 1) as it:
                    steps(it)
                steps(r.tiles // 2 - 1)

            def narrow_kv(L):
                if L.q0:
                    act.wait_ge(vbd_ready, L.q0)
                for b0, b1 in T_CHUNKS:
                    b = st.take()
                    st.empty(copy(kT_all[:, b0 * NK:b1 * NK], b[:, 0:(b1 - b0) * NK]))
                for q in range(4):
                    b = st.take()
                    st.empty(copy(v_narrow[:, q * 512:(q + 1) * 512], b[0:NK, :]))

            for q in range(4):
                b = st.take()
                st.empty(copy(CT[0:C, 4 * q * NK:(4 * q + 4) * NK], b[0:C, 0:4 * NK]))
            b = st.take()
            st.empty(copy(b1c[:, :], b[:, 0:32]))
            b = st.take()
            st.empty(copy(wr[1][:, :], b[:, 0:E]))
            prepare_m(0)
            make_t()
            if last_layer >= 3:
                prepare_m(1)
            b = st.take()
            st.empty(copy(nwq[0][:, :], b[:, 0:P]))
            b = st.take()
            st.empty(copy(nwo[0][:, :], b[:, 0:P]))
            for half in range(2):
                b = st.take()
                v = b[0:C, 0:P].rearrange("c (h e) -> c h e", e=16)
                copy(nwk[0][0:C, half * 64:half * 64 + 64].rearrange("c (h e) -> c h e", e=8), v[:, :, 0:8])
                st.empty(copy(nwv[0][0:C, half * 64:half * 64 + 64].rearrange("c (h e) -> c h e", e=8), v[:, :, 8:16]))
            act_attention(ATT[0])
            if last_layer >= 2:
                act_route(RT[0])
                if last_layer >= 3:
                    make_t()
                for q in range(RT[0].tiles // 4):
                    b = st.take()
                    st.empty(copy(bufT[:, q * 512:(q + 1) * 512], b[:, :]))
                act.preload_act_table(ACT.Gelu)

                def bend0(it, s):
                    e = 2 * it + s
                    for f in range(4):
                        act.wait_ge(h0_psum, 4 * e + f + 1)
                        if f == 0 and (not isinstance(e, int) or e >= 2):
                            act.wait_ge(o0_psum, e - 1)
                        a(hT0[s][:, f, :], bank[f][:, 0:CAP], ACT.Gelu, bias=b1c[:, ds(4 * e + f, 1)]).then_inc(h0_ready, 1)
                bend0(0, 0)
                bend0(0, 1)
                with act.Fori(1, E // 2) as it:
                    bend0(it, 0)
                    bend0(it, 1)
            if last_layer >= 3:
                act_attention(ATT[1])
            if last_layer >= 4:
                turned_all()
                for k in range(2):
                    b = st.take()
                    st.empty(copy((wg1, wu1)[k], b[:, 0:384]))
                b = st.take()
                st.empty(copy(wd1, b[:, 0:384].rearrange("p (j d) -> p j d", j=3)))
                act_shared(SH1)
            if last_layer >= 5:
                narrow_kv(ATT[2])
                act_attention(ATT[2])
            if last_layer >= 6:
                act_route(RT[1])
                for n in range(18):
                    b = st.take()
                    dst = (w2_2 if n % 2 else w1_2)[:, (n // 2) * 512:(n // 2 + 1) * 512]
                    st.empty(copy(dst, b[:, :]))
                act_shared(SH2)
                act_mlp(RO2)
            if last_layer >= 7:
                narrow_kv(ATT[3])
                act_attention(ATT[3])
            if last_layer >= 8:
                act_route(RT[2])
                act_shared(SH3)
                act_mlp(RO3)

        @block.vector
        def _(dve):
            v = nc.vector
            c = Chain(dve, dve_step)
            tt, ts, stt = v.tensor_tensor, v.tensor_scalar, v.scalar_tensor_tensor

            def flat(t):
                return t[:, :, :].rearrange("p a b -> p (a b)")

            LN_STEPS = 14

            def norm_stats(it, ready):
                ready(2 * it + 1)
                for s in range(2):
                    xb = X[:, ds((2 * it + s) * D, D)]
                    ins = v.bn_stats(ln_stats[:, s, :], xb)
                    if s == 0:
                        ins.then_inc(dve_step, 1)
                        c.n += 1
                    else:
                        c.link(ins)
                v.tensor_copy(ln_t[:, 0:1], ln_stats[:, 0, 0:1])
                for s in range(2):
                    ins = v.bn_aggr(ln_mv[:, s, :], ln_stats[:, s, :])
                    if s == 0:
                        ins.then_inc(dve_step, 1)
                        c.n += 1
                    else:
                        c.link(ins)

            def norm_guess():
                c.link(ts(ln_ve[:, :], ln_mv[:, :, 1], EPS, None, ALU.add))
                c.link(ts(ln_r[:, :].bitcast(I32), ln_ve[:, :].bitcast(I32), -0.5, RSQRT_MAGIC, ALU.mult, ALU.add))

            def norm_newton():
                c.link(stt(ln_t[:, :], ln_r[:, :], -0.5, ln_r[:, :], ALU.mult, ALU.mult))
                c.link(tt(ln_t[:, :], ln_t[:, :], ln_ve[:, :], ALU.mult))
                c.link(stt(ln_r[:, :], ln_t[:, :], 1.5, ln_r[:, :], ALU.add, ALU.mult))

            def norm_apply(it, free, to):
                free()
                for s in range(2):
                    xb = X[:, ds((2 * it + s) * D, D)]
                    for dst, done in to(it, s):
                        ins = ts(dst, xb, ln_mv[:, s, 0:1], ln_r[:, s:s + 1], ALU.subtract, ALU.mult)
                        ins.then_inc(done, 1)

            def norm_pair(it, ready, free, to):
                norm_stats(it, ready)
                norm_guess()
                for _ in range(3):
                    norm_newton()
                norm_apply(it, free, to)
            LN_LINKS = 2 + 2 + 2 + 9

            def blank():
                for s in range(2):
                    c.link(v.memset(vbd[s], 0.0))
                    c.link(v.memset(vbd_steps[s][:, 0:8, 64:72], 1.0))
                    v.memset(vbd_steps[s][:, 7:15, 72:80], 1.0).then_inc(vbd_blank, 1)

            def dve_attention(L):
                wide = L.wide
                sl = L.unit0

                def norm(it, part=None):
                    def ready(n):
                        if L.n in (1, 3):
                            combine_pair(RT[L.n // 2], it)
                        elif L.n == 2:
                            dve.wait_ge(*x_ready(3, n + 1))
                        if L.n > 0:
                            v.tensor_copy(carry[:, :], ln_mv[:, 0, 0:1])

                    def free():
                        if not isinstance(it, int) or it > 0:
                            dve.wait_ge(xnT_psum, L.batch0 + 2 * it)
                    if part in (None, 0):
                        norm_stats(it, ready)
                        norm_guess()
                    if part in (None, 1):
                        norm_newton()
                    if part in (None, 2):
                        norm_newton()
                    if part in (None, 3):
                        norm_newton()
                        norm_apply(it, free, lambda it, s: [(xn[s][:, :], xn_ready)])

                def add_y(b):
                    dve.wait_ge(y_psum, L.batch0 + b + 1)
                    if L.bias is not None:
                        dve.wait_ge(bias_added, L.b0 + b + 1)
                    xb = X[:, ds(b * D, D)]
                    tt(xb, xb, Y_BANK[:, 0:D], ALU.add).then_inc(L.x_out, 1)
                    dve.wait_ge(L.x_out, b + 1)
                    v.tensor_copy(carry[:, :], ln_mv[:, 0, 0:1])
                    v.bn_stats(all_stats[:, ds(b, 1), :].rearrange("p o s -> p (o s)"), xb).then_inc(stats_ready, 1)

                per = 0

                def steps(it):
                    for k in range(2 * NU):
                        U = 2 * NU * it + k
                        u = k % NU
                        if u == 0:
                            b = 2 * it + k // NU - 2
                            if not isinstance(b, int) or 0 <= b < NB:
                                add_y(b)
                        if not isinstance(U, int) or U < UNITS:
                            b = 2 * it + k // NU
                            dve.wait_ge(s_psum, sl + U + 1)
                            src = S_BANK[u % 2][:, 0:UW].rearrange("p (h k) -> p h k", h=UH)
                            if L.mask:
                                sm = SM[u % 2].rearrange("p (h k) -> p h k", h=UH)
                                c.link(tt(sm, src, spread(notmask[:, ds(b * NK, NK)].rearrange("p (o k) -> p o k", o=1), 1, UH), ALU.add))
                                src = sm
                            c.link(v.tensor_reduce(mx[u % 2][:, :], src, AX.X, ALU.max))
                            tt(Z[u % 2].rearrange("p (h k) -> p h k", h=UH), src,
                               spread(mx[u % 2][:, :].rearrange("p (h o) -> p h o", o=1), 2, NK), ALU.subtract).then_inc(z_ready, 1)
                        V = U - 2
                        if not wide and (k - 2) % 2 == 1 and (not isinstance(V, int) or 0 <= V < UNITS):
                            half = (k - 2) % NU // 2
                            rows_o, rows_d_ = (slice(0, 64), slice(64, P))[::1 - 2 * half]
                            ob = ON_BANK[half]
                            dve.wait_ge(o_psum, sl + V + 1)
                            c.link(v.reciprocal(rden[rows_o, :], ob[rows_d_, 0:P]))
                            tt(OTn[(k - 2) // NU % 2][rows_o, :], ob[rows_o, 0:P], rden[rows_o, :], ALU.mult).then_inc(on_ready, 1)
                        elif wide and (not isinstance(V, int) or 0 <= V < UNITS):
                            uu = (k - 2) % NU
                            dve.wait_ge(o_psum, sl + V + 1)
                            e = OB
                            o = O_BANK[:, 0:UH * e].rearrange("p (h e) -> p h e", h=UH)
                            c.link(v.reciprocal(rsum[uu % 2][:, :], o[:, :, e - 1]))
                            dst = ON[uu % 2].rearrange("p (h e) -> p h e", h=UH)
                            tt(dst, o[:, :, 0:e - 1], spread(rsum[uu % 2][:, :].rearrange("p (h o) -> p h o", o=1), 2, e - 1),
                               ALU.mult).then_inc(on_ready, 1)
                        if k < 4:
                            if not isinstance(it, int) or it + 1 < NB // 2:
                                norm(it + 1, k)

                links = 2 * NU * (1 + (1 if L.mask else 0)) + 2 * (NU if wide else 2) + LN_LINKS
                norm(0)
                steps(0)
                c.enter(0, links)
                with dve.Fori(1, NB // 2 - 1) as it:
                    c.resume(it - 1)
                    steps(it)
                c.leave(NB // 2 - 2)
                steps(NB // 2 - 1)
                steps(NB // 2)

            def norm_all(n):
                dve.wait_ge(stats_ready, NB * (n + 1))
                for t in range(NB):
                    ins = v.bn_aggr(all_mv[:, t, :], all_stats[:, t, :])
                    if t < NB - 1:
                        ins.then_inc(dve_step, 1)
                        c.n += 1
                    else:
                        c.link(ins)
                c.link(ts(all_ve[:, :], all_mv[:, :, 1], EPS, None, ALU.add))
                c.link(ts(all_r[:, :].bitcast(I32), all_ve[:, :].bitcast(I32), -0.5, RSQRT_MAGIC, ALU.mult, ALU.add))
                for _ in range(3):
                    c.link(stt(all_t[:, :], all_r[:, :], -0.5, all_r[:, :], ALU.mult, ALU.mult))
                    c.link(tt(all_t[:, :], all_t[:, :], all_ve[:, :], ALU.mult))
                    c.link(stt(all_r[:, :], all_t[:, :], 1.5, all_r[:, :], ALU.add, ALU.mult))
                for t in range(NB):
                    ts(XN[:, t * D:(t + 1) * D], X[:, t * D:(t + 1) * D], all_mv[:, t, 0:1], all_r[:, t:t + 1],
                       ALU.subtract, ALU.mult).then_inc(xn_kept, 1)

            def route(R, at):
                n = R.n
                norm_all(at)
                dve.wait_ge(const_done, 1)
                dve.wait_ge(logits_psum, n + 1)
                score, work, pick1, pick2, both, pos, tot, cum, cum2 = (rt[k] for k in "score work pick1 pick2 both pos tot cum cum2".split())
                X_ = R.experts

                def rows(t):
                    return spread(t[:, :].rearrange("p (t o) -> p t o", o=1), 2, E)

                def per_expert(t):
                    return spread(t[:, :].rearrange("p (o e) -> p o e", o=1), 1, NB)
                lg = TR_BANK[:, 0:NB * E].rearrange("p (t e) -> p t e", e=E)
                if n == 0:
                    c.link(tt(score[:, :, :], lg, per_expert(br_rows), ALU.add))
                else:
                    c.link(v.tensor_copy(score[:, :, :], lg))
                if X_ < E:
                    c.link(v.memset(score[:, :, X_:E], BELOW_ALL))
                if n != 1:
                    c.link(v.tensor_reduce(rc["best1"][:, :], score[:, :, :], AX.X, ALU.max))
                    tt(work[:, :, :], score[:, :, :], rows(rc["best1"]), ALU.subtract).then_inc(exps_in, 1)
                    dve.wait_ge(exps_out, n + 1)
                    c.link(v.tensor_reduce(rc["sum"][:, :], score[:, :, :], AX.X, ALU.add))
                    c.link(v.reciprocal(rc["inv"][:, :], rc["sum"][:, :]))
                    c.link(tt(score[:, :, :], score[:, :, :], rows(rc["inv"]), ALU.mult))
                    if X_ < E:
                        c.link(v.memset(score[:, :, X_:E], -1.0))

                def pick(src, best, first, out_):
                    c.link(v.tensor_reduce(best[:, :], src[:, :, :], AX.X, ALU.max))
                    c.link(tt(work[:, :, :], src[:, :, :], rows(best), ALU.is_equal))
                    c.link(tt(work[:, :, :], work[:, :, :], desc8[:, :, :], ALU.mult))
                    c.link(v.tensor_reduce(first[:, :], work[:, :, :], AX.X, ALU.max))
                    c.link(tt(out_[:, :, :], desc8[:, :, :], rows(first), ALU.is_equal))
                pick(score, rc["best1"], rc["first1"], pick1)
                if R.k == 2:
                    c.link(stt(cum[:, :, :], pick1[:, :, :], BELOW_ALL, score[:, :, :], ALU.mult, ALU.add))
                    pick(cum, rc["best2"], rc["first2"], pick2)
                    tt(both[:, :, :], pick1[:, :, :], pick2[:, :, :], ALU.add).then_inc(picked, 1)
                else:
                    v.tensor_copy(both[:, :, :], pick1[:, :, :]).then_inc(picked, 1)
                if n == 1:
                    tt(rc["diff"][:, :], rc["best2"][:, :], rc["best1"][:, :], ALU.subtract).then_inc(exps_in, 1)
                    dve.wait_ge(exps_out, n + 1)
                    c.link(ts(rc["sum"][:, :], rc["gate2"][:, :], 1.0, None, ALU.add))
                    c.link(v.reciprocal(rc["gate1"][:, :], rc["sum"][:, :]))
                    c.link(tt(rc["gate2"][:, :], rc["gate2"][:, :], rc["gate1"][:, :], ALU.mult))
                dve.wait_ge(ranked, n + 1)
                c.link(v.tensor_copy(tot[:, :, :], bank[5][:, 0:NB * E].rearrange("p (t e) -> p t e", e=E)))
                src, dst = tot, cum
                for sh in (1, 2, 4, 8):
                    c.link(v.tensor_copy(dst[:, 0:sh, :], src[:, 0:sh, :]))
                    c.link(tt(dst[:, sh:NB, :], src[:, sh:NB, :], src[:, 0:NB - sh, :], ALU.add))
                    src, dst = dst, (cum2 if dst is cum else cum)
                total = src
                c.link(tt(pos[:, :, :], bank[4][:, 0:NB * E].rearrange("p (t e) -> p t e", e=E), total[:, :, :], ALU.add))
                c.link(tt(pos[:, :, :], pos[:, :, :], tot[:, :, :], ALU.subtract))
                if n > 0:
                    ecm = ecmp[:, :].rearrange("p (e j) -> p e j", e=E)
                    c.link(tt(ecm, spread(total[:, NB - 1, :].rearrange("p (e o) -> p e o", o=1), 2, NB), steps128[:, :, :], ALU.is_gt))
                    c.link(v.tensor_reduce(ec["tiles"][:, :], ecm, AX.X, ALU.add))
                    s_, d_ = ec["tiles"], ec["end"]
                    for sh in (1, 2, 4):
                        c.link(v.tensor_copy(d_[:, 0:sh], s_[:, 0:sh]))
                        c.link(tt(d_[:, sh:E], s_[:, sh:E], s_[:, 0:E - sh], ALU.add))
                        s_, d_ = d_, (ec["end2"] if d_ is ec["end"] else ec["end"])
                    end = s_
                    c.link(tt(ec["start"][:, :], end[:, :], ec["tiles"][:, :], ALU.subtract))
                    c.link(ts(ec["start"][:, :], ec["start"][:, :], float(P), None, ALU.mult))
                    c.link(tt(pos[:, :, :], pos[:, :, :], per_expert(ec["start"]), ALU.add))
                    tc_ = tcmp[:, 0:TILES2 * E].rearrange("p (t e) -> p t e", e=E)
                    c.link(tt(tc_, tileno[:, :, :], spread(end[:, :].rearrange("p (o e) -> p o e", o=1), 1, TILES2), ALU.is_ge))
                    c.link(v.tensor_reduce(texp[:, :], tc_, AX.X, ALU.add))
                    c.link(ts(texp[:, :], texp[:, :], float(X_ - 1), None, ALU.min))
                    c.link(v.tensor_copy(texp_i[:, :], texp[:, :]))
                for k, (pk, first, best) in enumerate(((pick1, "first1", "best1"), (pick2, "first2", "best2"))[:R.k]):
                    place, keep = rc[f"place{k + 1}"], rc[f"keep{k + 1}"]
                    c.link(tt(work[:, :, :], pk[:, :, :], pos[:, :, :], ALU.mult))
                    c.link(v.tensor_reduce(place[:, :], work[:, :, :], AX.X, ALU.add))
                    if n == 0:
                        c.link(ts(keep[:, :], place[:, :], float(CAP), None, ALU.is_lt))
                        c.link(ts(place[:, :], place[:, :], float(CAP - 1), None, ALU.min))
                        c.link(stt(place[:, :], rc[first][:, :], -float(CAP), place[:, :], ALU.mult, ALU.add))
                        c.link(ts(place[:, :], place[:, :], float(E * CAP), None, ALU.add))
                        c.link(v.tensor_copy(from_row[k][:, :], place[:, :]))
                        c.link(tt(place[:, :], place[:, :], trash[:, k, :], ALU.subtract))
                        c.link(tt(place[:, :], place[:, :], keep[:, :], ALU.mult))
                        c.link(tt(place[:, :], place[:, :], trash[:, k, :], ALU.add))
                        c.link(v.tensor_copy(to_row[k][:, :], place[:, :]))
                        c.link(tt(rc[f"gate{k + 1}"][:, :], rc[best][:, :], keep[:, :], ALU.mult))
                    else:
                        c.link(v.tensor_copy(from_row[k][:, :], place[:, :]))
                        c.link(v.tensor_copy(to_row[k][:, :], place[:, :]))
                if n == 0:
                    c.link(tt(rc["sum"][:, :], rc["gate1"][:, :], rc["gate2"][:, :], ALU.add))
                    c.link(ts(rc["sum"][:, :], rc["sum"][:, :], 1e-6, None, ALU.max))
                    c.link(v.reciprocal(rc["inv"][:, :], rc["sum"][:, :]))
                    for g_ in ("gate1", "gate2"):
                        c.link(tt(rc[g_][:, :], rc[g_][:, :], rc["inv"][:, :], ALU.mult))
                v.tensor_copy(texp[:, 0:1], place[:, 0:1]).then_inc(routed, 1)

            def combine_pair(R, it):
                for j in range(4):
                    b, k = 2 * it + j // 2, j % 2
                    dve.wait_ge(gathered[j], 16 * (COMBINE0[R.n] // 4 + it + 1))
                    xb = X[:, ds(b * D, D)]
                    stt(xb, got[j][:, :], rc[f"gate{k + 1}"][:, ds(b, 1)], xb, ALU.mult, ALU.add).then_inc(combined, 1)
                    dve.wait_ge(combined, COMBINE0[R.n] + 4 * it + j + 1)

            def combine_last():
                for t in range(NB):
                    s = t % 4
                    dve.wait_ge(gathered[s], 16 * ((COMBINE0[2] + t) // 4 + 1))
                    xb = X[:, t * D:(t + 1) * D]
                    tt(xb, got[s][:, :], xb, ALU.add).then_inc(combined, 1)

            def dve_shared(S):
                def multiply(g):
                    for f in range(S.nf):
                        p = S.nf * g + f
                        dve.wait_ge(sh_gated, S.gates0 + p + 1)
                        dve.wait_ge(sh_psum, S.products0 + 2 * p + 2)
                        if g >= 2 and f == 0:
                            dve.wait_ge(so_psum, S.groups0 + g - 1)
                        tt(shT[g % 2][:, f, :], bank[2 * (p % 2) + 1][:, :], sh_gate[p % 2], ALU.mult).then_inc(sh_ready, 1)

                def add(g):
                    dve.wait_ge(so_psum, S.groups0 + g + 1)
                    for t in range(4):
                        xb = X[:, (4 * g + t) * D:(4 * g + t + 1) * D]
                        tt(xb, xb, bank[6 + g % 2][:, t * D:(t + 1) * D], ALU.add).then_inc(shared_done, 1)
                if S.gate:
                    multiply(0)
                for g in range(4):
                    if S.gate and g < 3:
                        multiply(g + 1)
                    add(g)

            def dve_mlp(r):
                w, nj = r.width, r.width // P
                h_bank = [[bank[0], bank[1]], [bank[2], bank[3]]]
                t_bank = [bank[4], bank[5]]

                def multiply(it, s):
                    i = 2 * it + s
                    dve.wait_ge(g_ready, r.gates0 + i + 1)
                    if not isinstance(it, int) or it > 0:
                        dve.wait_ge(hT_psum, r.at + i - 1)
                    tt(hid[s][:, 0:w], h_bank[s][0][:, 0:w], gate[s][:, 0:w], ALU.mult).then_inc(h_ready, 1)

                def turned(it, s):
                    i = 2 * it + s
                    dve.wait_ge(hT_psum, r.at + i + 1)
                    if not isinstance(it, int) or it > 0:
                        dve.wait_ge(m2_psum, r.at + i - 1)
                    v.tensor_copy(hidT[s][:, 0:nj, :], t_bank[s][:, 0:w].rearrange("p (j t) -> p j t", j=nj)).then_inc(hT_ready, 1)

                def finish(it, s):
                    i = 2 * it + s
                    dve.wait_ge(m2_psum, r.at + i + 1)
                    if not isinstance(it, int) or it > 0:
                        dve.wait_ge(stored[s], r.stored0 + 16 * it)
                    v.tensor_copy(row_out[s][:, :], Y_BANK[:, 0:D]).then_inc(m2_done, 1)

                def steps(it):
                    for s in range(2):
                        i = 2 * it + s
                        if not isinstance(i, int) or 1 <= i <= r.tiles:
                            turned(*((it - 1, 1) if s == 0 else (it, 0)))
                        if r.gated and (not isinstance(i, int) or i < r.tiles):
                            multiply(it, s)
                        if not isinstance(i, int) or 2 <= i <= r.tiles + 1:
                            finish(it - 1, s)
                steps(0)
                with dve.Fori(1, r.tiles // 2) as it:
                    steps(it)
                steps(r.tiles // 2)

            for s in range(2):
                v.memset(vw[s][:, :, 64:65], 1.0).then_inc(dve_prepared if s else dve_step, 1)
            c.n += 1
            dve.wait_ge(loaded["rowsof"], 16 * 5)
            dve.wait_ge(loaded["x"], 16)
            dve_attention(ATT[0])
            if last_layer >= 2:
                route(RT[0], 0)

                def finish0(it, s):
                    e = 2 * it + s
                    dve.wait_ge(o0_psum, e + 1)
                    if not isinstance(it, int) or it > 0:
                        dve.wait_ge(stored[s], 32 * it)
                    b2 = b2_rows[:, ds(e * D, D)].rearrange("p (o d) -> p o d", o=1)
                    c.link(tt(o0[s][:, 0:2, :], bank[4 + s][:, 0:256].rearrange("p (r d) -> p r d", r=2), spread(b2, 1, 2), ALU.add))
                    n = CAP - 2 * P
                    tt(o0[s][0:n, 2, :], bank[4 + s][0:n, 256:384], b2_rows[0:n, ds(e * D, D)], ALU.add).then_inc(o0_ready, 1)
                dve.wait_ge(loaded["b2"], 16)
                finish0(0, 0)
                finish0(0, 1)
                c.enter(0, 2)
                with dve.Fori(1, E // 2) as it:
                    c.resume(it - 1)
                    finish0(it, 0)
                    finish0(it, 1)
                c.leave(E // 2 - 1)
            if last_layer >= 3:
                dve_attention(ATT[1])
            if last_layer >= 4:
                norm_all(1)
                dve.wait_ge(loaded["mlp1"], 48)
                c.link(v.tensor_copy(w1n, w1n.bitcast(I32)))
                ts(w1n, w1n, 1.0 / 127.0, None, ALU.mult).then_inc(dve_prepared, 1)
                dve_shared(SH1)
            if last_layer >= 5:
                blank()
                c.link(ts(notmask, mask8[:, :], -1.0, FLT_MAX, ALU.add, ALU.mult))
                dve_attention(ATT[2])
            if last_layer >= 6:
                route(RT[1], 2)
                dve_shared(SH2)
                dve_mlp(RO2)
            if last_layer >= 7:
                blank()
                dve_attention(ATT[3])
            if last_layer >= 8:
                route(RT[2], 3)
                dve_shared(SH3)
                dve_mlp(RO3)
                combine_last()


_INS = ['x', 'ctx_768', 'mask_BxS2_bf1', 'L0_xattn_Wq', 'L0_xattn_Wkv', 'L0_xattn_Wproj', 'L0_xattn_bproj',
        'L0_ffn_w_router', 'L0_ffn_b_router', 'L0_ffn_w1', 'L0_ffn_b1', 'L0_ffn_w2', 'L0_ffn_b2',
        'L1_xattn_Wq', 'L1_xattn_Wk', 'L1_xattn_Wv', 'L1_xattn_Wo', 'L1_xattn_bo',
        'L1_ffn_w_gate', 'L1_ffn_w_up', 'L1_ffn_w_down',
        'L2_xattn_Wq', 'L2_xattn_bq', 'L2_xattn_Wkv', 'L2_xattn_bkv', 'L2_xattn_Wo', 'L2_xattn_bo',
        'L2_ffn_shared_w1', 'L2_ffn_shared_w2', 'L2_ffn_experts_w1', 'L2_ffn_experts_w2', 'L2_ffn_gate_w',
        'L3_xattn_Wq', 'L3_xattn_Wk', 'L3_xattn_Wv', 'L3_xattn_Wo', 'L3_ffn_Wg_DN', 'L3_ffn_Wl1_ND2H', 'L3_ffn_Wl2_NHD']


def kernel(**inputs):
    import numpy as _np
    import concourse.bacc as _bacc
    from concourse import mybir as _mybir
    from concourse.bass_utils import run_bass_kernel_spmd as _run

    nc = _bacc.Bacc("TRN2", target_bir_lowering=False, num_devices=1)
    arrays, args = {}, {}
    for name in _INS:
        a = _np.ascontiguousarray(inputs[name])
        if a.dtype == bool:
            a = a.view(_np.uint8)
        arrays[f"in_{name}_dram"] = a
        args[name] = nc.dram_tensor(f"in_{name}_dram", a.shape, _mybir.dt.from_np(a.dtype), kind="ExternalInput").ap()
    out = nc.dram_tensor("out_0_dram", (NB, P, D), F32, kind="ExternalOutput").ap()
    build(nc, args, out, LAST)
    r = _run(nc, [arrays], core_ids=[0])
    return r.results[0]["out_0_dram"]
```

```python
import concourse.bass as bass
from concourse import mybir
from contextlib import ExitStack

F32 = mybir.dt.float32
I32 = mybir.dt.int32
U32 = mybir.dt.uint32
U8 = mybir.dt.uint8
ACT = mybir.ActivationFunctionType
ALU = mybir.AluOpType
AX = mybir.AxisListType
ds = bass.ds

P = 128
NB = 16
D = 128
NK = 77
C = 96
H = 16
UH = 4
NU = H // UH
UNITS = NB * NU
UW = UH * NK
KW = H * NK
E = 8
NT = NB * P
EPS = 1e-5
RSQRT_MAGIC = 1597463007.0
BELOW_ALL = -3.0e38
MASKED = 1e30

CAP = int(1.25 * NT / E)
CAP_ROWS = E * CAP
TILES2 = (2 * NT + E * (P - 1)) // P
TILES2 += -TILES2 % 4
TILES3 = (NT + (E - 1) * (P - 1)) // P
TILES3 += TILES3 % 2
F1 = 384
F2 = 512
F3 = 256
T_CHUNKS = ((0, 6), (6, 11), (11, 16))
OB = 65


def spread(ap, dim, n):
    shape = list(ap.shape)
    assert shape[dim] == 1
    shape[dim] = n
    return ap.broadcast_to(shape)


class Attention:
    def __init__(self, n, wide, scale, bias, mask, wide_n=None, nar_n=None):
        self.n, self.unit0, self.batch0 = n, n * UNITS, n * NB
        self.wide, self.scale, self.bias, self.mask = wide, scale, bias, mask
        self.wide_n, self.nar_n = wide_n, nar_n
        self.x_out = None
        self.oT0 = self.v0 = self.q0 = self.c0 = self.b0 = 0


class Routing:
    def __init__(self, n, k, experts, rows, outs, total):
        self.n, self.k, self.experts = n, k, experts
        self.rows, self.outs, self.total = rows, outs, total
        self.tiles = total // P
        self.scatter0 = 0


class MlpRun:
    def __init__(self, tiles, width, gated, w1, w2, R):
        self.tiles, self.width, self.gated = tiles, width, gated
        self.w1, self.w2, self.R = w1, w2, R
        self.at = self.gates0 = self.rows0 = self.stored0 = 0


class SharedMlp:
    def __init__(self, nf, w1, gate, w2):
        self.nf, self.w1, self.gate, self.w2 = nf, w1, gate, w2
        self.products0 = self.gates0 = self.parts0 = self.groups0 = 0


class Chain:

    def __init__(self, eng, sem):
        self.eng, self.sem, self.base, self.n = eng, sem, 0, 0

    def link(self, ins):
        ins.then_inc(self.sem, 1)
        self.n += 1
        self.eng.wait_ge(self.sem, self.base + self.n)

    def enter(self, it, steps):
        self.before, self.steps = self.base + self.n, steps
        self.resume(it)

    def resume(self, it):
        self.base, self.n = self.before + it * self.steps, 0

    def leave(self, count):
        assert self.n == self.steps, (self.n, self.steps)
        self.base, self.n = self.before + count * self.steps, 0


class Turns:

    def __init__(self, eng, filled, emptied, banks):
        self.eng, self.filled, self.emptied, self.banks, self.n = eng, filled, emptied, banks, 0

    def bank(self):
        return self.banks[self.n % len(self.banks)]

    def claim(self):
        if self.n >= len(self.banks):
            self.eng.wait_ge(self.emptied, self.n - len(self.banks) + 1)
        return self.bank()

    def fill(self, ins):
        ins.then_inc(self.filled, 1)
        self.n += 1

    def take(self):
        self.eng.wait_ge(self.filled, self.n + 1)
        return self.bank()

    def empty(self, ins):
        ins.then_inc(self.emptied, 1)
        self.n += 1

    def settle(self):
        self.eng.wait_ge(self.emptied, self.n)


def build(nc, A, out):
    ctx = ExitStack()
    with ctx:
        def sb(name, shape, dt=F32):
            return ctx.enter_context(nc.sbuf_tensor(name, shape, dt))

        def sem(name):
            return ctx.enter_context(nc.semaphore(name))

        bank = [ctx.enter_context(nc.psum_tensor(f"bank{i}", [P, 512], F32)) for i in range(8)]
        S_BANK, PT_BANK = bank[0:2], bank[2:4]
        O_BANK, V_BANK, TR_BANK, Y_BANK = bank[4], bank[5], bank[6], bank[7]
        ON_BANK = bank[4:6]

        ident = sb("ident", [P, P])
        earlier = sb("earlier", [P, P])
        ones = sb("ones", [P, P])
        headmask = sb("headmask", [P, H])
        desc8 = sb("desc8", [P, NB, E])
        tileno = sb("tileno", [P, TILES2, E])
        steps128 = sb("steps128", [P, E, NB])
        trash = sb("trash", [P, 2, NB])
        X = sb("X", [P, NT])
        XN = sb("XN", [P, NT])
        CT = sb("CT", [C + 1, KW])
        R1 = sb("R1", [P, NB * KW])
        RP = sb("RP", [P, 3840])
        RV = sb("RV", [P, 2 * H * OB])
        RM = sb("RM", [P, H * D])
        RA = sb("RA", [P, 3296])
        RH = sb("RH", [P, 3072])
        RW = sb("RW", [P, 2304])
        wv = sb("wv", [C, H * 64])
        wo = sb("wo", [P, 8, D])
        nwq = [sb(f"nwq{i}", [P, D]) for i in range(2)]
        nwk = [sb(f"nwk{i}", [C + 1, D]) for i in range(2)]
        nwv = [sb(f"nwv{i}", [C + 1, D]) for i in range(2)]
        nwo = [sb(f"nwo{i}", [P, D]) for i in range(2)]
        bq2 = sb("bq2", [P, 1])
        bo_rows = [sb(f"bo_rows{i}", [P, D]) for i in range(3)]
        wr = [sb(f"wr{i}", [P, E]) for i in range(3)]
        br_rows = sb("br_rows", [P, E])
        b1c = sb("b1c", [P, E * 4])
        mask8 = sb("mask8", [P, KW], U8)
        qT = [sb(f"qT{i}", [P, P]) for i in range(2)]
        mxT = [sb(f"mxT{i}", [P, P]) for i in range(2)]
        ln_stats = sb("ln_stats", [P, 2, 6])
        ln_mv = sb("ln_mv", [P, 2, 2])
        ln_ve = sb("ln_ve", [P, 2])
        ln_r = sb("ln_r", [P, 2])
        ln_t = sb("ln_t", [P, 2])
        all_stats = sb("all_stats", [P, NB, 6])
        carry = sb("carry", [P, 1])
        all_mv = sb("all_mv", [P, NB, 2])
        all_ve, all_r, all_t = sb("all_ve", [P, NB]), sb("all_r", [P, NB]), sb("all_t", [P, NB])
        xn = [sb(f"xn{i}", [P, D]) for i in range(2)]
        xnT = [sb(f"xnT{i}", [P, P]) for i in range(2)]
        cts = [sb(f"cts{i}", [C, NK]) for i in range(2)]
        mx = [sb(f"mx{i}", [P, UH]) for i in range(2)]
        rsum = [sb(f"rsum{i}", [P, UH]) for i in range(2)]
        rt = {n: sb(f"rt_{n}", [P, NB, E]) for n in
              "score work pick1 pick2 both pos tot cum cum2".split()}
        rc = {n: sb(f"rc_{n}", [P, NB]) for n in
              "best1 best2 first1 first2 place1 place2 keep1 keep2 gate1 gate2 sum inv diff".split()}
        to_row = [sb(f"to_row{k}", [P, NB], U32) for k in range(2)]
        from_row = [sb(f"from_row{k}", [P, NB], U32) for k in range(2)]
        ec = {n: sb(f"ec_{n}", [P, E]) for n in "count tiles end end2 start".split()}
        ecmp = sb("ecmp", [P, E * NB])
        tcmp = sb("tcmp", [P, TILES2 * E])
        texp = sb("texp", [P, TILES2])
        texp_i = sb("texp_i", [P, TILES2], I32)
        got = [sb(f"got{i}", [P, D]) for i in range(4)]

        T_all = R1
        wq_nat = RP[:, 0:1024]
        wk_nat = RP[0:C, 1024:2048]
        wqT = RP[:, 2048:3072].rearrange("p (j d) -> p j d", j=8)
        wkT = RP[:, 3072:3840].rearrange("p (j c) -> p j c", j=8)
        bufT = RP[:, 0:CAP_ROWS]
        kbd = [RP[:, i * KW:(i + 1) * KW] for i in range(2)]
        vw = [RV[0:NK, i * H * OB:(i + 1) * H * OB].rearrange("k (h e) -> k h e", h=H) for i in range(2)]
        v_narrow = RV[0:NK, 0:NB * D]
        MT = RM[0:C, :].rearrange("c (h d) -> c h d", h=H)
        kT_all = RM[:, 0:KW]
        ctx_nat = R1[0:NK, 0:NB * C].rearrange("k (b c) -> k b c", b=NB)

        def ra(at, n):
            return RA[:, at:at + n]
        Z = [ra(i * UW, UW) for i in range(2)]
        PR = [ra(2 * UW + i * UW, UW) for i in range(2)]
        PT = [RA[0:NK, 4 * UW + i * 512:4 * UW + (i + 1) * 512].rearrange("k (h q) -> k h q", h=UH) for i in range(2)]
        ON = [ra(4 * UW + 1024 + i * 256, 256) for i in range(2)]
        OT = [ra(4 * UW + 1536 + i * 256, 256).rearrange("p (j q) -> p j q", j=2) for i in range(2)]
        OTn = [ra(4 * UW + 1024 + i * P, P) for i in range(2)]
        rden = ra(4 * UW + 1280, P)
        rows0 = RA[:, 0:CAP_ROWS].rearrange("p (t d) -> p t d", d=D)

        w1s = [RW[:, i * 512:(i + 1) * 512] for i in range(2)]
        w2s = [RW[:, 1024 + i * 512:1024 + (i + 1) * 512].rearrange("p (f d) -> p f d", f=4) for i in range(2)]
        hT0 = [RH[:, i * 1280:(i + 1) * 1280].rearrange("p (f t) -> p f t", f=4) for i in range(2)]
        o0 = [RA[:, i * 384:(i + 1) * 384].rearrange("p (r d) -> p r d", r=3) for i in range(2)]
        b2_rows = RA[:, 768:768 + E * D]
        w1n = RW[:, 0:1152]
        wg1, wu1 = RW[:, 1152:1152 + F1], RW[:, 1152 + F1:1152 + 2 * F1]
        wd1 = RW[:, 1920:2304].rearrange("p (j d) -> p j d", j=3)
        notmask = RW[:, 0:KW]
        q_last = mxT
        LAST_UNIT = (NU - 1) * UW
        hid = [RH[:, i * 512:(i + 1) * 512] for i in range(2)]
        gate = [RH[:, 1024 + i * 384:1024 + (i + 1) * 384] for i in range(2)]
        hidT = [RH[:, 1792 + i * 512:1792 + (i + 1) * 512].rearrange("p (j t) -> p j t", j=4) for i in range(2)]
        vbd = [R[0:NK, at:at + 16 * 136] for R, at in ((RH, 0), (R1, 34 * 512))]
        vbd_steps = [v_.rearrange("k (h x) -> k h x", x=136) for v_ in vbd]
        row_in = [sb(f"row_in{i}", [P, D]) for i in range(2)] + [RV[:, i * D:(i + 1) * D] for i in range(2)]
        row_out = [sb(f"row_out{i}", [P, D]) for i in range(2)]
        xnT_all = RA[:, 0:NT]
        shT = [R[:, 0:2048].rearrange("p (f t) -> p f t", f=4) for R in (RP, RH)]
        sh_gate = [RH[:, 2048 + i * 512:2048 + (i + 1) * 512] for i in range(2)]
        w1_2 = R1[:, 0:9 * 512]
        w2_2 = R1[:, 9 * 512:18 * 512]
        nat2 = [R1[:, (18 + i) * 512:(19 + i) * 512] for i in range(4)]
        w1_3 = R1[:, 22 * 512:30 * 512]
        w2_3 = R1[:, 30 * 512:34 * 512]

        rows_d = [nc.dram_tensor(f"rows{i}", [n + (2 * NT if i == 0 else 0), D], F32, kind="Internal")
                  for i, n in enumerate((CAP_ROWS, TILES2 * P, TILES3 * P))]
        outs_d = [nc.dram_tensor(f"outs{i}", [n, D], F32, kind="Internal")
                  for i, n in enumerate((CAP_ROWS, TILES2 * P, TILES3 * P))]
        zero_tile = sb("zero_tile", [P, D])

        const_step = sem("const_step")
        const_done, ident_ready = sem("const_done"), sem("ident_ready")
        loaded = {}

        def arrives(name):
            loaded[name] = sem("loaded_" + name)
            return loaded[name]
        for n in ("x ctx wqk0 wvo0 wqk1 wvo1 narrow2 narrow3 rowsof misc b2 mlp1 mlp3").split():
            arrives(n)
        zeroed, xn_kept = sem("zeroed"), sem("xn_kept")
        filled, emptied = sem("stage_filled"), sem("stage_emptied")
        dve_step = sem("dve_step")
        dve_prepared, weights_float = sem("dve_prepared"), sem("weights_float")
        xn_ready, xnT_psum, xnT_ready = sem("xn_ready"), sem("xnT_psum"), sem("xnT_ready")
        q_psum, q_ready = sem("q_psum"), sem("q_ready")
        cts_ready, kbd_ready, bias_added = sem("cts_ready"), sem("kbd_ready"), sem("bias_added")
        vbd_ready = sem("vbd_ready")
        last_spread = sem("last_spread")
        notmask_ready, mask_loaded = sem("notmask_ready"), [sem(f"mask_loaded{i}") for i in range(2)]
        v_psum, v_ready = sem("v_psum"), sem("v_ready")
        s_psum, z_ready, p_ready = sem("s_psum"), sem("z_ready"), sem("p_ready")
        pT_psum, pT_ready = sem("pT_psum"), sem("pT_ready")
        o_psum, on_ready = sem("o_psum"), sem("on_ready")
        oT_psum, oT_ready, y_psum = sem("oT_psum"), sem("oT_ready"), sem("y_psum")
        x_done = [sem(f"x_done{i}") for i in range(4)]
        stats_ready, vbd_blank = sem("stats_ready"), sem("vbd_blank")
        logits_psum = sem("logits_psum")
        exps_in, exps_out = sem("exps_in"), sem("exps_out")
        picked, ranked = sem("picked"), sem("ranked")
        routed = sem("routed")
        scattered = sem("scattered")
        rows_loaded = [sem(f"rows_loaded{i}") for i in range(4)]
        gathered = [sem(f"gathered{i}") for i in range(4)]
        combined = sem("combined")
        stored = [sem(f"stored{i}") for i in range(2)]
        w1_loaded = [sem(f"w1_loaded{i}") for i in range(2)]
        w2_loaded = [sem(f"w2_loaded{i}") for i in range(2)]
        h0_psum, h0_ready, o0_psum, o0_ready = sem("h0_psum"), sem("h0_ready"), sem("o0_psum"), sem("o0_ready")
        sh_psum, sh_gated, sh_ready, so_psum, shared_done = (sem(n) for n in
                                                             "sh_psum sh_gated sh_ready so_psum shared_done".split())
        mT_psum, mT_ready = sem("mT_psum"), sem("mT_ready")
        m1_psum, g_ready, h_ready = sem("m1_psum"), sem("g_ready"), sem("h_ready")
        hT_psum, hT_ready, m2_psum, m2_done = sem("hT_psum"), sem("hT_ready"), sem("m2_psum"), sem("m2_done")
        nat_loaded = [sem(f"nat_loaded{i}") for i in range(4)]
        written = sem("written")

        def attention(n, **k):
            return Attention(n, **k)
        ATT = [attention(0, wide=True, scale=64 ** -0.5, bias=0, mask=False, wide_n=0),
               attention(1, wide=True, scale=64 ** -0.5, bias=1, mask=False, wide_n=1),
               attention(2, wide=False, scale=8 ** -0.5, bias=2, mask=False, nar_n=0),
               attention(3, wide=False, scale=8 ** -0.5, bias=None, mask=True, nar_n=1)]
        for L in ATT:
            L.x_out = x_done[L.n]
            L.oT0 = sum(UNITS if K.wide else 0 for K in ATT[:L.n])
            L.on0 = sum(UNITS if K.wide else 2 * NB for K in ATT[:L.n])
            L.v0 = sum(2 * NB if K.wide else 0 for K in ATT[:L.n])
            L.q0 = sum(0 if K.wide else NB for K in ATT[:L.n])
            L.c0 = sum(NB if K.wide else 0 for K in ATT[:L.n])
            L.b0 = sum(NB if K.bias is not None else 0 for K in ATT[:L.n])
        RT = [Routing(n=0, k=2, experts=8, rows=rows_d[0], outs=outs_d[0], total=CAP_ROWS),
              Routing(n=1, k=2, experts=8, rows=rows_d[1], outs=outs_d[1], total=TILES2 * P),
              Routing(n=2, k=1, experts=7, rows=rows_d[2], outs=outs_d[2], total=TILES3 * P)]
        for R in RT:
            R.tiles = R.total // P
            R.scatter0 = sum(16 * NB * K.k for K in RT[:R.n])
        def parts(w, f0):
            return lambda f: w[:, f0 + f * P:f0 + (f + 1) * P]
        SH1 = SharedMlp(3, parts(wu1, 0), parts(wg1, 0), lambda f: wd1[:, f, :])
        SH2 = SharedMlp(4, parts(w1_2, 8 * 512), None, parts(w2_2, 8 * 512))
        SH3 = SharedMlp(2, parts(w1_3, 7 * 512), parts(w1_3, 7 * 512 + F3), parts(w2_3, 7 * F3))
        products = gates = parts_n = 0
        for n, S in enumerate((SH1, SH2, SH3)):
            S.products0, S.gates0, S.parts0, S.groups0 = products, gates, parts_n, 4 * n
            products += 4 * S.nf * (2 if S.gate else 1)
            gates += 4 * S.nf if S.gate else 0
            parts_n += 4 * S.nf
        RO2 = MlpRun(TILES2, F2, False, w1_2, w2_2, RT[1])
        RO3 = MlpRun(TILES3, F3, True, w1_3, w2_3, RT[2])
        RO3.at = TILES2
        RO2.rows0, RO2.stored0 = (1, 1, 1, 0), 32 * (E // 2)
        RO3.rows0, RO3.stored0 = [n + TILES2 // 4 for n in RO2.rows0], 32 * (E // 2) + 16 * (TILES2 // 2)
        ROW_PIECES = ((0, 4), (4, 12), (12, RT[0].tiles))
        STORED_END = [RO2.stored0, RO3.stored0, RO3.stored0 + 16 * (TILES3 // 2)]
        COMBINE0 = [0, 2 * NB, 4 * NB]

        def x_ready(layer, n):
            if layer % 2 == 0:
                return x_done[layer // 2], n
            if layer == 3:
                return shared_done, n
            return combined, COMBINE0[layer // 3 if layer < 7 else 2] + n * (1 if layer == 7 else 2)

        NAT_FIRST = 8
        STAGE_END, filled_n = {}, 0
        for name, n in (("ct", 4), ("m0", 8), ("t0", 48), ("small", 2), ("m1", 8), ("xn0", 4),
                        ("narrow2", 4), ("t1", 48), ("rows", CAP_ROWS // 512), ("mlp1", 3), ("xn1", 4),
                        ("kv2", 7), ("nat2", NAT_FIRST), ("xn2", 4), ("nat2_rest", 18 - NAT_FIRST), ("kv3", 7), ("xn3", 4)):
            filled_n += n
            STAGE_END[name] = filled_n

        block = ctx.enter_context(nc.Block())

        def bcast(src, n):
            return bass.AP(src.tensor, src.offset, [[0, P], [1, n]])

        @block.sync
        def _(sp):
            def load(dst, src, name):
                sp.dma_start(dst, src).then_inc(loaded[name], 16)

            load(ctx_nat, A["ctx_768"].rearrange("b k c -> k b c"), "ctx")
            load(wk_nat, A["L0_xattn_Wkv"][:, 0:1024], "wqk0")
            sp.wait_ge(loaded["wqk0"], 32)
            load(X[:, :].rearrange("p (b d) -> p b d", b=NB), A["x"].rearrange("b s d -> s b d"), "x")
            load(wv[:, :], A["L0_xattn_Wkv"][:, 1024:2048], "wvo0")
            load(wo[:, :, :], A["L0_xattn_Wproj"].rearrange("(j p) d -> p j d", p=P), "wvo0")
            for i, name in enumerate(("L0_xattn_bproj", "L1_xattn_bo", "L2_xattn_bo")):
                load(bo_rows[i][:, :], bcast(A[name], D), "rowsof")
            load(br_rows[:, :], bcast(A["L0_ffn_b_router"], E), "rowsof")
            load(mask8[:, :], bcast(A["mask_BxS2_bf1"], KW), "rowsof")
            load(wr[0][:, :], A["L0_ffn_w_router"], "misc")
            load(wr[2][:, :], A["L3_ffn_Wg_DN"], "misc")
            load(row_in[0][0:32, :], A["L0_ffn_b1"].rearrange("e (f p) -> (e f) p", p=P), "misc")
            load(row_in[1][0:E, :], A["L2_ffn_gate_w"], "misc")
            sp.wait_ge(emptied, STAGE_END["m0"])
            load(wq_nat, A["L1_xattn_Wq"], "wqk1")
            load(wk_nat, A["L1_xattn_Wk"], "wqk1")
            load(got[0][:, :], A["L2_xattn_Wq"], "narrow2")
            load(got[1][:, :], A["L2_xattn_Wo"], "narrow2")
            load(got[2][:, 0:C], A["L2_xattn_Wkv"][0:P, :], "narrow2")
            load(got[3][:, 0:C], A["L2_xattn_Wkv"][P:2 * P, :], "narrow2")
            load(bq2[:, :], A["L2_xattn_bq"].rearrange("(p o) -> p o", o=1), "narrow2")
            bkv = A["L2_xattn_bkv"].rearrange("(o h t e) -> t o h e", o=1, t=2, e=8)
            load(nwk[0][C:C + 1, :].rearrange("o (h e) -> o h e", e=8), bkv[0], "narrow2")
            load(nwv[0][C:C + 1, :].rearrange("o (h e) -> o h e", e=8), bkv[1], "narrow2")
            load(nwq[1][:, :], A["L3_xattn_Wq"], "narrow3")
            load(nwk[1][0:C, :], A["L3_xattn_Wk"], "narrow3")
            load(nwv[1][0:C, :], A["L3_xattn_Wv"], "narrow3")
            load(nwo[1][:, :], A["L3_xattn_Wo"], "narrow3")

            sp.wait_ge(x_done[0], NB)
            load(wv[:, :], A["L1_xattn_Wv"], "wvo1")
            load(wo[:, :, :], A["L1_xattn_Wo"].rearrange("(j p) d -> p j d", p=P), "wvo1")
            def load_w1(it, s):
                e = 2 * it + s
                if not isinstance(it, int) or it > 0:
                    sp.wait_ge(h0_psum, 4 * (e - 1))
                sp.dma_start(w1s[s], A["L0_ffn_w1"].rearrange("e p f -> p e f")[:, ds(e, 1), :]
                             .rearrange("p o f -> p (o f)")).then_inc(w1_loaded[s], 16)

            def load_w2(it, s):
                e = 2 * it + s
                if not isinstance(it, int) or it > 0:
                    sp.wait_ge(o0_psum, e - 1)
                sp.dma_start(w2s[s], A["L0_ffn_w2"].rearrange("e (f p) d -> p e f d", p=P)[:, ds(e, 1), :, :]
                             .rearrange("p o f d -> p (o f) d")).then_inc(w2_loaded[s], 16)
            load_w1(0, 0)
            load_w1(0, 1)
            load_w2(0, 0)
            load_w2(0, 1)
            sp.wait_ge(zeroed, 16 * 3)
            sp.wait_ge(scattered, RT[0].scatter0 + 16 * NB * RT[0].k)
            for i, (t0, t1) in enumerate(ROW_PIECES):
                sp.dma_start(rows0[:, t0:t1, :], rows_d[0][t0 * P:t1 * P, :].rearrange("(t p) d -> p t d", p=P))\
                    .then_inc(rows_loaded[i], 16)

            sp.wait_ge(emptied, STAGE_END["rows"])
            load(b2_rows, bcast(A["L0_ffn_b2"], E * D), "b2")

            load_w1(1, 0)
            with sp.Fori(1, E // 2 - 1) as it:
                load_w2(it, 0)
                load_w1(it, 1)
                load_w2(it, 1)
                load_w1(it + 1, 0)
            load_w2(E // 2 - 1, 0)
            load_w1(E // 2 - 1, 1)
            load_w2(E // 2 - 1, 1)
            sp.wait_ge(o0_psum, E)
            load(w1n.bitcast(I32)[:, 0:384].rearrange("p (j d) -> p j d", j=3), A["L1_ffn_w_gate"].rearrange("(j p) d -> p j d", p=P), "mlp1")
            load(w1n.bitcast(I32)[:, 384:768].rearrange("p (j d) -> p j d", j=3), A["L1_ffn_w_up"].rearrange("(j p) d -> p j d", p=P), "mlp1")
            load(w1n.bitcast(I32)[:, 768:1152], A["L1_ffn_w_down"], "mlp1")
            sp.wait_ge(s_psum, 2 * UNITS)
            for n in range(18):
                if n >= 4:
                    sp.wait_ge(emptied, STAGE_END["kv2"] + n - 3 + (4 if n - 4 >= NAT_FIRST else 0))
                e, second = n // 2, n % 2
                if second:
                    src = A["L2_ffn_shared_w2"] if e == 8 else A["L2_ffn_experts_w2"][e]
                    sp.dma_start(nat2[n % 4], src).then_inc(nat_loaded[n % 4], 16)
                else:
                    src = A["L2_ffn_shared_w1"] if e == 8 else A["L2_ffn_experts_w1"][e]
                    sp.dma_start(nat2[n % 4].rearrange("p (j d) -> p j d", j=4),
                                 src.rearrange("(j p) d -> p j d", p=P)).then_inc(nat_loaded[n % 4], 16)
            load(w1_3.rearrange("p (e f) -> p e f", e=E), A["L3_ffn_Wl1_ND2H"].rearrange("e p f -> p e f"), "mlp3")
            load(w2_3.rearrange("p (e j d) -> p e j d", e=E, j=2), A["L3_ffn_Wl2_NHD"].rearrange("e (j p) d -> p e j d", p=P), "mlp3")

            def load_rows(r):
                R = r.R
                sp.wait_ge(scattered, R.scatter0 + 16 * NB * R.k)

                def one(it, s):
                    if r.at or not isinstance(it, int):
                        sp.wait_ge(mT_psum, r.at + 4 * it + s - 3)
                    sp.dma_start(row_in[s][:, :], R.rows[ds((4 * it + s) * P, P), :]).then_inc(rows_loaded[s], 16)
                for s in range(4):
                    one(0, s)
                with sp.Fori(1, r.tiles // 4) as it:
                    for s in range(4):
                        one(it, s)
                for s in range(r.tiles % 4):
                    one(r.tiles // 4, s)
            load_rows(RO2)
            sp.wait_ge(notmask_ready, 1)
            sp.wait_ge(vbd_blank, 4)

            def load_mask(it, s, first):
                b = 2 * it + s
                if not first:
                    sp.wait_ge(s_psum, ATT[3].unit0 + NU * (b - 1))
                src = notmask[0:1, ds(b * NK, NK)].rearrange("p (o k) -> p o k", o=1)
                sp.dma_start(kbd[s][C:C + 1, 0:LAST_UNIT].rearrange("p (h k) -> p h k", k=NK),
                             spread(src, 1, H - UH)).then_inc(mask_loaded[s], 16)
                sp.dma_start(kbd[s][64:65, LAST_UNIT:KW].rearrange("p (h k) -> p h k", k=NK),
                             spread(src, 1, UH)).then_inc(mask_loaded[s], 16)
            load_mask(0, 0, True)
            load_mask(0, 1, True)
            with sp.Fori(1, NB // 2) as it:
                load_mask(it, 0, False)
                load_mask(it, 1, False)
            load_rows(RO3)

            with sp.Fori(0, NB) as b:
                sp.wait_ge(*x_ready(7, b + 1))
                sp.dma_start(out.rearrange("b s d -> s b d")[:, ds(b, 1), :].rearrange("s o d -> s (o d)"), X[:, ds(b * D, D)]).then_inc(written, 16)
            sp.wait_ge(written, 16 * NB)

        @block.gpsimd
        def _(pool):
            g = nc.gpsimd
            c = Chain(pool, const_step)
            c.link(g.memset(ident[:, :], 0.0))
            g.affine_select(out=ident[:, :], in_=ident[:, :], compare_op=ALU.not_equal, fill=1.0,
                            base=0, pattern=[[-1, P]], channel_multiplier=1).then_inc(ident_ready, 1)
            c.link(g.memset(ones[:, :], 1.0))
            c.link(g.memset(CT[C:C + 1, :], 1.0))
            c.link(g.memset(earlier[:, :], 0.0))
            c.link(g.affine_select(out=earlier[:, :], in_=earlier[:, :], compare_op=ALU.is_ge, fill=1.0,
                                   base=0, pattern=[[-1, P]], channel_multiplier=1))
            c.link(g.memset(headmask[:, :], 1.0))
            c.link(g.affine_select(out=headmask[:, :], in_=headmask[:, :], compare_op=ALU.is_ge, fill=0.0,
                                   base=0, pattern=[[-8, H]], channel_multiplier=1))
            c.link(g.affine_select(out=headmask[:, :], in_=headmask[:, :], compare_op=ALU.is_ge, fill=0.0,
                                   base=7, pattern=[[8, H]], channel_multiplier=-1))
            scratch_i = texp_i
            c.link(g.iota(tcmp[:, 0:NB * E].bitcast(I32).rearrange("p (t e) -> p t e", e=E), pattern=[[0, NB], [-1, E]], base=8, channel_multiplier=0))
            c.link(g.tensor_copy(desc8[:, :, :], tcmp[:, 0:NB * E].bitcast(I32).rearrange("p (t e) -> p t e", e=E)))
            c.link(g.iota(tcmp[:, :].bitcast(I32).rearrange("p (t e) -> p t e", e=E), pattern=[[1, TILES2], [0, E]], base=0, channel_multiplier=0))
            c.link(g.tensor_copy(tileno[:, :, :], tcmp[:, :].bitcast(I32).rearrange("p (t e) -> p t e", e=E)))
            c.link(g.iota(ecmp[:, :].bitcast(I32).rearrange("p (e j) -> p e j", e=E), pattern=[[0, E], [P, NB]], base=0, channel_multiplier=0))
            c.link(g.tensor_copy(steps128[:, :, :], ecmp[:, :].bitcast(I32).rearrange("p (e j) -> p e j", e=E)))
            picks = scratch_i[:, 0:2 * NB].rearrange("p (k t) -> p k t", k=2)
            c.link(g.iota(picks, pattern=[[NT, 2], [P, NB]], base=CAP_ROWS, channel_multiplier=1))
            g.tensor_copy(trash[:, :, :], picks).then_inc(const_done, 1)
            c.link(g.memset(zero_tile[:, :], 0.0))
            pool.wait_ge(loaded["x"], 16)
            for i, n in enumerate((CAP_ROWS, TILES2 * P, TILES3 * P)):
                view = rows_d[i][0:n, :].rearrange("(t p) d -> p t d", p=P)
                z = spread(zero_tile[:, :].rearrange("p (o d) -> p o d", o=1), 1, n // P)
                pool.dma_start(view, z).then_inc(zeroed, 16)

            def pool_attention(L, R=None):
                def one(it, s, first):
                    b = 2 * it + s
                    if L.wide:
                        if not first:
                            pool.wait_ge(v_psum, L.v0 + 2 * (b - 2) + 2)
                        g.tensor_copy(cts[s][:, :], CT[0:C, ds(b * NK, NK)]).then_inc(cts_ready, 1)
                    else:
                        if not first:
                            pool.wait_ge(s_psum, L.unit0 + NU * (b - 2) + NU)
                        rows, nh = (slice(0, C), H - UH) if L.mask else (slice(0, P), H)
                        g.tensor_tensor(kbd[s][rows, 0:nh * NK].rearrange("p (h k) -> p h k", k=NK),
                                        spread(kT_all[rows, ds(b * NK, NK)].rearrange("p (o k) -> p o k", o=1), 1, nh),
                                        spread(headmask[rows, 0:nh].rearrange("p (h o) -> p h o", o=1), 2, NK),
                                        ALU.mult).then_inc(kbd_ready, 1)
                        if not first:
                            pool.wait_ge(o_psum, L.unit0 + NU * (b - 2) + NU)
                        g.tensor_copy(vbd_steps[s][:, :, 0:8], v_narrow[:, ds(b * D, D)].rearrange("k (h e) -> k h e", e=8))\
                            .then_inc(vbd_ready, 1)

                def bias(b):
                    pool.wait_ge(xn_ready, L.batch0 + b + 1)
                    g.tensor_tensor(X[:, ds(b * D, D)], X[:, ds(b * D, D)], bo_rows[L.bias][:, :], ALU.add).then_inc(bias_added, 1)
                if L.wide:
                    pool.wait_ge(emptied, STAGE_END["ct"])
                else:
                    pool.wait_ge(vbd_blank, 2 * L.nar_n + 2)
                    pool.wait_ge(emptied, STAGE_END[f"kv{L.n}"])
                def pair(it):
                    for s in range(2):
                        one(it, s, False)
                        if L.bias is not None:
                            bias(2 * it + s - 2)
                        if R is not None and it + 2 < NB // 2:
                            gather(R, it + 2, s)
                if R is not None:
                    gather(R, 0)
                    gather(R, 1)
                one(0, 0, True)
                one(0, 1, True)
                if R is not None:
                    gather(R, 2)
                    for it in range(1, NB // 2):
                        pair(it)
                else:
                    with pool.Fori(1, NB // 2) as it:
                        pair(it)
                if L.bias is not None:
                    bias(NB - 2)
                    bias(NB - 1)

            def scatter(R):
                pool.wait_ge(zeroed, 16 * 3)
                pool.wait_ge(routed, R.n + 1)
                for t in range(NB):
                    for k in range(R.k):
                        g.indirect_dma_start(R.rows[:, :], bass.IndirectOffsetOnAxis(ap=to_row[k][:, t:t + 1], axis=0),
                                             XN[:, t * D:(t + 1) * D], None).then_inc(scattered, 16)
                pool.wait_ge(scattered, R.scatter0 + 16 * NB * R.k)

            def gather(R, pair, tile=None):
                if pair == 0:
                    for s in range(2):
                        pool.wait_ge(stored[s], STORED_END[R.n])
                first, last = (2 * pair, 2 * pair + 2) if tile is None else (2 * pair + tile, 2 * pair + tile + 1)
                for n in range(R.k * first, R.k * last):
                    t, k, s = n // R.k, n % R.k, n % 4
                    if n >= 4:
                        pool.wait_ge(combined, COMBINE0[R.n] + n - 3)
                    g.indirect_dma_start(got[s][:, :], None, R.outs[0:R.total, :],
                                         bass.IndirectOffsetOnAxis(ap=from_row[k][:, t:t + 1], axis=0)).then_inc(gathered[s], 16)

            def store_rows(r):
                def one(it, s):
                    pool.wait_ge(m2_done, r.at + 2 * it + s + 1)
                    pool.dma_start(r.R.outs[ds((2 * it + s) * P, P), :], row_out[s][:, :]).then_inc(stored[s], 16)
                with pool.Fori(0, r.tiles // 2) as it:
                    one(it, 0)
                    one(it, 1)

            pool_attention(ATT[0])
            scatter(RT[0])
            def store0(it, s):
                e = 2 * it + s
                pool.wait_ge(o0_ready, e + 1)
                pool.dma_start(outs_d[0][ds(e * CAP, 2 * P), :].rearrange("(r p) d -> p r d", p=P), o0[s][:, 0:2, :]).then_inc(stored[s], 16)
                pool.dma_start(outs_d[0][ds(e * CAP + 2 * P, CAP - 2 * P), :], o0[s][0:CAP - 2 * P, 2, :]).then_inc(stored[s], 16)
            with pool.Fori(0, E // 2) as it:
                store0(it, 0)
                store0(it, 1)
            pool_attention(ATT[1], RT[0])
            pool.wait_ge(loaded["mlp1"], 48)
            g.tensor_copy(w1n, w1n.bitcast(I32)).then_inc(weights_float, 1)
            pool_attention(ATT[2])
            scatter(RT[1])
            store_rows(RO2)
            pool_attention(ATT[3], RT[1])
            scatter(RT[2])
            store_rows(RO3)
            for pair in range(NB // 2):
                gather(RT[2], pair)

        @block.tensor
        def _(pe):
            st = Turns(pe, filled, emptied, bank[0:4])
            mm, tp = nc.tensor.matmul, nc.tensor.transpose

            def prepare_m(n):
                pe.wait_ge(loaded[f"wqk{n}"], 32)
                for half in range(2):
                    b = st.claim()
                    for i in range(4):
                        j = 4 * half + i
                        last = tp(b[:, i * P:(i + 1) * P], wq_nat[:, j * P:(j + 1) * P], ident[:, :])
                    st.fill(last)
                for half in range(2):
                    b = st.claim()
                    for i in range(4):
                        j = 4 * half + i
                        last = tp(b[:, i * C:(i + 1) * C], wk_nat[:, j * P:(j + 1) * P], ident[0:C, 0:C])
                    st.fill(last)
                st.settle()
                for q in range(4):
                    b = st.claim()
                    for i in range(4):
                        h = 8 * (q // 2) + 2 * i + q % 2
                        at = 64 * (h % 2)
                        last = mm(b[0:C, i * D:(i + 1) * D], wkT[at:at + 64, h // 2, :], wqT[at:at + 64, h // 2, :],
                                  start=True, stop=True)
                    st.fill(last)
                st.settle()

            def make_t(h0, h1):
                for h in range(h0, h1):
                    for b0, b1 in T_CHUNKS:
                        b = st.claim()
                        st.fill(mm(b[:, 0:(b1 - b0) * NK], MT[:, h, :], CT[0:C, b0 * NK:b1 * NK], start=True, stop=True))
                if h1 == H:
                    st.settle()

            def pe_attention(L):
                wide = L.wide

                def turn_x(b, s):
                    pe.wait_ge(xn_ready, L.batch0 + b + 1)
                    if not isinstance(b, int) or b > 0:
                        pe.wait_ge(xnT_ready, L.batch0 + b)
                    tp(TR_BANK[:, 0:P], xn[s][:, :], ident[:, :]).then_inc(xnT_psum, 1)

                def query(b, s):
                    pe.wait_ge(xnT_ready, L.batch0 + b + 1)
                    mm(TR_BANK[:, 0:P], nwq[L.nar_n][:, :], xnT[s][:, :], start=True, stop=True).then_inc(q_psum, 1)

                def values(b, s, half):
                    if half == 0:
                        pe.wait_ge(cts_ready, L.c0 + b + 1)
                    n = 2 * b + half
                    if not isinstance(b, int) or b > 0 or half:
                        pe.wait_ge(v_ready, L.v0 + n)
                    mm(V_BANK[0:NK, :], cts[s][:, :], wv[:, half * 512:(half + 1) * 512],
                       start=True, stop=True).then_inc(v_psum, 1)

                def scores(U, b, s, u):
                    if u == 0:
                        if wide:
                            pe.wait_ge(xnT_ready, L.batch0 + b + 1)
                        else:
                            pe.wait_ge(q_ready, L.q0 + b + 1)
                            pe.wait_ge(kbd_ready, L.q0 + b + 1)
                    if not isinstance(U, int) or U >= 2:
                        pe.wait_ge(z_ready, L.unit0 + U - 1)
                    rhs = T_all[:, ds(b * KW + u * UW, UW)] if wide else kbd[s][:, u * UW:(u + 1) * UW]
                    lhs = xnT[s][:, :] if wide else qT[s][:, :]
                    if L.mask and u == NU - 1:
                        lhs, rhs = q_last[s][64:P, :], kbd[s][64:P, LAST_UNIT:KW]
                    mm(S_BANK[u % 2][:, 0:UW], lhs, rhs, start=True, stop=True).then_inc(s_psum, 1)

                def turn_p(U, u):
                    pe.wait_ge(p_ready, L.unit0 + U + 1)
                    if not isinstance(U, int) or U >= 2:
                        pe.wait_ge(pT_ready, L.unit0 + U - 1)
                    for i in range(UH):
                        last = tp(PT_BANK[u % 2][0:NK, i * P:(i + 1) * P], PR[u % 2][:, i * NK:(i + 1) * NK], ident[:, :])
                    last.then_inc(pT_psum, 1)

                def weigh(U, b, s, u):
                    pe.wait_ge(pT_ready, L.unit0 + U + 1)
                    if wide and u == 0:
                        pe.wait_ge(v_ready, L.v0 + 2 * b + 2)
                    if not wide:
                        if u == 0:
                            pe.wait_ge(vbd_ready, L.q0 + b + 1)
                        if u % 2 == 0 and (not isinstance(b, int) or b > 0):
                            pe.wait_ge(on_ready, L.on0 + 2 * (b - 1) + u // 2 + 1)
                    elif not isinstance(U, int) or U >= 1:
                        pe.wait_ge(on_ready, L.on0 + U)
                    for i in range(UH):
                        h = u * UH + i
                        if wide:
                            last = mm(O_BANK[:, i * OB:(i + 1) * OB], PT[u % 2][:, i, :], vw[s][:, h, :], start=True, stop=True)
                        else:
                            last = mm(ON_BANK[u // 2][:, 0:P], vbd[s][:, h * P:(h + 1) * P], PT[u % 2][:, i, :],
                                      start=(h % 8 == 0), stop=(h % 8 == 7))
                    last.then_inc(o_psum, 1)

                def project(U, b, s, u):
                    if wide:
                        pe.wait_ge(oT_ready, L.oT0 + U + 1)
                        if u == 0 and (not isinstance(b, int) or b > 0):
                            pe.wait_ge(L.x_out, b)
                        for j in range(2):
                            last = mm(Y_BANK[:, 0:D], OT[u % 2][:, j, :], wo[:, 2 * u + j, :],
                                      start=(u == 0 and j == 0), stop=(u == NU - 1 and j == 1))
                        if u == NU - 1:
                            last.then_inc(y_psum, 1)
                    elif u == NU - 1:
                        pe.wait_ge(on_ready, L.on0 + 2 * b + 2)
                        if not isinstance(b, int) or b > 0:
                            pe.wait_ge(L.x_out, b)
                        mm(Y_BANK[:, 0:D], OTn[s][:, :], nwo[L.nar_n][:, :], start=True, stop=True).then_inc(y_psum, 1)

                def steps(it):
                    for k in range(2 * NU):
                        U = 2 * NU * it + k

                        def stage(lag):
                            V = U - lag
                            kk = k - lag
                            bb = 2 * it + kk // NU
                            if isinstance(V, int) and not 0 <= V < UNITS:
                                return None
                            return V, bb, (kk // NU) % 2, kk % NU
                        if a := stage(0):
                            if L.mask and a[3] == 0:
                                pe.wait_ge(mask_loaded[a[2]], 32 * (it + 1))
                                pe.wait_ge(last_spread, a[1] + 1)
                            scores(*a)
                        if a := stage(1):
                            turn_p(a[0], a[3])
                        if a := stage(2):
                            weigh(*a)
                        if wide and (a := stage(3)):
                            V, b, s, u = a
                            pe.wait_ge(on_ready, L.on0 + V + 1)
                            nb = 2 * it + (k - 2) // NU + 2
                            if isinstance(nb, int):
                                nb = min(max(nb, 1), NB)
                            pe.wait_ge(xnT_ready, L.batch0 + nb)
                            if not isinstance(V, int) or V >= 1:
                                pe.wait_ge(oT_ready, L.oT0 + V)
                            for j in range(2):
                                last = tp(TR_BANK[:, j * P:(j + 1) * P], ON[u % 2][:, j * P:(j + 1) * P], ident[:, :])
                            last.then_inc(oT_psum, 1)
                        if a := stage(4):
                            project(*a)
                        b1 = 2 * it + k // NU + 1
                        if isinstance(b1, int) and b1 >= NB:
                            continue
                        s1 = (k // NU + 1) % 2
                        u = k % NU
                        if u == 1:
                            if wide:
                                done = 2 * NU * it + k - 2
                                if not isinstance(done, int) or done >= 1:
                                    pe.wait_ge(oT_ready, L.oT0 + done)
                            else:
                                pe.wait_ge(q_ready, L.q0 + b1)
                            turn_x(b1, s1)
                        if wide and u >= 2:
                            values(b1, s1, u - 2)
                        if not wide and u == 3:
                            query(b1, s1)

                turn_x(0, 0)
                if wide:
                    pe.wait_ge(loaded[f"wvo{L.wide_n}"], 32)
                    values(0, 0, 0)
                    values(0, 0, 1)
                else:
                    query(0, 0)
                steps(0)
                with pe.Fori(1, NB // 2 - 1) as it:
                    steps(it)
                steps(NB // 2 - 1)
                steps(NB // 2)

            def turn_all(n):
                for q in range(4):
                    b = st.claim()
                    for i in range(4):
                        t = 4 * q + i
                        pe.wait_ge(xn_kept, NB * n + t + 1)
                        last = tp(b[:, i * P:(i + 1) * P], XN[:, t * D:(t + 1) * D], ident[:, :])
                    st.fill(last)

            def pe_route(R, n):
                turn_all(n)
                for t in range(NB):
                    if t % 4 == 0:
                        pe.wait_ge(emptied, STAGE_END[f"xn{n}"] - 3 + t // 4)
                    last = mm(TR_BANK[:, t * E:(t + 1) * E], xnT_all[:, t * P:(t + 1) * P], wr[R.n][:, :], start=True, stop=True)
                last.then_inc(logits_psum, 1)

            def pe_shared(S):
                def first(g):
                    for f in range(S.nf):
                        p = S.nf * g + f
                        rhs = xnT_all[:, g * 512:(g + 1) * 512]
                        if S.gate:
                            if p >= 2:
                                pe.wait_ge(sh_ready, S.parts0 + p - 1)
                            mm(bank[2 * (p % 2)][:, :], S.gate(f), rhs, start=True, stop=True).then_inc(sh_psum, 1)
                            mm(bank[2 * (p % 2) + 1][:, :], S.w1(f), rhs, start=True, stop=True).then_inc(sh_psum, 1)
                        else:
                            if p >= 4:
                                pe.wait_ge(sh_ready, S.parts0 + p - 3)
                            mm(bank[p % 4][:, :], S.w1(f), rhs, start=True, stop=True).then_inc(sh_psum, 1)

                def second(g):
                    pe.wait_ge(sh_ready, S.parts0 + S.nf * (g + 1))
                    if g >= 2:
                        pe.wait_ge(shared_done, 4 * (S.groups0 + g - 1))
                    for t in range(4):
                        for f in range(S.nf):
                            last = mm(bank[6 + g % 2][:, t * D:(t + 1) * D], shT[g % 2][:, f, t * P:(t + 1) * P], S.w2(f),
                                      start=(f == 0), stop=(f == S.nf - 1))
                    last.then_inc(so_psum, 1)
                first(0)
                for g in range(4):
                    if g < 3:
                        first(g + 1)
                    second(g)
                pe.wait_ge(shared_done, 4 * (S.groups0 + 4))

            def pe_rank(R):
                pe.wait_ge(picked, R.n + 1)
                both = rt["both"][:, :, :].rearrange("p t e -> p (t e)")
                mm(bank[4][:, 0:NB * E], earlier[:, :], both, start=True, stop=True)
                mm(bank[5][:, 0:NB * E], ones[:, :], both, start=True, stop=True).then_inc(ranked, 1)

            def pe_mlp(r):
                w, nj = r.width, r.width // P
                tr, out_b = TR_BANK, Y_BANK
                h_bank = [[bank[0], bank[1]], [bank[2], bank[3]]]
                t_bank = [bank[4], bank[5]]

                def turn(it, s):
                    i = 4 * it + s
                    if s == 4:
                        it, s = it + 1, 0
                    pe.wait_ge(rows_loaded[s], 16 * (r.rows0[s] + it + 1))
                    if r.at or not isinstance(it, int) or i > 0:
                        pe.wait_ge(mT_ready, r.at + i)
                    tp(tr[:, 0:P], row_in[s][:, :], ident[:, :]).then_inc(mT_psum, 1)

                def expert(it, s):
                    return pe.value_load(texp_i[0:1, ds(4 * it + s, 1)], min_val=0, max_val=E - 1)

                def first(it, s, e):
                    i = 4 * it + s
                    pe.wait_ge(mT_ready, r.at + i + 1)
                    if not isinstance(it, int) or i >= 2:
                        pe.wait_ge(h_ready, r.at + i - 1)
                    mm(h_bank[s % 2][0][:, :], mxT[s % 2][:, :], r.w1[:, ds(e * 512, 512)], start=True, stop=True).then_inc(m1_psum, 1)

                def turn_h(it, s):
                    i = 4 * it + s
                    pe.wait_ge(h_ready, r.at + i + 1)
                    if not isinstance(it, int) or i >= 2:
                        pe.wait_ge(hT_ready, r.at + i - 1)
                    for j in range(nj):
                        last = tp(t_bank[s % 2][:, j * P:(j + 1) * P], hid[s % 2][:, j * P:(j + 1) * P], ident[:, :])
                    last.then_inc(hT_psum, 1)

                def second(it, s, e):
                    i = 4 * it + s
                    pe.wait_ge(hT_ready, r.at + i + 1)
                    if not isinstance(it, int) or i > 0:
                        pe.wait_ge(m2_done, r.at + i)
                    for j in range(nj):
                        last = mm(out_b[:, 0:D], hidT[s % 2][:, j, :], r.w2[:, ds(e * w + j * P, P)], start=(j == 0), stop=(j == nj - 1))
                    last.then_inc(m2_psum, 1)

                def steps(it):
                    def runs(s):
                        return not isinstance(it, int) or 0 <= 4 * it + s < r.tiles
                    e = {}

                    def read(*ss):
                        for s in ss:
                            if runs(s):
                                e[s] = expert(it, s)
                    read(0)
                    for s in range(4):
                        if runs(s):
                            first(it, s, e[s])
                        read(*((1, -2), (2, -1), (3,), ())[s])
                        if runs(s + 1):
                            turn(it, s + 1)
                        if runs(s - 1):
                            turn_h(it, s - 1)
                        if runs(s - 2):
                            second(it, s - 2, e[s - 2])
                whole = r.tiles // 4
                turn(0, 0)
                steps(0)
                with pe.Fori(1, whole if r.tiles % 4 else whole - 1) as it:
                    steps(it)
                for it in range(whole if r.tiles % 4 else whole - 1, (r.tiles + 1) // 4 + 1):
                    steps(it)

            def narrow_kv(L):
                n, rows = L.nar_n, C + 1 if L.n == 2 else C
                if L.n == 3:
                    pe.wait_ge(loaded["narrow3"], 64)
                pe.wait_ge(const_done, 1)
                for b0, b1 in T_CHUNKS:
                    b = st.claim()
                    st.fill(mm(b[:, 0:(b1 - b0) * NK], nwk[n][0:rows, :], CT[0:rows, b0 * NK:b1 * NK], start=True, stop=True))
                for q in range(4):
                    b = st.claim()
                    for i in range(4):
                        last = mm(b[0:NK, i * D:(i + 1) * D], CT[0:rows, (4 * q + i) * NK:(4 * q + i + 1) * NK],
                                  nwv[n][0:rows, :], start=True, stop=True)
                    st.fill(last)
                st.settle()

            pe.wait_ge(ident_ready, 1)
            pe.wait_ge(loaded["ctx"], 16)
            for q in range(4):
                b = st.claim()
                for i in range(4):
                    last = tp(b[0:C, i * NK:(i + 1) * NK], ctx_nat[:, 4 * q + i, :], ident[0:NK, 0:NK])
                st.fill(last)
            prepare_m(0)
            make_t(0, H)
            pe.wait_ge(loaded["misc"], 16 * 4)
            b = st.claim()
            st.fill(tp(b[:, 0:32], row_in[0][0:32, :], ident[0:32, 0:32]))
            b = st.claim()
            st.fill(tp(b[:, 0:E], row_in[1][0:E, :], ident[0:E, 0:E]))
            pe.wait_ge(dve_prepared, 1)
            pe_attention(ATT[0])
            prepare_m(1)
            pe_route(RT[0], 0)
            pe.wait_ge(loaded["narrow2"], 16 * 7)
            for src in (got[0], got[1]):
                b = st.claim()
                st.fill(tp(b[:, 0:P], src[:, :], ident[:, :]))
            for src in (got[2], got[3]):
                b = st.claim()
                st.fill(tp(b[0:C, 0:P], src[:, 0:C], ident[:, :]))
            st.settle()
            make_t(0, 1)
            pe_rank(RT[0])
            make_t(1, H)
            for q in range(RT[0].tiles // 4):
                for i, (t0, _) in enumerate(ROW_PIECES):
                    if 4 * q == t0:
                        pe.wait_ge(rows_loaded[i], 16)
                b = st.claim()
                for i in range(4):
                    last = tp(b[:, i * P:(i + 1) * P], rows0[:, 4 * q + i, :], ident[:, :])
                st.fill(last)
            st.settle()

            def hidden(it, s):
                e = 2 * it + s
                pe.wait_ge(w1_loaded[s], 16 * (it + 1))
                for f in range(4):
                    if not isinstance(e, int) or e > 0:
                        pe.wait_ge(h0_ready, 4 * e + f - 3)
                    mm(bank[f][:, 0:CAP], w1s[s][:, f * P:(f + 1) * P], bufT[:, ds(e * CAP, CAP)],
                       start=True, stop=True).then_inc(h0_psum, 1)

            def outputs(it, s):
                e = 2 * it + s
                pe.wait_ge(w2_loaded[s], 16 * (it + 1))
                pe.wait_ge(h0_ready, 4 * e + 4)
                if not isinstance(e, int) or e >= 2:
                    pe.wait_ge(o0_ready, e - 1)
                ob = bank[4 + s]
                for q in range(3):
                    n = min(P, CAP - q * P)
                    for f in range(4):
                        last = mm(ob[0:n, q * D:(q + 1) * D], hT0[s][:, f, q * P:q * P + n], w2s[s][:, f, :],
                                  start=(f == 0), stop=(f == 3))
                last.then_inc(o0_psum, 1)
            hidden(0, 0)
            hidden(0, 1)
            outputs(0, 0)
            with pe.Fori(1, E // 2) as it:
                hidden(it, 0)
                outputs(it - 1, 1)
                hidden(it, 1)
                outputs(it, 0)
            outputs(E // 2 - 1, 1)
            pe.wait_ge(o0_ready, E)
            pe_attention(ATT[1])
            pe.wait_ge(weights_float, 1)
            for k in range(2):
                b = st.claim()
                for j in range(3):
                    last = tp(b[:, j * P:(j + 1) * P], w1n[:, k * 384 + j * P:k * 384 + (j + 1) * P], ident[:, :])
                st.fill(last)
            b = st.claim()
            for j in range(3):
                last = tp(b[:, j * P:(j + 1) * P], w1n[:, 768 + j * P:768 + (j + 1) * P], ident[:, :])
            st.fill(last)
            turn_all(1)
            st.settle()
            pe_shared(SH1)
            narrow_kv(ATT[2])
            pe_attention(ATT[2])
            def turn_weights(n0, n1):
                for n in range(n0, n1):
                    pe.wait_ge(nat_loaded[n % 4], 16 * (n // 4 + 1))
                    b = st.claim()
                    for j in range(4):
                        last = tp(b[:, j * P:(j + 1) * P], nat2[n % 4][:, j * P:(j + 1) * P], ident[:, :])
                    st.fill(last)
            turn_weights(0, NAT_FIRST)
            pe_route(RT[1], 2)
            turn_weights(NAT_FIRST, NAT_FIRST + 2)
            pe_rank(RT[1])
            turn_weights(NAT_FIRST + 2, 18)
            st.settle()
            pe_shared(SH2)
            pe.wait_ge(routed, 2)
            pe_mlp(RO2)
            pe.wait_ge(m2_done, RO2.at + RO2.tiles)
            narrow_kv(ATT[3])
            pe_attention(ATT[3])
            pe_route(RT[2], 3)
            pe_rank(RT[2])
            pe.wait_ge(loaded["mlp3"], 32)
            pe_shared(SH3)
            pe.wait_ge(routed, 3)
            pe_mlp(RO3)

        @block.scalar
        def _(act):
            st = Turns(act, filled, emptied, bank[0:4])
            a = nc.scalar.activation

            def copy(o, i):
                return a(o, i, ACT.Copy)

            def prepare_m(n):
                for half in range(2):
                    b = st.take()
                    st.empty(copy(wqT[:, 4 * half:4 * half + 4, :], b[:, :].rearrange("p (j d) -> p j d", j=4)))
                for half in range(2):
                    b = st.take()
                    st.empty(copy(wkT[:, 4 * half:4 * half + 4, :], b[:, 0:4 * C].rearrange("p (j c) -> p j c", j=4)))
                for q in range(4):
                    b = st.take()
                    heads = MT[:, 8 * (q // 2):8 * (q // 2) + 8, :].rearrange("c (i two) d -> c i two d", two=2)
                    st.empty(copy(heads[:, :, q % 2, :], b[0:C, :].rearrange("p (j d) -> p j d", j=4)))

            def make_t():
                for h in range(H):
                    for b0, b1 in T_CHUNKS:
                        b = st.take()
                        o = T_all[:, b0 * KW:b1 * KW].rearrange("p (b h k) -> p b h k", h=H, k=NK)[:, :, h, :]
                        st.empty(copy(o, b[:, 0:(b1 - b0) * NK].rearrange("p (b k) -> p b k", k=NK)))

            def act_attention(L):
                wide = L.wide

                def turned_x(b, s):
                    act.wait_ge(xnT_psum, L.batch0 + b + 1)
                    copy(xnT[s][:, :], TR_BANK[:, 0:P]).then_inc(xnT_ready, 1)

                def query(b, s):
                    act.wait_ge(q_psum, L.q0 + b + 1)
                    if L.n == 2:
                        a(qT[s][:, :], TR_BANK[:, 0:P], ACT.Identity, bias=bq2[:, 0:1]).then_inc(q_ready, 1)
                    else:
                        copy(qT[s][0:C, :], TR_BANK[0:C, 0:P])
                        copy(q_last[s][C:P, :], TR_BANK[C:P, 0:P]).then_inc(q_ready, 1)

                def values(b, s, half):
                    act.wait_ge(v_psum, L.v0 + 2 * b + half + 1)
                    copy(vw[s][:, half * 8:half * 8 + 8, 0:64], V_BANK[0:NK, :].rearrange("k (h e) -> k h e", h=8)).then_inc(v_ready, 1)

                def steps(it):
                    for k in range(2 * NU):
                        U = 2 * NU * it + k

                        def stage(lag):
                            V = U - lag
                            kk = k - lag
                            if isinstance(V, int) and not 0 <= V < UNITS:
                                return None
                            return V, 2 * it + kk // NU, kk % NU
                        if t := stage(1):
                            V, b, u = t
                            act.wait_ge(pT_psum, L.unit0 + V + 1)
                            copy(PT[u % 2], PT_BANK[u % 2][0:NK, :].rearrange("k (h q) -> k h q", h=UH)).then_inc(pT_ready, 1)
                        if wide and (t := stage(3)):
                            V, b, u = t
                            act.wait_ge(oT_psum, L.oT0 + V + 1)
                            copy(OT[u % 2], TR_BANK[:, 0:256].rearrange("p (j q) -> p j q", j=2)).then_inc(oT_ready, 1)
                        if t := stage(0):
                            V, b, u = t
                            act.wait_ge(z_ready, L.unit0 + V + 1)
                            a(PR[u % 2], Z[u % 2], ACT.Exp, scale=L.scale).then_inc(p_ready, 1)
                        b1 = 2 * it + k // NU + 1
                        if isinstance(b1, int) and b1 >= NB:
                            continue
                        s1 = (k // NU + 1) % 2
                        u = k % NU
                        if u == 1:
                            turned_x(b1, s1)
                        if wide and u >= 2:
                            values(b1, s1, u - 2)
                        if not wide and u == 3:
                            query(b1, s1)
                act.preload_act_table(ACT.Exp)
                turned_x(0, 0)
                if wide:
                    values(0, 0, 0)
                    values(0, 0, 1)
                else:
                    query(0, 0)
                steps(0)
                with act.Fori(1, NB // 2 - 1) as it:
                    steps(it)
                steps(NB // 2 - 1)
                steps(NB // 2)

            def turned_all():
                for q in range(4):
                    b = st.take()
                    st.empty(copy(xnT_all[:, q * 512:(q + 1) * 512], b[:, :]))

            def act_route(R):
                turned_all()
                act.wait_ge(exps_in, R.n + 1)
                if R.n == 1:
                    a(rc["gate2"][:, :], rc["diff"][:, :], ACT.Exp).then_inc(exps_out, 1)
                else:
                    a(rt["score"][:, :, :], rt["work"][:, :, :], ACT.Exp).then_inc(exps_out, 1)

            def act_shared(S):
                act.preload_act_table(ACT.Silu)
                for p in range(4 * S.nf):
                    g, f = p // S.nf, p % S.nf
                    if S.gate:
                        act.wait_ge(sh_psum, S.products0 + 2 * p + 1)
                        a(sh_gate[p % 2], bank[2 * (p % 2)][:, :], ACT.Silu).then_inc(sh_gated, 1)
                    else:
                        act.wait_ge(sh_psum, S.products0 + p + 1)
                        if g >= 2 and f == 0:
                            act.wait_ge(so_psum, S.groups0 + g - 1)
                        a(shT[g % 2][:, f, :], bank[p % 4][:, :], ACT.Silu).then_inc(sh_ready, 1)

            def act_mlp(r):
                w, nj = r.width, r.width // P
                h_bank = [[bank[0], bank[1]], [bank[2], bank[3]]]

                def turned(it, s):
                    i = 2 * it + s
                    act.wait_ge(mT_psum, r.at + i + 1)
                    if not isinstance(it, int) or it > 0:
                        act.wait_ge(m1_psum, r.at + i - 1)
                    copy(mxT[s][:, :], TR_BANK[:, 0:P]).then_inc(mT_ready, 1)

                def bend(it, s):
                    i = 2 * it + s
                    act.wait_ge(m1_psum, r.at + i + 1)
                    if r.gated:
                        if not isinstance(it, int) or it > 0:
                            act.wait_ge(h_ready, r.at + i - 1)
                        a(gate[s][:, 0:w], h_bank[s][0][:, w:2 * w], ACT.Silu).then_inc(g_ready, 1)
                    else:
                        if not isinstance(it, int) or it > 0:
                            act.wait_ge(hT_psum, r.at + i - 1)
                        a(hid[s][:, 0:w], h_bank[s][0][:, 0:w], ACT.Silu).then_inc(h_ready, 1)
                act.preload_act_table(ACT.Silu)

                def steps(it):
                    for s in range(2):
                        i = 2 * it + s
                        bend(it, s)
                        if not isinstance(i, int) or i + 1 < r.tiles:
                            turned(*((it, 1) if s == 0 else (it + 1, 0)))
                turned(0, 0)
                steps(0)
                with act.Fori(1, r.tiles // 2 - 1) as it:
                    steps(it)
                steps(r.tiles // 2 - 1)

            def narrow_kv(L):
                if L.q0:
                    act.wait_ge(vbd_ready, L.q0)
                for b0, b1 in T_CHUNKS:
                    b = st.take()
                    st.empty(copy(kT_all[:, b0 * NK:b1 * NK], b[:, 0:(b1 - b0) * NK]))
                for q in range(4):
                    b = st.take()
                    st.empty(copy(v_narrow[:, q * 512:(q + 1) * 512], b[0:NK, :]))

            act.dma_start(wq_nat, A["L0_xattn_Wq"]).then_inc(loaded["wqk0"], 16)
            for q in range(4):
                b = st.take()
                st.empty(copy(CT[0:C, 4 * q * NK:(4 * q + 4) * NK], b[0:C, 0:4 * NK]))
            prepare_m(0)
            make_t()
            b = st.take()
            st.empty(copy(b1c[:, :], b[:, 0:32]))
            b = st.take()
            st.empty(copy(wr[1][:, :], b[:, 0:E]))
            act_attention(ATT[0])
            prepare_m(1)
            act_route(RT[0])
            b = st.take()
            st.empty(copy(nwq[0][:, :], b[:, 0:P]))
            b = st.take()
            st.empty(copy(nwo[0][:, :], b[:, 0:P]))
            for half in range(2):
                b = st.take()
                v = b[0:C, 0:P].rearrange("c (h e) -> c h e", e=16)
                copy(nwk[0][0:C, half * 64:half * 64 + 64].rearrange("c (h e) -> c h e", e=8), v[:, :, 0:8])
                st.empty(copy(nwv[0][0:C, half * 64:half * 64 + 64].rearrange("c (h e) -> c h e", e=8), v[:, :, 8:16]))
            make_t()
            for q in range(RT[0].tiles // 4):
                b = st.take()
                st.empty(copy(bufT[:, q * 512:(q + 1) * 512], b[:, :]))
            act.preload_act_table(ACT.Gelu)

            def bend0(it, s):
                e = 2 * it + s
                for f in range(4):
                    act.wait_ge(h0_psum, 4 * e + f + 1)
                    if f == 0 and (not isinstance(e, int) or e >= 2):
                        act.wait_ge(o0_psum, e - 1)
                    a(hT0[s][:, f, :], bank[f][:, 0:CAP], ACT.Gelu, bias=b1c[:, ds(4 * e + f, 1)]).then_inc(h0_ready, 1)
            bend0(0, 0)
            bend0(0, 1)
            with act.Fori(1, E // 2) as it:
                bend0(it, 0)
                bend0(it, 1)
            act_attention(ATT[1])
            for k in range(2):
                b = st.take()
                st.empty(a((wg1, wu1)[k], b[:, 0:384], ACT.Copy, scale=1.0 / 127.0))
            b = st.take()
            st.empty(a(wd1, b[:, 0:384].rearrange("p (j d) -> p j d", j=3), ACT.Copy, scale=1.0 / 127.0))
            turned_all()
            act_shared(SH1)
            narrow_kv(ATT[2])
            act_attention(ATT[2])
            def turned_weights(n0, n1):
                for n in range(n0, n1):
                    b = st.take()
                    dst = (w2_2 if n % 2 else w1_2)[:, (n // 2) * 512:(n // 2 + 1) * 512]
                    st.empty(copy(dst, b[:, :]))
            turned_weights(0, NAT_FIRST)
            act_route(RT[1])
            turned_weights(NAT_FIRST, 18)
            act_shared(SH2)
            act_mlp(RO2)
            narrow_kv(ATT[3])
            act_attention(ATT[3])
            act_route(RT[2])
            act_shared(SH3)
            act_mlp(RO3)

        @block.vector
        def _(dve):
            v = nc.vector
            c = Chain(dve, dve_step)
            tt, ts, stt = v.tensor_tensor, v.tensor_scalar, v.scalar_tensor_tensor

            def norm_stats(it, ready):
                ready(2 * it + 1)
                for s in range(2):
                    xb = X[:, ds((2 * it + s) * D, D)]
                    ins = v.bn_stats(ln_stats[:, s, :], xb)
                    if s == 0:
                        ins.then_inc(dve_step, 1)
                        c.n += 1
                    else:
                        c.link(ins)
                v.tensor_copy(ln_t[:, 0:1], ln_stats[:, 0, 0:1])
                for s in range(2):
                    ins = v.bn_aggr(ln_mv[:, s, :], ln_stats[:, s, :])
                    if s == 0:
                        ins.then_inc(dve_step, 1)
                        c.n += 1
                    else:
                        c.link(ins)

            def norm_guess():
                c.link(ts(ln_ve[:, :], ln_mv[:, :, 1], EPS, None, ALU.add))
                c.link(ts(ln_r[:, :].bitcast(I32), ln_ve[:, :].bitcast(I32), -0.5, RSQRT_MAGIC, ALU.mult, ALU.add))

            def norm_newton():
                c.link(stt(ln_t[:, :], ln_r[:, :], -0.5, ln_r[:, :], ALU.mult, ALU.mult))
                c.link(tt(ln_t[:, :], ln_t[:, :], ln_ve[:, :], ALU.mult))
                c.link(stt(ln_r[:, :], ln_t[:, :], 1.5, ln_r[:, :], ALU.add, ALU.mult))

            def norm_apply(it, free, to):
                free()
                for s in range(2):
                    xb = X[:, ds((2 * it + s) * D, D)]
                    for dst, done in to(it, s):
                        ins = ts(dst, xb, ln_mv[:, s, 0:1], ln_r[:, s:s + 1], ALU.subtract, ALU.mult)
                        ins.then_inc(done, 1)

            LN_LINKS = 2 + 2 + 2 + 9

            def blank(L):
                for s in range(2):
                    if L.mask:
                        c.link(v.memset(kbd[s][C:P, 0:LAST_UNIT], 0.0))
                        c.link(v.memset(kbd[s][64:C, LAST_UNIT:KW], 0.0))
                        c.link(v.memset(qT[s][C:P, :], 1.0))
                        c.link(v.memset(q_last[s][64:C, :], 1.0))
                    c.link(v.memset(vbd[s], 0.0))
                    c.link(v.memset(vbd_steps[s][:, 0:8, 64:72], 1.0))
                    v.memset(vbd_steps[s][:, 7:15, 72:80], 1.0).then_inc(vbd_blank, 1)

            NORM_PARTS = {1: (0, 1), 2: (2,), 3: (3, 4)}

            def dve_attention(L):
                wide = L.wide
                sl = L.unit0

                def norm(it, part=None):
                    def ready(n):
                        if L.n == 2:
                            dve.wait_ge(*x_ready(3, n + 1))
                        if L.n > 0:
                            v.tensor_copy(carry[:, :], ln_mv[:, 0, 0:1])

                    def free():
                        if not isinstance(it, int) or it > 0:
                            dve.wait_ge(xnT_psum, L.batch0 + 2 * it)
                    if part in (None, 0):
                        norm_stats(it, ready)
                    if part in (None, 1):
                        norm_guess()
                        norm_newton()
                    if part in (None, 2):
                        norm_newton()
                    if part in (None, 3):
                        norm_newton()
                    if part in (None, 4):
                        norm_apply(it, free, lambda it, s: [(xn[s][:, :], xn_ready)])

                def add_y(b):
                    dve.wait_ge(y_psum, L.batch0 + b + 1)
                    if L.bias is not None:
                        dve.wait_ge(bias_added, L.b0 + b + 1)
                    xb = X[:, ds(b * D, D)]
                    tt(xb, xb, Y_BANK[:, 0:D], ALU.add).then_inc(L.x_out, 1)
                    dve.wait_ge(L.x_out, b + 1)
                    v.tensor_copy(carry[:, :], ln_mv[:, 0, 0:1])
                    v.bn_stats(all_stats[:, ds(b, 1), :].rearrange("p o s -> p (o s)"), xb).then_inc(stats_ready, 1)

                def spread_last(b, s):
                    tt(kbd[s][C:P, LAST_UNIT:KW].rearrange("p (h k) -> p h k", k=NK),
                       spread(kT_all[C:P, ds(b * NK, NK)].rearrange("p (o k) -> p o k", o=1), 1, UH),
                       spread(headmask[C:P, H - UH:H].rearrange("p (h o) -> p h o", o=1), 2, NK), ALU.mult).then_inc(last_spread, 1)

                def steps(it):
                    for k in range(2 * NU):
                        U = 2 * NU * it + k
                        u = k % NU
                        if u == 0:
                            b = 2 * it + k // NU - 2
                            if not isinstance(b, int) or 0 <= b < NB:
                                add_y(b)
                            nb = 2 * it + k // NU + 1
                            if L.mask and (not isinstance(nb, int) or nb < NB):
                                if not isinstance(nb, int) or nb >= 2:
                                    dve.wait_ge(s_psum, sl + NU * (nb - 1))
                                spread_last(nb, (k // NU + 1) % 2)
                        if not isinstance(U, int) or U < UNITS:
                            b = 2 * it + k // NU
                            dve.wait_ge(s_psum, sl + U + 1)
                            src = S_BANK[u % 2][:, 0:UW].rearrange("p (h k) -> p h k", h=UH)
                            c.link(v.tensor_reduce(mx[u % 2][:, :], src, AX.X, ALU.max))
                            tt(Z[u % 2].rearrange("p (h k) -> p h k", h=UH), src,
                               spread(mx[u % 2][:, :].rearrange("p (h o) -> p h o", o=1), 2, NK), ALU.subtract).then_inc(z_ready, 1)
                        lag = 2 if wide else 3
                        V = U - lag
                        if not wide and (k - 3) % 2 == 1 and (not isinstance(V, int) or 0 <= V < UNITS):
                            half = (k - 3) % NU // 2
                            rows_o, rows_d_ = (slice(0, 64), slice(64, P))[::1 - 2 * half]
                            ob = ON_BANK[half]
                            dve.wait_ge(o_psum, sl + V + 1)
                            c.link(v.reciprocal(rden[rows_o, :], ob[rows_d_, 0:P]))
                            tt(OTn[(k - 3) // NU % 2][rows_o, :], ob[rows_o, 0:P], rden[rows_o, :], ALU.mult).then_inc(on_ready, 1)
                        elif wide and (not isinstance(V, int) or 0 <= V < UNITS):
                            uu = (k - 2) % NU
                            dve.wait_ge(o_psum, sl + V + 1)
                            e = OB
                            o = O_BANK[:, 0:UH * e].rearrange("p (h e) -> p h e", h=UH)
                            c.link(v.reciprocal(rsum[uu % 2][:, :], o[:, :, e - 1]))
                            dst = ON[uu % 2].rearrange("p (h e) -> p h e", h=UH)
                            tt(dst, o[:, :, 0:e - 1], spread(rsum[uu % 2][:, :].rearrange("p (h o) -> p h o", o=1), 2, e - 1),
                               ALU.mult).then_inc(on_ready, 1)
                        if not isinstance(it, int) or it + 1 < NB // 2:
                            for part in NORM_PARTS.get(k, ()):
                                norm(it + 1, part)
                        if k >= 4 and L.n in (1, 3) and (not isinstance(it, int) or it + 2 < NB // 2):
                            combine_pair(RT[L.n // 2], it + 2, (k - 4,))

                links = 2 * NU + 2 * (NU if wide else 2) + LN_LINKS
                if L.mask:
                    dve.wait_ge(emptied, STAGE_END["kv3"])
                    spread_last(0, 0)
                if L.n in (1, 3):
                    combine_pair(RT[L.n // 2], 0)
                norm(0)
                if L.n in (1, 3):
                    combine_pair(RT[L.n // 2], 1)
                steps(0)
                c.enter(0, links)
                with dve.Fori(1, NB // 2 - 2) as it:
                    c.resume(it - 1)
                    steps(it)
                c.leave(NB // 2 - 3)
                for it in range(NB // 2 - 2, NB // 2 + 1):
                    steps(it)

            def norm_all(n):
                dve.wait_ge(stats_ready, NB * (n + 1))
                for t in range(NB):
                    ins = v.bn_aggr(all_mv[:, t, :], all_stats[:, t, :])
                    if t < NB - 1:
                        ins.then_inc(dve_step, 1)
                        c.n += 1
                    else:
                        c.link(ins)
                c.link(ts(all_ve[:, :], all_mv[:, :, 1], EPS, None, ALU.add))
                c.link(ts(all_r[:, :].bitcast(I32), all_ve[:, :].bitcast(I32), -0.5, RSQRT_MAGIC, ALU.mult, ALU.add))
                for _ in range(3):
                    c.link(stt(all_t[:, :], all_r[:, :], -0.5, all_r[:, :], ALU.mult, ALU.mult))
                    c.link(tt(all_t[:, :], all_t[:, :], all_ve[:, :], ALU.mult))
                    c.link(stt(all_r[:, :], all_t[:, :], 1.5, all_r[:, :], ALU.add, ALU.mult))
                for t in range(NB):
                    ts(XN[:, t * D:(t + 1) * D], X[:, t * D:(t + 1) * D], all_mv[:, t, 0:1], all_r[:, t:t + 1],
                       ALU.subtract, ALU.mult).then_inc(xn_kept, 1)

            def route(R, at):
                n = R.n
                norm_all(at)
                dve.wait_ge(const_done, 1)
                dve.wait_ge(logits_psum, n + 1)
                score, work, pick1, pick2, both, pos, tot, cum, cum2 = (rt[k] for k in "score work pick1 pick2 both pos tot cum cum2".split())
                X_ = R.experts

                def rows(t):
                    return spread(t[:, :].rearrange("p (t o) -> p t o", o=1), 2, E)

                def per_expert(t):
                    return spread(t[:, :].rearrange("p (o e) -> p o e", o=1), 1, NB)
                lg = TR_BANK[:, 0:NB * E].rearrange("p (t e) -> p t e", e=E)
                if n == 0:
                    c.link(tt(score[:, :, :], lg, per_expert(br_rows), ALU.add))
                else:
                    c.link(v.tensor_copy(score[:, :, :], lg))
                if X_ < E:
                    c.link(v.memset(score[:, :, X_:E], BELOW_ALL))
                if n != 1:
                    c.link(v.tensor_reduce(rc["best1"][:, :], score[:, :, :], AX.X, ALU.max))
                    tt(work[:, :, :], score[:, :, :], rows(rc["best1"]), ALU.subtract).then_inc(exps_in, 1)
                    dve.wait_ge(exps_out, n + 1)
                    c.link(v.tensor_reduce(rc["sum"][:, :], score[:, :, :], AX.X, ALU.add))
                    c.link(v.reciprocal(rc["inv"][:, :], rc["sum"][:, :]))
                    c.link(tt(score[:, :, :], score[:, :, :], rows(rc["inv"]), ALU.mult))
                    if X_ < E:
                        c.link(v.memset(score[:, :, X_:E], -1.0))

                def pick(src, best, first, out_):
                    c.link(v.tensor_reduce(best[:, :], src[:, :, :], AX.X, ALU.max))
                    c.link(tt(work[:, :, :], src[:, :, :], rows(best), ALU.is_equal))
                    c.link(tt(work[:, :, :], work[:, :, :], desc8[:, :, :], ALU.mult))
                    c.link(v.tensor_reduce(first[:, :], work[:, :, :], AX.X, ALU.max))
                    c.link(tt(out_[:, :, :], desc8[:, :, :], rows(first), ALU.is_equal))
                pick(score, rc["best1"], rc["first1"], pick1)
                if R.k == 2:
                    c.link(stt(cum[:, :, :], pick1[:, :, :], BELOW_ALL, score[:, :, :], ALU.mult, ALU.add))
                    pick(cum, rc["best2"], rc["first2"], pick2)
                    tt(both[:, :, :], pick1[:, :, :], pick2[:, :, :], ALU.add).then_inc(picked, 1)
                else:
                    v.tensor_copy(both[:, :, :], pick1[:, :, :]).then_inc(picked, 1)
                if n == 1:
                    tt(rc["diff"][:, :], rc["best2"][:, :], rc["best1"][:, :], ALU.subtract).then_inc(exps_in, 1)
                    dve.wait_ge(exps_out, n + 1)
                    c.link(ts(rc["sum"][:, :], rc["gate2"][:, :], 1.0, None, ALU.add))
                    c.link(v.reciprocal(rc["gate1"][:, :], rc["sum"][:, :]))
                    c.link(tt(rc["gate2"][:, :], rc["gate2"][:, :], rc["gate1"][:, :], ALU.mult))
                dve.wait_ge(ranked, n + 1)
                c.link(v.tensor_copy(tot[:, :, :], bank[5][:, 0:NB * E].rearrange("p (t e) -> p t e", e=E)))
                src, dst = tot, cum
                for sh in (1, 2, 4, 8):
                    c.link(v.tensor_copy(dst[:, 0:sh, :], src[:, 0:sh, :]))
                    c.link(tt(dst[:, sh:NB, :], src[:, sh:NB, :], src[:, 0:NB - sh, :], ALU.add))
                    src, dst = dst, (cum2 if dst is cum else cum)
                total = src
                c.link(tt(pos[:, :, :], bank[4][:, 0:NB * E].rearrange("p (t e) -> p t e", e=E), total[:, :, :], ALU.add))
                c.link(tt(pos[:, :, :], pos[:, :, :], tot[:, :, :], ALU.subtract))
                if n > 0:
                    ecm = ecmp[:, :].rearrange("p (e j) -> p e j", e=E)
                    c.link(tt(ecm, spread(total[:, NB - 1, :].rearrange("p (e o) -> p e o", o=1), 2, NB), steps128[:, :, :], ALU.is_gt))
                    c.link(v.tensor_reduce(ec["tiles"][:, :], ecm, AX.X, ALU.add))
                    s_, d_ = ec["tiles"], ec["end"]
                    for sh in (1, 2, 4):
                        c.link(v.tensor_copy(d_[:, 0:sh], s_[:, 0:sh]))
                        c.link(tt(d_[:, sh:E], s_[:, sh:E], s_[:, 0:E - sh], ALU.add))
                        s_, d_ = d_, (ec["end2"] if d_ is ec["end"] else ec["end"])
                    end = s_
                    c.link(tt(ec["start"][:, :], end[:, :], ec["tiles"][:, :], ALU.subtract))
                    c.link(ts(ec["start"][:, :], ec["start"][:, :], float(P), None, ALU.mult))
                    c.link(tt(pos[:, :, :], pos[:, :, :], per_expert(ec["start"]), ALU.add))
                    tc_ = tcmp[:, 0:TILES2 * E].rearrange("p (t e) -> p t e", e=E)
                    c.link(tt(tc_, tileno[:, :, :], spread(end[:, :].rearrange("p (o e) -> p o e", o=1), 1, TILES2), ALU.is_ge))
                    c.link(v.tensor_reduce(texp[:, :], tc_, AX.X, ALU.add))
                    c.link(ts(texp[:, :], texp[:, :], float(X_ - 1), None, ALU.min))
                    c.link(v.tensor_copy(texp_i[:, :], texp[:, :]))
                for k, (pk, first, best) in enumerate(((pick1, "first1", "best1"), (pick2, "first2", "best2"))[:R.k]):
                    place, keep = rc[f"place{k + 1}"], rc[f"keep{k + 1}"]
                    c.link(tt(work[:, :, :], pk[:, :, :], pos[:, :, :], ALU.mult))
                    c.link(v.tensor_reduce(place[:, :], work[:, :, :], AX.X, ALU.add))
                    if n == 0:
                        c.link(ts(keep[:, :], place[:, :], float(CAP), None, ALU.is_lt))
                        c.link(ts(place[:, :], place[:, :], float(CAP - 1), None, ALU.min))
                        c.link(stt(place[:, :], rc[first][:, :], -float(CAP), place[:, :], ALU.mult, ALU.add))
                        c.link(ts(place[:, :], place[:, :], float(E * CAP), None, ALU.add))
                        c.link(v.tensor_copy(from_row[k][:, :], place[:, :]))
                        c.link(tt(place[:, :], place[:, :], trash[:, k, :], ALU.subtract))
                        c.link(tt(place[:, :], place[:, :], keep[:, :], ALU.mult))
                        c.link(tt(place[:, :], place[:, :], trash[:, k, :], ALU.add))
                        c.link(v.tensor_copy(to_row[k][:, :], place[:, :]))
                    else:
                        c.link(v.tensor_copy(from_row[k][:, :], place[:, :]))
                        c.link(v.tensor_copy(to_row[k][:, :], place[:, :]))
                v.tensor_copy(texp[:, 0:1], place[:, 0:1]).then_inc(routed, 1)
                if n == 0:
                    for g_, best, keep in (("gate1", "best1", "keep1"), ("gate2", "best2", "keep2")):
                        c.link(tt(rc[g_][:, :], rc[best][:, :], rc[keep][:, :], ALU.mult))
                    c.link(tt(rc["sum"][:, :], rc["gate1"][:, :], rc["gate2"][:, :], ALU.add))
                    c.link(ts(rc["sum"][:, :], rc["sum"][:, :], 1e-6, None, ALU.max))
                    c.link(v.reciprocal(rc["inv"][:, :], rc["sum"][:, :]))
                    for g_ in ("gate1", "gate2"):
                        c.link(tt(rc[g_][:, :], rc[g_][:, :], rc["inv"][:, :], ALU.mult))

            def combine_pair(R, it, js=range(4)):
                for j in js:
                    b, k = 2 * it + j // 2, j % 2
                    dve.wait_ge(gathered[j], 16 * (COMBINE0[R.n] // 4 + it + 1))
                    xb = X[:, ds(b * D, D)]
                    stt(xb, got[j][:, :], rc[f"gate{k + 1}"][:, ds(b, 1)], xb, ALU.mult, ALU.add).then_inc(combined, 1)
                    dve.wait_ge(combined, COMBINE0[R.n] + 4 * it + j + 1)

            def combine_last():
                for t in range(NB):
                    s = t % 4
                    dve.wait_ge(gathered[s], 16 * ((COMBINE0[2] + t) // 4 + 1))
                    xb = X[:, t * D:(t + 1) * D]
                    tt(xb, got[s][:, :], xb, ALU.add).then_inc(combined, 1)

            def dve_shared(S):
                def multiply(g):
                    for f in range(S.nf):
                        p = S.nf * g + f
                        dve.wait_ge(sh_gated, S.gates0 + p + 1)
                        dve.wait_ge(sh_psum, S.products0 + 2 * p + 2)
                        if g >= 2 and f == 0:
                            dve.wait_ge(so_psum, S.groups0 + g - 1)
                        tt(shT[g % 2][:, f, :], bank[2 * (p % 2) + 1][:, :], sh_gate[p % 2], ALU.mult).then_inc(sh_ready, 1)

                def add(g):
                    dve.wait_ge(so_psum, S.groups0 + g + 1)
                    for t in range(4):
                        xb = X[:, (4 * g + t) * D:(4 * g + t + 1) * D]
                        tt(xb, xb, bank[6 + g % 2][:, t * D:(t + 1) * D], ALU.add).then_inc(shared_done, 1)
                if S.gate:
                    multiply(0)
                for g in range(4):
                    if S.gate and g < 3:
                        multiply(g + 1)
                    add(g)

            def dve_mlp(r):
                w, nj = r.width, r.width // P
                h_bank = [[bank[0], bank[1]], [bank[2], bank[3]]]
                t_bank = [bank[4], bank[5]]

                def multiply(it, s):
                    i = 2 * it + s
                    dve.wait_ge(g_ready, r.gates0 + i + 1)
                    if not isinstance(it, int) or it > 0:
                        dve.wait_ge(hT_psum, r.at + i - 1)
                    tt(hid[s][:, 0:w], h_bank[s][0][:, 0:w], gate[s][:, 0:w], ALU.mult).then_inc(h_ready, 1)

                def turned(it, s):
                    i = 2 * it + s
                    dve.wait_ge(hT_psum, r.at + i + 1)
                    if not isinstance(it, int) or it > 0:
                        dve.wait_ge(m2_psum, r.at + i - 1)
                    v.tensor_copy(hidT[s][:, 0:nj, :], t_bank[s][:, 0:w].rearrange("p (j t) -> p j t", j=nj)).then_inc(hT_ready, 1)

                def finish(it, s):
                    i = 2 * it + s
                    dve.wait_ge(m2_psum, r.at + i + 1)
                    if not isinstance(it, int) or it > 0:
                        dve.wait_ge(stored[s], r.stored0 + 16 * it)
                    v.tensor_copy(row_out[s][:, :], Y_BANK[:, 0:D]).then_inc(m2_done, 1)

                def steps(it):
                    for s in range(2):
                        i = 2 * it + s
                        if not isinstance(i, int) or 1 <= i <= r.tiles:
                            turned(*((it - 1, 1) if s == 0 else (it, 0)))
                        if r.gated and (not isinstance(i, int) or i < r.tiles):
                            multiply(it, s)
                        if not isinstance(i, int) or 2 <= i <= r.tiles + 1:
                            finish(it - 1, s)
                steps(0)
                with dve.Fori(1, r.tiles // 2) as it:
                    steps(it)
                steps(r.tiles // 2)

            for s in range(2):
                v.memset(vw[s][:, :, 64:65], 1.0).then_inc(dve_prepared if s else dve_step, 1)
            c.n += 1
            dve.wait_ge(loaded["rowsof"], 16 * 5)
            dve.wait_ge(loaded["x"], 16)
            dve_attention(ATT[0])
            route(RT[0], 0)

            def finish0(it, s):
                e = 2 * it + s
                dve.wait_ge(o0_psum, e + 1)
                if not isinstance(it, int) or it > 0:
                    dve.wait_ge(stored[s], 32 * it)
                b2 = b2_rows[:, ds(e * D, D)].rearrange("p (o d) -> p o d", o=1)
                c.link(tt(o0[s][:, 0:2, :], bank[4 + s][:, 0:256].rearrange("p (r d) -> p r d", r=2), spread(b2, 1, 2), ALU.add))
                n = CAP - 2 * P
                tt(o0[s][0:n, 2, :], bank[4 + s][0:n, 256:384], b2_rows[0:n, ds(e * D, D)], ALU.add).then_inc(o0_ready, 1)
            dve.wait_ge(loaded["b2"], 16)
            finish0(0, 0)
            finish0(0, 1)
            c.enter(0, 2)
            with dve.Fori(1, E // 2) as it:
                c.resume(it - 1)
                finish0(it, 0)
                finish0(it, 1)
            c.leave(E // 2 - 1)
            dve_attention(ATT[1])
            norm_all(1)
            dve_shared(SH1)
            blank(ATT[2])
            ts(notmask, mask8[:, :], -1.0, MASKED, ALU.add, ALU.mult).then_inc(notmask_ready, 1)
            dve_attention(ATT[2])
            route(RT[1], 2)
            dve_shared(SH2)
            dve_mlp(RO2)
            blank(ATT[3])
            dve_attention(ATT[3])
            route(RT[2], 3)
            dve_shared(SH3)
            dve_mlp(RO3)
            combine_last()


_INS = ['x', 'ctx_768', 'mask_BxS2_bf1', 'L0_xattn_Wq', 'L0_xattn_Wkv', 'L0_xattn_Wproj', 'L0_xattn_bproj',
        'L0_ffn_w_router', 'L0_ffn_b_router', 'L0_ffn_w1', 'L0_ffn_b1', 'L0_ffn_w2', 'L0_ffn_b2',
        'L1_xattn_Wq', 'L1_xattn_Wk', 'L1_xattn_Wv', 'L1_xattn_Wo', 'L1_xattn_bo',
        'L1_ffn_w_gate', 'L1_ffn_w_up', 'L1_ffn_w_down',
        'L2_xattn_Wq', 'L2_xattn_bq', 'L2_xattn_Wkv', 'L2_xattn_bkv', 'L2_xattn_Wo', 'L2_xattn_bo',
        'L2_ffn_shared_w1', 'L2_ffn_shared_w2', 'L2_ffn_experts_w1', 'L2_ffn_experts_w2', 'L2_ffn_gate_w',
        'L3_xattn_Wq', 'L3_xattn_Wk', 'L3_xattn_Wv', 'L3_xattn_Wo', 'L3_ffn_Wg_DN', 'L3_ffn_Wl1_ND2H', 'L3_ffn_Wl2_NHD']


def kernel(**inputs):
    import numpy as _np
    import concourse.bacc as _bacc
    from concourse import mybir as _mybir
    from concourse.bass_utils import run_bass_kernel_spmd as _run

    nc = _bacc.Bacc("TRN2", target_bir_lowering=False, num_devices=1)
    arrays, args = {}, {}
    for name in _INS:
        a = _np.ascontiguousarray(inputs[name])
        if a.dtype == bool:
            a = a.view(_np.uint8)
        arrays[f"in_{name}_dram"] = a
        args[name] = nc.dram_tensor(f"in_{name}_dram", a.shape, _mybir.dt.from_np(a.dtype), kind="ExternalInput").ap()
    out = nc.dram_tensor("out_0_dram", (NB, P, D), F32, kind="ExternalOutput").ap()
    build(nc, args, out)
    r = _run(nc, [arrays], core_ids=[0])
    return r.results[0]["out_0_dram"]
```
